# Optimizing a Trainium2 kernel written in Bass

```python
import numpy as np
import jax
import jax.numpy as jnp

def _softmax(x, axis=-1):
    return jax.nn.softmax(x, axis=axis)

def _gelu(x):
    return jax.nn.gelu(x, approximate=True)

def _silu(x):
    return jax.nn.silu(x)

def _sigmoid(x):
    return jax.nn.sigmoid(x)

def _layernorm(x, axis=-1, eps=1e-05):
    m = jnp.mean(x, axis=axis, keepdims=True)
    v = jnp.var(x, axis=axis, keepdims=True)
    return (x - m) / jnp.sqrt(v + eps)

def _scatter_add(tgt, idx, src, axis=0):
    return tgt.at[idx].add(src)

def _segment_sum(src, seg, n):
    return jax.ops.segment_sum(src, seg, n)
kernel_name = 'mk_recurrent_d4_jaxref_r8_07f868'

def setup_inputs(seed: int=0):
    np.random.seed(seed)
    _w = jnp.asarray

    def _L0_attn_setup():
        import jax, jax.numpy as jnp
        import numpy as np
        FP32_EPS = 1.1920929e-07

        def rms_norm(x):
            return x * jax.lax.rsqrt(jnp.mean(x * x, axis=-1, keepdims=True) + FP32_EPS)
        key = jax.random.key(seed)
        k1, k2, k3, k4 = jax.random.split(key, 4)
        n_embd, n_qkv = (128, 128)
        B, T = (4, 1024)

        def casted_init(k, out_f, in_f):
            s = 3.0 ** 0.5 * in_f ** (-0.5)
            return jax.random.uniform(k, (out_f, in_f), jnp.float32, -s, s)
        return {'x': jax.random.normal(k1, (B, T, n_embd), jnp.float32), 'w_qkv': casted_init(k2, 3 * n_qkv, n_embd), 'w_swiglu': casted_init(k3, 2 * n_embd, n_qkv), 'w_out': casted_init(k4, n_embd, n_embd)}
    _L0_attn_in = _L0_attn_setup()

    def _L0_ffn_setup():
        import jax, jax.numpy as jnp
        import numpy as np
        D_IN, D_HID = (128, 512)

        def _ternary(key, shape):
            return jax.random.randint(key, shape, -1, 2).astype(jnp.float32)

        def _tlin(x, w, s):
            return jnp.einsum('bsi,oi->bso', x, w) * s
        key = jax.random.key(seed)
        ks = jax.random.split(key, 12)
        inv = lambda fan: 1.0 / np.sqrt(fan).astype(np.float32)
        return {'x': jax.random.normal(ks[0], (4, 256, D_IN), dtype=jnp.float32), 'w1_w': _ternary(ks[1], (D_HID, D_IN)), 'w1_s': jax.random.uniform(ks[2], (D_HID,), dtype=jnp.float32) * inv(D_IN), 'w2_w': _ternary(ks[3], (D_HID, D_IN)), 'w2_s': jax.random.uniform(ks[4], (D_HID,), dtype=jnp.float32) * inv(D_IN), 'h1_w': _ternary(ks[5], (D_HID, D_HID)), 'h1_s': jax.random.uniform(ks[6], (D_HID,), dtype=jnp.float32) * inv(D_HID), 'h2_w': _ternary(ks[7], (D_HID, D_HID)), 'h2_s': jax.random.uniform(ks[8], (D_HID,), dtype=jnp.float32) * inv(D_HID), 'w3_w': _ternary(ks[9], (D_IN, D_HID)), 'w3_s': jax.random.uniform(ks[10], (D_IN,), dtype=jnp.float32) * inv(D_HID)}
    _L0_ffn_in = _L0_ffn_setup()

    def _L1_attn_setup():
        import jax, jax.numpy as jnp
        import numpy as np
        DIM = 128
        HEADS = 16
        DIM_HEAD = 64
        CHUNK = 64
        INNER = HEADS * DIM_HEAD
        key = jax.random.key(seed)
        k1, k2, k3 = jax.random.split(key, 3)
        x = jax.random.normal(k1, (4, 512, DIM), dtype=jnp.float32)
        w_qkv = jax.random.normal(k2, (INNER * 3, DIM), dtype=jnp.float32) * DIM ** (-0.5)
        w_out = jax.random.normal(k3, (DIM, INNER), dtype=jnp.float32) * INNER ** (-0.5)
        b_out = jnp.zeros((DIM,), dtype=jnp.float32)
        return {'x': x, 'w_qkv': w_qkv, 'w_out': w_out, 'b_out': b_out}
    _L1_attn_in = _L1_attn_setup()

    def _L1_ffn_setup():
        import jax, jax.numpy as jnp
        import numpy as np
        B, T, D = (2, 128, 128)
        E = 16
        H = 256
        K = 2
        HS = H * 2
        key = jax.random.key(seed)
        ks = jax.random.split(key, 16)
        s = 0.02
        f32 = jnp.float32
        return {'x': jax.random.normal(ks[0], (B, T, D), f32), 'Wg': jax.random.normal(ks[1], (D, E), f32) * s, 'W1': jax.random.normal(ks[2], (E, D, H), f32) * s, 'b1': jax.random.normal(ks[3], (E, H), f32) * s, 'W11': jax.random.normal(ks[4], (E, D, H), f32) * s, 'b11': jax.random.normal(ks[5], (E, H), f32) * s, 'W2': jax.random.normal(ks[6], (E, H, D), f32) * s, 'b2': jax.random.normal(ks[7], (E, D), f32) * s, 'Ws1': jax.random.normal(ks[8], (D, HS), f32) * s, 'bs1': jax.random.normal(ks[9], (HS,), f32) * s, 'Ws11': jax.random.normal(ks[10], (D, HS), f32) * s, 'bs11': jax.random.normal(ks[11], (HS,), f32) * s, 'Ws2': jax.random.normal(ks[12], (HS, D), f32) * s, 'bs2': jax.random.normal(ks[13], (D,), f32) * s}
    _L1_ffn_in = _L1_ffn_setup()

    def _L2_attn_setup():
        import jax, jax.numpy as jnp
        import numpy as np
        import math
        INPUT_WIDTH = 128
        KEY_WIDTH = 64
        VALUE_WIDTH = 64
        NUM_HEADS = 16
        key = jax.random.key(seed)
        k_x, k_q, k_k, k_v, k_p = jax.random.split(key, 5)
        n, s = (2, 256)
        scale = 1.0 / math.sqrt(INPUT_WIDTH)
        X = jax.random.normal(k_x, (n, s, INPUT_WIDTH), dtype=jnp.float32)
        Wq = jax.random.uniform(k_q, (INPUT_WIDTH, NUM_HEADS * KEY_WIDTH), jnp.float32, -scale, scale)
        Wk = jax.random.uniform(k_k, (INPUT_WIDTH, NUM_HEADS * KEY_WIDTH), jnp.float32, -scale, scale)
        Wv = jax.random.uniform(k_v, (INPUT_WIDTH, NUM_HEADS * VALUE_WIDTH), jnp.float32, -scale, scale)
        p_scale = 1.0 / math.sqrt(NUM_HEADS * VALUE_WIDTH)
        Wpost = jax.random.uniform(k_p, (NUM_HEADS * VALUE_WIDTH, INPUT_WIDTH), jnp.float32, -p_scale, p_scale)
        return {'X': X, 'Wq': Wq, 'Wk': Wk, 'Wv': Wv, 'Wpost': Wpost}
    _L2_attn_in = _L2_attn_setup()

    def _L2_ffn_setup():
        import jax, jax.numpy as jnp
        import numpy as np
        BLOCK = 16
        _GRID = jnp.array([0.0, 0.5, 1.0, 1.5, 2.0, 3.0, 4.0, 6.0], dtype=jnp.float32)
        _MID = jnp.array([0.25, 0.75, 1.25, 1.75, 2.5, 3.5, 5.0], dtype=jnp.float32)

        def fp4_quant_dequant(x):
            shape = x.shape
            xb = x.reshape(shape[:-1] + (shape[-1] // BLOCK, BLOCK))
            scale = jnp.max(jnp.abs(xb), axis=-1, keepdims=True) / 6.0
            scale = jnp.maximum(scale, jnp.float32(1e-12))
            xn = xb / scale
            idx = jnp.searchsorted(_MID, jnp.abs(xn))
            q = _GRID[idx] * jnp.sign(xn) * scale
            return q.reshape(shape)

        def fp4_linear(x, w):
            xq = fp4_quant_dequant(x)
            wq = fp4_quant_dequant(w)
            return jnp.einsum('bsk,nk->bsn', xq, wq)
        key = jax.random.key(seed)
        k1, k2, k3, k4 = jax.random.split(key, 4)
        H, I = (128, 352)
        x = jax.random.normal(k1, (4, 512, H), dtype=jnp.float32)
        w_gate = jax.random.normal(k2, (I, H), dtype=jnp.float32) * 0.02
        w_up = jax.random.normal(k3, (I, H), dtype=jnp.float32) * 0.02
        w_down = jax.random.normal(k4, (H, I), dtype=jnp.float32) * 0.02
        return {'x': x, 'w_gate': w_gate, 'w_up': w_up, 'w_down': w_down}
    _L2_ffn_in = _L2_ffn_setup()

    def _L3_attn_setup():
        import jax, jax.numpy as jnp
        import numpy as np
        B, S, D, H = (2, 256, 128, 16)
        DH = D // H
        RD = DH // 2
        EPS = 1e-05

        def _rope(x):
            seq = x.shape[-2]
            inv_freq = 1.0 / 10000.0 ** (jnp.arange(0, RD, 2, dtype=jnp.float32) / RD)
            t = jnp.arange(seq, dtype=jnp.float32)
            freqs = t[:, None] * inv_freq[None, :]
            freqs = jnp.repeat(freqs, 2, axis=-1)
            cosf, sinf = (jnp.cos(freqs), jnp.sin(freqs))
            xr, xp = (x[..., :RD], x[..., RD:])
            pairs = xr.reshape(*xr.shape[:-1], RD // 2, 2)
            rot = jnp.stack([-pairs[..., 1], pairs[..., 0]], axis=-1).reshape(xr.shape)
            return jnp.concatenate([xr * cosf + rot * sinf, xp], axis=-1)
        key = jax.random.key(seed)
        ks = jax.random.split(key, 4)
        s = 0.02
        return {'X': jax.random.normal(ks[0], (B, S, D), jnp.float32), 'W_in': jax.random.normal(ks[1], (D, 3 * D), jnp.float32) * s, 'b_in': jnp.zeros((3 * D,), jnp.float32), 'W_out': jax.random.normal(ks[2], (D, D), jnp.float32) * s, 'b_out': jnp.zeros((D,), jnp.float32), 'gamma': jnp.ones((D,), jnp.float32), 'beta': jnp.zeros((D,), jnp.float32)}
    _L3_attn_in = _L3_attn_setup()

    def _L3_ffn_setup():
        import jax, jax.numpy as jnp
        import numpy as np
        DIM = 128
        DEPTH = 6
        HEADS = 16
        DIM_HEAD = 64
        WINDOW = 32
        INNER = HEADS * DIM_HEAD
        DIM_INNER = int(DIM * 4 * 2 / 3)
        QK_SCALE = 8.0

        def shift_tokens(t):
            a, s = jnp.split(t, 2, -1)
            s = jnp.pad(s, ((0, 0), (1, 0), (0, 0)))[:, :-1]
            return jnp.concatenate([a, s], -1)

        def l2norm(t):
            return t / jnp.maximum(jnp.linalg.norm(t, axis=-1, keepdims=True), 1e-12)

        def rotate_half(x):
            x1, x2 = jnp.split(x, 2, -1)
            return jnp.concatenate([-x2, x1], -1)

        def rotary_tables(n):
            half = jnp.arange(0, DIM_HEAD, 2, dtype=jnp.float32)
            inv_freq = 1.0 / 10000.0 ** (half / DIM_HEAD)
            t = jnp.arange(n, dtype=jnp.float32)
            freqs = t[:, None] * inv_freq[None, :]
            freqs = jnp.concatenate([freqs, freqs], -1)
            base_scale = (half + 0.4 * DIM_HEAD) / (1.4 * DIM_HEAD)
            power = (t - n // 2) / (WINDOW // 2)
            scale = base_scale[None, :] ** power[:, None]
            scale = jnp.concatenate([scale, scale], -1)
            return (freqs, scale)

        def local_attention(q, k, v):
            b, h, n, d = q.shape
            w = WINDOW
            nw = n // w
            bq = q.reshape(b, h, nw, w, d)
            bk = k.reshape(b, h, nw, w, d)
            bv = v.reshape(b, h, nw, w, d)

            def look(t):
                p = jnp.pad(t, ((0, 0), (0, 0), (1, 0), (0, 0), (0, 0)))
                return jnp.concatenate([p[:, :, :nw], p[:, :, 1:]], axis=3)
            bk2, bv2 = (look(bk), look(bv))
            seq = jnp.arange(n).reshape(nw, w)
            seq_p = jnp.pad(seq, ((1, 0), (0, 0)), constant_values=-1)
            jt = jnp.concatenate([seq_p[:nw], seq_p[1:]], axis=1)
            it = seq[:, :, None]
            jb = jt[:, None, :]
            mask = (it < jb) | (it > jb + w) | (jb == -1)
            sim = jnp.einsum('bhwie,bhwje->bhwij', bq, bk2) * QK_SCALE
            sim = jnp.where(mask, -jnp.finfo(sim.dtype).max, sim)
            attn = jax.nn.softmax(sim, -1)
            out = jnp.einsum('bhwij,bhwje->bhwie', attn, bv2)
            return out.reshape(b, h, n, d)

        def attn_layer(x, Wqkv, qs, ksc, Wo):
            b, n, _ = x.shape
            qkv = x @ Wqkv
            q, k, v = jnp.split(qkv, 3, -1)
            sh = lambda t: t.reshape(b, n, HEADS, DIM_HEAD).transpose(0, 2, 1, 3)
            q, k, v = (sh(q), sh(k), sh(v))
            q = l2norm(q) * qs
            k = l2norm(k) * ksc
            freqs, scale = rotary_tables(n)
            cos, sin = (jnp.cos(freqs), jnp.sin(freqs))
            q = q * cos * scale + rotate_half(q) * sin * scale
            inv = 1.0 / scale
            k = k * cos * inv + rotate_half(k) * sin * inv
            out = local_attention(q, k, v)
            out = out.transpose(0, 2, 1, 3).reshape(b, n, INNER)
            return out @ Wo

        def ffn_layer(x, g, bln, W1, b1, W2, b2):
            mu = x.mean(-1, keepdims=True)
            var = ((x - mu) ** 2).mean(-1, keepdims=True)
            xn = (x - mu) / jnp.sqrt(var + 1e-05) * g + bln
            hg = xn @ W1 + b1
            a, gate = jnp.split(hg, 2, -1)
            return a * jax.nn.gelu(gate, approximate=False) @ W2 + b2
        key = jax.random.key(seed)
        ks = jax.random.split(key, 8)
        B, N = (2, 256)
        init = lambda k, shape: jax.random.normal(k, shape, jnp.float32) * 0.02
        return {'x': jax.random.normal(ks[0], (B, N, DIM), jnp.float32), 'Wqkv': init(ks[1], (DEPTH, DIM, 3 * INNER)), 'q_scale': jnp.ones((DEPTH, DIM_HEAD), jnp.float32), 'k_scale': jnp.ones((DEPTH, DIM_HEAD), jnp.float32), 'Wo': init(ks[2], (DEPTH, INNER, DIM)), 'ln_g': jnp.ones((DEPTH, DIM), jnp.float32), 'ln_b': jnp.zeros((DEPTH, DIM), jnp.float32), 'W1': init(ks[3], (DEPTH, DIM, 2 * DIM_INNER)), 'b1': jnp.zeros((DEPTH, 2 * DIM_INNER), jnp.float32), 'W2': init(ks[4], (DEPTH, DIM_INNER, DIM)), 'b2': jnp.zeros((DEPTH, DIM), jnp.float32)}
    _L3_ffn_in = _L3_ffn_setup()
    _d = {'L0_attn_x': _L0_attn_in['x'], 'L0_attn_w_qkv': _L0_attn_in['w_qkv'], 'L0_attn_w_swiglu': _L0_attn_in['w_swiglu'], 'L0_attn_w_out': _L0_attn_in['w_out'], 'L0_ffn_w1_w': _L0_ffn_in['w1_w'], 'L0_ffn_w1_s': _L0_ffn_in['w1_s'], 'L0_ffn_w2_w': _L0_ffn_in['w2_w'], 'L0_ffn_w2_s': _L0_ffn_in['w2_s'], 'L0_ffn_h1_w': _L0_ffn_in['h1_w'], 'L0_ffn_h1_s': _L0_ffn_in['h1_s'], 'L0_ffn_h2_w': _L0_ffn_in['h2_w'], 'L0_ffn_h2_s': _L0_ffn_in['h2_s'], 'L0_ffn_w3_w': _L0_ffn_in['w3_w'], 'L0_ffn_w3_s': _L0_ffn_in['w3_s'], 'L1_attn_w_qkv': _L1_attn_in['w_qkv'], 'L1_attn_w_out': _L1_attn_in['w_out'], 'L1_attn_b_out': _L1_attn_in['b_out'], 'L1_ffn_Wg': _L1_ffn_in['Wg'], 'L1_ffn_W1': _L1_ffn_in['W1'], 'L1_ffn_b1': _L1_ffn_in['b1'], 'L1_ffn_W11': _L1_ffn_in['W11'], 'L1_ffn_b11': _L1_ffn_in['b11'], 'L1_ffn_W2': _L1_ffn_in['W2'], 'L1_ffn_b2': _L1_ffn_in['b2'], 'L1_ffn_Ws1': _L1_ffn_in['Ws1'], 'L1_ffn_bs1': _L1_ffn_in['bs1'], 'L1_ffn_Ws11': _L1_ffn_in['Ws11'], 'L1_ffn_bs11': _L1_ffn_in['bs11'], 'L1_ffn_Ws2': _L1_ffn_in['Ws2'], 'L1_ffn_bs2': _L1_ffn_in['bs2'], 'L2_attn_Wq': _L2_attn_in['Wq'], 'L2_attn_Wk': _L2_attn_in['Wk'], 'L2_attn_Wv': _L2_attn_in['Wv'], 'L2_attn_Wpost': _L2_attn_in['Wpost'], 'L2_ffn_w_gate': _L2_ffn_in['w_gate'], 'L2_ffn_w_up': _L2_ffn_in['w_up'], 'L2_ffn_w_down': _L2_ffn_in['w_down'], 'L3_attn_W_in': _L3_attn_in['W_in'], 'L3_attn_b_in': _L3_attn_in['b_in'], 'L3_attn_W_out': _L3_attn_in['W_out'], 'L3_attn_b_out': _L3_attn_in['b_out'], 'L3_attn_gamma': _L3_attn_in['gamma'], 'L3_attn_beta': _L3_attn_in['beta'], 'L3_ffn_Wqkv': _L3_ffn_in['Wqkv'], 'L3_ffn_q_scale': _L3_ffn_in['q_scale'], 'L3_ffn_k_scale': _L3_ffn_in['k_scale'], 'L3_ffn_Wo': _L3_ffn_in['Wo'], 'L3_ffn_ln_g': _L3_ffn_in['ln_g'], 'L3_ffn_ln_b': _L3_ffn_in['ln_b'], 'L3_ffn_W1': _L3_ffn_in['W1'], 'L3_ffn_b1': _L3_ffn_in['b1'], 'L3_ffn_W2': _L3_ffn_in['W2'], 'L3_ffn_b2': _L3_ffn_in['b2']}
    _x0 = _d['L0_attn_x']
    _d['L0_attn_x'] = jax.random.normal(jax.random.fold_in(jax.random.key(seed), 1), (2, 1024, 128), dtype=_x0.dtype)
    del _x0
    return _d

def reference(L0_attn_x, L0_attn_w_qkv, L0_attn_w_swiglu, L0_attn_w_out, L0_ffn_w1_w, L0_ffn_w1_s, L0_ffn_w2_w, L0_ffn_w2_s, L0_ffn_h1_w, L0_ffn_h1_s, L0_ffn_h2_w, L0_ffn_h2_s, L0_ffn_w3_w, L0_ffn_w3_s, L1_attn_w_qkv, L1_attn_w_out, L1_attn_b_out, L1_ffn_Wg, L1_ffn_W1, L1_ffn_b1, L1_ffn_W11, L1_ffn_b11, L1_ffn_W2, L1_ffn_b2, L1_ffn_Ws1, L1_ffn_bs1, L1_ffn_Ws11, L1_ffn_bs11, L1_ffn_Ws2, L1_ffn_bs2, L2_attn_Wq, L2_attn_Wk, L2_attn_Wv, L2_attn_Wpost, L2_ffn_w_gate, L2_ffn_w_up, L2_ffn_w_down, L3_attn_W_in, L3_attn_b_in, L3_attn_W_out, L3_attn_b_out, L3_attn_gamma, L3_attn_beta, L3_ffn_Wqkv, L3_ffn_q_scale, L3_ffn_k_scale, L3_ffn_Wo, L3_ffn_ln_g, L3_ffn_ln_b, L3_ffn_W1, L3_ffn_b1, L3_ffn_W2, L3_ffn_b2):

    def _L0_attn_ref(x, w_qkv, w_swiglu, w_out):
        import jax, jax.numpy as jnp
        import numpy as np
        FP32_EPS = 1.1920929e-07

        def rms_norm(x):
            return x * jax.lax.rsqrt(jnp.mean(x * x, axis=-1, keepdims=True) + FP32_EPS)
        qkv = jnp.einsum('btd,ed->bte', rms_norm(x), w_qkv)
        q, k, v = jnp.split(qkv, 3, axis=-1)
        q = rms_norm(q)
        k = rms_norm(k)
        w = jnp.exp(k)
        kv = w * v
        w = jnp.cumsum(w, axis=1)
        kv = jnp.cumsum(kv, axis=1)
        y = kv / (w + 1e-06)
        y = jax.nn.sigmoid(q) * y
        uv = jnp.einsum('bte,fe->btf', y, w_swiglu)
        u, g = jnp.split(uv, 2, axis=-1)
        return x + jnp.einsum('btd,ed->bte', u * jax.nn.silu(g), w_out)

    def _L0_ffn_ref(x, w1_w, w1_s, w2_w, w2_s, h1_w, h1_s, h2_w, h2_s, w3_w, w3_s):
        import jax, jax.numpy as jnp
        import numpy as np
        D_IN, D_HID = (128, 512)

        def _ternary(key, shape):
            return jax.random.randint(key, shape, -1, 2).astype(jnp.float32)

        def _tlin(x, w, s):
            return jnp.einsum('bsi,oi->bso', x, w) * s
        h = jax.nn.silu(_tlin(x, w1_w, w1_s)) * _tlin(x, w2_w, w2_s)
        h = jax.nn.gelu(_tlin(h, h1_w, h1_s), approximate=False)
        h = jax.nn.gelu(_tlin(h, h2_w, h2_s), approximate=False)
        return _tlin(h, w3_w, w3_s)

    def _L1_attn_ref(x, w_qkv, w_out, b_out):
        import jax, jax.numpy as jnp
        import numpy as np
        DIM = 128
        HEADS = 16
        DIM_HEAD = 64
        CHUNK = 64
        INNER = HEADS * DIM_HEAD
        b, n, _ = x.shape
        scale = DIM_HEAD ** (-0.5)
        qkv = jnp.einsum('bnd,ed->bne', x, w_qkv)
        q, k, v = jnp.split(qkv, 3, axis=-1)
        nblk = n // CHUNK

        def to_blocks(t):
            t = t.reshape(b, n, HEADS, DIM_HEAD).transpose(0, 2, 1, 3)
            return t.reshape(b, HEADS, nblk, CHUNK, DIM_HEAD)
        qb, kb, vb = (to_blocks(q), to_blocks(k), to_blocks(v))
        scores = jnp.einsum('bhgqd,bhgkd->bhgqk', qb, kb) * scale
        attn = jax.nn.softmax(scores, axis=-1)
        ob = jnp.einsum('bhgqk,bhgkd->bhgqd', attn, vb)
        out = ob.reshape(b, HEADS, n, DIM_HEAD).transpose(0, 2, 1, 3).reshape(b, n, INNER)
        return jnp.einsum('bne,de->bnd', out, w_out) + b_out

    def _L1_ffn_ref(x, Wg, W1, b1, W11, b11, W2, b2, Ws1, bs1, Ws11, bs11, Ws2, bs2):
        import jax, jax.numpy as jnp
        import numpy as np
        B, T, D = (2, 128, 128)
        E = 16
        H = 256
        K = 2
        HS = H * 2
        b, t, d = x.shape
        xf = x.reshape(b * t, d)
        n = xf.shape[0]
        logits = xf @ Wg
        _, topi = jax.lax.top_k(logits, K)
        mask = jnp.zeros((n, E), bool).at[jnp.arange(n)[:, None], topi].set(True)
        gates = jax.nn.softmax(jnp.where(mask, logits, -jnp.inf), axis=-1)
        y = jnp.zeros_like(xf)
        for e in range(E):
            h = jax.nn.silu(xf @ W1[e] + b1[e]) * (xf @ W11[e] + b11[e])
            y = y + (h @ W2[e] + b2[e]) * gates[:, e, None]
        z = jax.nn.silu(xf @ Ws1 + bs1) * (xf @ Ws11 + bs11) @ Ws2 + bs2
        return (y + z).reshape(b, t, d)

    def _L2_attn_ref(X, Wq, Wk, Wv, Wpost):
        import jax, jax.numpy as jnp
        import numpy as np
        import math
        INPUT_WIDTH = 128
        KEY_WIDTH = 64
        VALUE_WIDTH = 64
        NUM_HEADS = 16
        n, s, _ = X.shape
        Q = (X @ Wq).reshape(n, s, NUM_HEADS, KEY_WIDTH)
        K = (X @ Wk).reshape(n, s, NUM_HEADS, KEY_WIDTH)
        V = (X @ Wv).reshape(n, s, NUM_HEADS, VALUE_WIDTH)
        inv_sqrt_d = 1.0 / math.sqrt(KEY_WIDTH)
        raw_attn = jnp.einsum('bshe,bthe->bsth', Q, K * inv_sqrt_d)
        attn = jax.nn.softmax(raw_attn, axis=2)
        A = jnp.einsum('bsth,bthe->bshe', attn, V).reshape(n, s, NUM_HEADS * VALUE_WIDTH)
        A = jax.nn.gelu(A, approximate=False)
        P = A @ Wpost
        return X + P

    def _L2_ffn_ref(x, w_gate, w_up, w_down):
        import jax, jax.numpy as jnp
        import numpy as np
        BLOCK = 16
        _GRID = jnp.array([0.0, 0.5, 1.0, 1.5, 2.0, 3.0, 4.0, 6.0], dtype=jnp.float32)
        _MID = jnp.array([0.25, 0.75, 1.25, 1.75, 2.5, 3.5, 5.0], dtype=jnp.float32)

        def fp4_quant_dequant(x):
            shape = x.shape
            xb = x.reshape(shape[:-1] + (shape[-1] // BLOCK, BLOCK))
            scale = jnp.max(jnp.abs(xb), axis=-1, keepdims=True) / 6.0
            scale = jnp.maximum(scale, jnp.float32(1e-12))
            xn = xb / scale
            idx = jnp.searchsorted(_MID, jnp.abs(xn))
            q = _GRID[idx] * jnp.sign(xn) * scale
            return q.reshape(shape)

        def fp4_linear(x, w):
            xq = fp4_quant_dequant(x)
            wq = fp4_quant_dequant(w)
            return jnp.einsum('bsk,nk->bsn', xq, wq)
        gate = fp4_linear(x, w_gate)
        y = fp4_linear(x, w_up)
        h = jax.nn.silu(gate) * y
        return fp4_linear(h, w_down)

    def _L3_attn_ref(X, W_in, b_in, W_out, b_out, gamma, beta):
        import jax, jax.numpy as jnp
        import numpy as np
        B, S, D, H = (2, 256, 128, 16)
        DH = D // H
        RD = DH // 2
        EPS = 1e-05

        def _rope(x):
            seq = x.shape[-2]
            inv_freq = 1.0 / 10000.0 ** (jnp.arange(0, RD, 2, dtype=jnp.float32) / RD)
            t = jnp.arange(seq, dtype=jnp.float32)
            freqs = t[:, None] * inv_freq[None, :]
            freqs = jnp.repeat(freqs, 2, axis=-1)
            cosf, sinf = (jnp.cos(freqs), jnp.sin(freqs))
            xr, xp = (x[..., :RD], x[..., RD:])
            pairs = xr.reshape(*xr.shape[:-1], RD // 2, 2)
            rot = jnp.stack([-pairs[..., 1], pairs[..., 0]], axis=-1).reshape(xr.shape)
            return jnp.concatenate([xr * cosf + rot * sinf, xp], axis=-1)
        b, s, d = X.shape
        mu = jnp.mean(X, axis=-1, keepdims=True)
        var = jnp.var(X, axis=-1, keepdims=True)
        xn = (X - mu) * jax.lax.rsqrt(var + EPS) * gamma + beta
        qkv = xn @ W_in + b_in
        q, k, v = jnp.split(qkv, 3, axis=-1)

        def to_heads(t):
            return t.reshape(b, s, H, DH).transpose(0, 2, 1, 3)
        q, k, v = (to_heads(q), to_heads(k), to_heads(v))
        q, k = (_rope(q), _rope(k))
        scores = jnp.einsum('bhqd,bhkd->bhqk', q, k) / jnp.sqrt(jnp.float32(DH))
        attn = jax.nn.softmax(scores, axis=-1)
        ctx = jnp.einsum('bhqk,bhkd->bhqd', attn, v)
        ctx = ctx.transpose(0, 2, 1, 3).reshape(b, s, d)
        return ctx @ W_out + b_out + X

    def _L3_ffn_ref(x, Wqkv, q_scale, k_scale, Wo, ln_g, ln_b, W1, b1, W2, b2):
        import jax, jax.numpy as jnp
        import numpy as np
        DIM = 128
        DEPTH = 6
        HEADS = 16
        DIM_HEAD = 64
        WINDOW = 32
        INNER = HEADS * DIM_HEAD
        DIM_INNER = int(DIM * 4 * 2 / 3)
        QK_SCALE = 8.0

        def shift_tokens(t):
            a, s = jnp.split(t, 2, -1)
            s = jnp.pad(s, ((0, 0), (1, 0), (0, 0)))[:, :-1]
            return jnp.concatenate([a, s], -1)

        def l2norm(t):
            return t / jnp.maximum(jnp.linalg.norm(t, axis=-1, keepdims=True), 1e-12)

        def rotate_half(x):
            x1, x2 = jnp.split(x, 2, -1)
            return jnp.concatenate([-x2, x1], -1)

        def rotary_tables(n):
            half = jnp.arange(0, DIM_HEAD, 2, dtype=jnp.float32)
            inv_freq = 1.0 / 10000.0 ** (half / DIM_HEAD)
            t = jnp.arange(n, dtype=jnp.float32)
            freqs = t[:, None] * inv_freq[None, :]
            freqs = jnp.concatenate([freqs, freqs], -1)
            base_scale = (half + 0.4 * DIM_HEAD) / (1.4 * DIM_HEAD)
            power = (t - n // 2) / (WINDOW // 2)
            scale = base_scale[None, :] ** power[:, None]
            scale = jnp.concatenate([scale, scale], -1)
            return (freqs, scale)

        def local_attention(q, k, v):
            b, h, n, d = q.shape
            w = WINDOW
            nw = n // w
            bq = q.reshape(b, h, nw, w, d)
            bk = k.reshape(b, h, nw, w, d)
            bv = v.reshape(b, h, nw, w, d)

            def look(t):
                p = jnp.pad(t, ((0, 0), (0, 0), (1, 0), (0, 0), (0, 0)))
                return jnp.concatenate([p[:, :, :nw], p[:, :, 1:]], axis=3)
            bk2, bv2 = (look(bk), look(bv))
            seq = jnp.arange(n).reshape(nw, w)
            seq_p = jnp.pad(seq, ((1, 0), (0, 0)), constant_values=-1)
            jt = jnp.concatenate([seq_p[:nw], seq_p[1:]], axis=1)
            it = seq[:, :, None]
            jb = jt[:, None, :]
            mask = (it < jb) | (it > jb + w) | (jb == -1)
            sim = jnp.einsum('bhwie,bhwje->bhwij', bq, bk2) * QK_SCALE
            sim = jnp.where(mask, -jnp.finfo(sim.dtype).max, sim)
            attn = jax.nn.softmax(sim, -1)
            out = jnp.einsum('bhwij,bhwje->bhwie', attn, bv2)
            return out.reshape(b, h, n, d)

        def attn_layer(x, Wqkv, qs, ksc, Wo):
            b, n, _ = x.shape
            qkv = x @ Wqkv
            q, k, v = jnp.split(qkv, 3, -1)
            sh = lambda t: t.reshape(b, n, HEADS, DIM_HEAD).transpose(0, 2, 1, 3)
            q, k, v = (sh(q), sh(k), sh(v))
            q = l2norm(q) * qs
            k = l2norm(k) * ksc
            freqs, scale = rotary_tables(n)
            cos, sin = (jnp.cos(freqs), jnp.sin(freqs))
            q = q * cos * scale + rotate_half(q) * sin * scale
            inv = 1.0 / scale
            k = k * cos * inv + rotate_half(k) * sin * inv
            out = local_attention(q, k, v)
            out = out.transpose(0, 2, 1, 3).reshape(b, n, INNER)
            return out @ Wo

        def ffn_layer(x, g, bln, W1, b1, W2, b2):
            mu = x.mean(-1, keepdims=True)
            var = ((x - mu) ** 2).mean(-1, keepdims=True)
            xn = (x - mu) / jnp.sqrt(var + 1e-05) * g + bln
            hg = xn @ W1 + b1
            a, gate = jnp.split(hg, 2, -1)
            return a * jax.nn.gelu(gate, approximate=False) @ W2 + b2
        for i in range(DEPTH):
            x = attn_layer(shift_tokens(x), Wqkv[i], q_scale[i], k_scale[i], Wo[i]) + x
            x = ffn_layer(shift_tokens(x), ln_g[i], ln_b[i], W1[i], b1[i], W2[i], b2[i]) + x
        return x
    x = L0_attn_x
    xn = _layernorm(x, axis=-1)
    s = _L0_attn_ref(xn, L0_attn_w_qkv, L0_attn_w_swiglu, L0_attn_w_out)
    g = _silu(_L0_ffn_ref(xn, L0_ffn_w1_w, L0_ffn_w1_s, L0_ffn_w2_w, L0_ffn_w2_s, L0_ffn_h1_w, L0_ffn_h1_s, L0_ffn_h2_w, L0_ffn_h2_s, L0_ffn_w3_w, L0_ffn_w3_s))
    x = x + s * g
    xn = _layernorm(x, axis=-1)
    s = _L1_attn_ref(xn, L1_attn_w_qkv, L1_attn_w_out, L1_attn_b_out)
    g = _silu(_L1_ffn_ref(xn, L1_ffn_Wg, L1_ffn_W1, L1_ffn_b1, L1_ffn_W11, L1_ffn_b11, L1_ffn_W2, L1_ffn_b2, L1_ffn_Ws1, L1_ffn_bs1, L1_ffn_Ws11, L1_ffn_bs11, L1_ffn_Ws2, L1_ffn_bs2))
    x = x + s * g
    xn = _layernorm(x, axis=-1)
    s = _L2_attn_ref(xn, L2_attn_Wq, L2_attn_Wk, L2_attn_Wv, L2_attn_Wpost)
    g = _silu(_L2_ffn_ref(xn, L2_ffn_w_gate, L2_ffn_w_up, L2_ffn_w_down))
    x = x + s * g
    xn = _layernorm(x, axis=-1)
    s = _L3_attn_ref(xn, L3_attn_W_in, L3_attn_b_in, L3_attn_W_out, L3_attn_b_out, L3_attn_gamma, L3_attn_beta)
    g = _silu(_L3_ffn_ref(xn, L3_ffn_Wqkv, L3_ffn_q_scale, L3_ffn_k_scale, L3_ffn_Wo, L3_ffn_ln_g, L3_ffn_ln_b, L3_ffn_W1, L3_ffn_b1, L3_ffn_W2, L3_ffn_b2))
    x = x + s * g
    return x

_drawn_inputs = setup_inputs


def setup_inputs(seed=0):
    import zlib

    import numpy as np

    out = dict(_drawn_inputs(seed))
    spreads = {'L1_attn_b_out': (0.0, 0.1),
     'L3_attn_b_in': (0.0, 0.1),
     'L3_attn_b_out': (0.0, 0.1),
     'L3_attn_gamma': (1.0, 0.2),
     'L3_attn_beta': (0.0, 0.1),
     'L3_ffn_q_scale': (1.0, 0.2),
     'L3_ffn_k_scale': (1.0, 0.2),
     'L3_ffn_ln_g': (1.0, 0.2),
     'L3_ffn_ln_b': (0.0, 0.1),
     'L3_ffn_b1': (0.0, 0.1),
     'L3_ffn_b2': (0.0, 0.1)}
    factors = {}
    for name, (base, spread) in spreads.items():
        noise = np.random.default_rng([zlib.crc32(name.encode()), seed]).standard_normal(out[name].shape)
        drawn = base * np.exp(spread * noise) if base else spread * noise
        out[name] = jnp.asarray(drawn.astype(out[name].dtype))
    for name, factor in factors.items():
        out[name] = (out[name] * factor).astype(out[name].dtype)
    return out
```

```python
from contextlib import ExitStack, contextmanager

import numpy as np

import concourse.bass as bass
from concourse import mybir

F32 = mybir.dt.float32
BF16 = mybir.dt.bfloat16
ALU = mybir.AluOpType
ACT = mybir.ActivationFunctionType
AX = mybir.AxisListType

P = 128
D = 128
B, T = 2, 1024
N = B * T
TILE = 512
NT = N // TILE
BT = T // TILE
HEADS, DH = 16, 64
PAIRS = HEADS // 2
INNER = HEADS * DH
WIN = 32
DEPTH = 6
EXPERTS, EH, SH = 16, 256, 512
FFI = 352
QB = 16
DI = 341
DI3 = 3
RMS_EPS = 1.1920929e-07
LN_EPS = 1e-05


def tok(t):
    return slice(TILE * t, TILE * t + TILE)


class Steps:

    def __init__(self, eng, sem):
        self.eng, self.sem, self.n = eng, sem, 0

    def did(self, ins):
        ins.then_inc(self.sem, 1)
        self.n += 1

    def settle(self):
        self.eng.wait_ge(self.sem, self.n)

    def link(self, ins):
        self.did(ins)
        self.settle()


class Core:

    def __init__(self, nc, ctx):
        self.nc, self.ctx, self.sems = nc, ctx, []
        self.x = self.sb(ctx, "x_stream", [P, N])
        self.xn = self.sb(ctx, "x_normed", [P, N])
        self.s = self.sb(ctx, "s_branch", [P, N])
        self.g = self.sb(ctx, "g_branch", [P, N])
        self.ident = self.sb(ctx, "ident", [P, P])
        self.mean_w = self.sb(ctx, "mean_w", [P, P])
        self.eps = self.sb(ctx, "eps_cols", [P, 2])
        self.bank = ctx.enter_context(nc.psum_tensor("banks", [P, 8, TILE], F32))

    def sb(self, ctx, name, shape, dt=F32):
        return ctx.enter_context(self.nc.sbuf_tensor(name, shape, dt))

    def sem(self, ctx, name):
        self.sems.append(ctx.enter_context(self.nc.semaphore(name)))
        return self.sems[-1]

    @contextmanager
    def stage(self):
        outer, self.sems = self.ctx, []
        with ExitStack() as self.ctx:
            yield
            clear(self.nc, self.sems)
        self.ctx = outer


def clear(nc, sems):
    with nc.Block(no_gpsimd_drain=True) as block:
        @block.sync
        def _(sp):
            for s in sems:
                sp.sem_clear(s)


def load_start(k, x, consts):
    nc = k.nc
    loaded = k.sem(k.ctx, "start_loaded")
    with nc.Block() as block:
        @block.sync
        def _(sp):
            sp.dma_start(k.x[:, :], x).then_inc(loaded, 16)
            sp.dma_start(k.ident[:, :], consts["ident"]).then_inc(loaded, 16)
            sp.dma_start(k.mean_w[:, :], consts["mean_w"]).then_inc(loaded, 16)
            sp.dma_start(k.eps[:, :], consts["eps"]).then_inc(loaded, 16)
            sp.wait_ge(loaded, 64)


def layer_norm(k, name, src, dst, gamma=None, beta=None, sems=None):
    nc = k.nc
    with ExitStack() as ctx:
        sq = k.sb(ctx, f"{name}_sq", [P, 2, TILE])
        rstd = k.sb(ctx, f"{name}_rstd", [P, 2, TILE])
        mean_done, centred, squared, var_done, std_done, dve_own = sems or [
            k.sem(k.ctx, f"{name}_{s}") for s in ("mean", "centred", "squared", "var", "std", "dve")]
        with nc.Block() as block:
            @block.tensor
            def _(pe):
                def mean(t):
                    if t >= 2:
                        pe.wait_ge(centred, t - 1)
                    pe.matmul(k.bank[:, t % 2, :], k.mean_w[:, :], src[:, tok(t)], start=True, stop=True).then_inc(mean_done, 1)

                mean(0)
                for t in range(NT):
                    if t + 1 < NT:
                        mean(t + 1)
                    pe.wait_ge(squared, t + 1)
                    if t >= 2:
                        pe.wait_ge(std_done, t - 1)
                    pe.matmul(k.bank[:, 2 + t % 2, :], k.mean_w[:, :], sq[:, t % 2, :], start=True, stop=True).then_inc(var_done, 1)

            @block.vector
            def _(dve):
                own = Steps(dve, dve_own)

                def finish(t):
                    dve.wait_ge(std_done, t + 1)
                    own.link(dve.reciprocal(rstd[:, t % 2, :], rstd[:, t % 2, :]))
                    own.did(dve.tensor_tensor(dst[:, tok(t)], dst[:, tok(t)], rstd[:, t % 2, :], ALU.mult))
                    if gamma is not None:
                        own.settle()
                        own.did(dve.tensor_scalar(dst[:, tok(t)], dst[:, tok(t)], gamma, beta, ALU.mult, ALU.add))

                for t in range(NT):
                    dve.wait_ge(mean_done, t + 1)
                    dve.tensor_tensor(dst[:, tok(t)], src[:, tok(t)], k.bank[:, t % 2, :], ALU.subtract).then_inc(centred, 1)
                    if t:
                        finish(t - 1)
                finish(NT - 1)

            @block.scalar
            def _(act):
                for t in range(NT):
                    act.wait_ge(centred, t + 1)
                    if t >= 2:
                        act.wait_ge(var_done, t - 1)
                    act.activation(sq[:, t % 2, :], dst[:, tok(t)], ACT.Square).then_inc(squared, 1)
                    act.wait_ge(var_done, t + 1)
                    if t >= 2:
                        act.wait_ge(dve_own, (3 if gamma is not None else 2) * (t - 1))
                    act.activation(rstd[:, t % 2, :], k.bank[:, 2 + t % 2, :], ACT.Sqrt, bias=k.eps[:, 0:1]).then_inc(std_done, 1)


def combine(k, name):
    nc = k.nc
    done = k.sem(k.ctx, f"{name}_combined")
    with nc.Block() as block:
        @block.vector
        def _(dve):
            own = Steps(dve, done)
            for t in range(NT):
                own.did(dve.tensor_tensor(k.s[:, tok(t)], k.s[:, tok(t)], k.g[:, tok(t)], ALU.mult))
            for t in range(NT):
                dve.wait_ge(done, t + 1)
                own.did(dve.tensor_tensor(k.x[:, tok(t)], k.x[:, tok(t)], k.s[:, tok(t)], ALU.add))


def gated_scan(k, w):
    nc = k.nc
    with ExitStack() as ctx:
        wt = k.sb(ctx, "l0a_w", [P, 3 * D + 2 * D + D])
        wq, wsw, wo = wt[:, 0:3 * D], wt[:, 3 * D:5 * D], wt[:, 5 * D:6 * D]
        ones = k.sb(ctx, "l0a_ones", [P, TILE])
        bufs = {n: k.sb(ctx, "l0a_" + n, [P, N]) for n in ("a", "b", "xr", "q", "k", "v", "y")}
        a, b, xr, q, kk, v, y = (bufs[n] for n in ("a", "b", "xr", "q", "k", "v", "y"))
        S = {n: k.sem(k.ctx, "l0a_" + n) for n in (
            "loaded", "sq", "ms", "std", "xr", "mm", "qsq", "qms", "qstd", "qn", "copied",
            "sig", "exp", "y", "uv", "silu", "h", "out", "dve", "stored")}
        with nc.Block() as block:
            @block.sync
            def _(sp):
                sp.dma_start(wq, w["qkv"]).then_inc(S["loaded"], 16)
                sp.dma_start(wsw, w["swiglu"]).then_inc(S["loaded"], 16)
                sp.dma_start(wo, w["out"]).then_inc(S["loaded"], 16)

            @block.tensor
            def _(pe):
                for t in range(NT):
                    pe.wait_ge(S["sq"], t + 1)
                    if t >= 2:
                        pe.wait_ge(S["std"], t - 1)
                    pe.matmul(k.bank[:, t % 2, :], k.mean_w[:, :], a[:, tok(t)], start=True, stop=True).then_inc(S["ms"], 1)
                pe.wait_ge(S["loaded"], 48)
                for t in range(NT):
                    pe.wait_ge(S["xr"], t + 1)
                    for j in range(3):
                        i = 3 * t + j
                        if i >= 6:
                            pe.wait_ge(S["copied"], i - 5)
                        pe.matmul(k.bank[:, 2 + i % 6, :], wq[:, D * j:D * j + D], xr[:, tok(t)], start=True, stop=True).then_inc(S["mm"], 1)
                pe.wait_ge(S["std"], NT)
                for i in range(2 * NT):
                    pe.wait_ge(S["qsq"], i + 1)
                    if i >= 2:
                        pe.wait_ge(S["qstd"], i - 1)
                    src = (a if i % 2 == 0 else b)
                    pe.matmul(k.bank[:, i % 2, :], k.mean_w[:, :], src[:, tok(i // 2)], start=True, stop=True).then_inc(S["qms"], 1)
                pe.wait_ge(S["copied"], 3 * NT)
                for t in range(NT):
                    pe.wait_ge(S["y"], t + 1)
                    if t >= 2:
                        pe.wait_ge(S["h"], t - 1)
                    for j in range(2):
                        pe.matmul(k.bank[:, 2 + 2 * (t % 2) + j, :], wsw[:, D * j:D * j + D], y[:, tok(t)], start=True, stop=True).then_inc(S["uv"], 1)
                for t in range(NT):
                    pe.wait_ge(S["h"], t + 1)
                    if t >= 2:
                        pe.wait_ge(S["stored"], t - 1)
                    pe.matmul(k.bank[:, 6 + t % 2, :], wo, a[:, tok(t)], start=True, stop=True).then_inc(S["out"], 1)

            @block.scalar
            def _(act):
                for t in range(NT):
                    act.activation(a[:, tok(t)], k.xn[:, tok(t)], ACT.Square).then_inc(S["sq"], 1)
                for t in range(NT):
                    act.wait_ge(S["ms"], t + 1)
                    act.activation(b[:, tok(t)], k.bank[:, t % 2, :], ACT.Sqrt, bias=k.eps[:, 1:2]).then_inc(S["std"], 1)
                for t in range(NT):
                    for j, dst in enumerate((q, kk, v)):
                        act.wait_ge(S["mm"], 3 * t + j + 1)
                        act.copy(dst[:, tok(t)], k.bank[:, 2 + (3 * t + j) % 6, :]).then_inc(S["copied"], 1)
                act.wait_ge(S["xr"], NT)
                act.wait_ge(S["copied"], 3 * NT)
                for i in range(2 * NT):
                    dst, src = ((a, q), (b, kk))[i % 2]
                    act.activation(dst[:, tok(i // 2)], src[:, tok(i // 2)], ACT.Square).then_inc(S["qsq"], 1)
                for i in range(2 * NT):
                    act.wait_ge(S["qms"], i + 1)
                    dst = (a, b)[i % 2]
                    act.activation(dst[:, tok(i // 2)], k.bank[:, i % 2, :], ACT.Sqrt, bias=k.eps[:, 1:2]).then_inc(S["qstd"], 1)
                for t in range(NT):
                    act.wait_ge(S["qn"], 2 * t + 2)
                    act.activation(kk[:, tok(t)], kk[:, tok(t)], ACT.Exp).then_inc(S["exp"], 1)
                for t in range(NT):
                    act.activation(q[:, tok(t)], q[:, tok(t)], ACT.Sigmoid).then_inc(S["sig"], 1)
                for t in range(NT):
                    act.wait_ge(S["uv"], 2 * t + 2)
                    act.activation(b[:, tok(t)], k.bank[:, 3 + 2 * (t % 2), :], ACT.Silu).then_inc(S["silu"], 1)

            @block.vector
            def _(dve):
                own = Steps(dve, S["dve"])
                own.did(dve.memset(ones[:, :], 1.0))
                for t in range(NT):
                    dve.wait_ge(S["std"], t + 1)
                    own.link(dve.reciprocal(b[:, tok(t)], b[:, tok(t)]))
                    dve.tensor_tensor(xr[:, tok(t)], k.xn[:, tok(t)], b[:, tok(t)], ALU.mult).then_inc(S["xr"], 1)
                for i in range(2 * NT):
                    dve.wait_ge(S["qstd"], i + 1)
                    r, z = ((a, q), (b, kk))[i % 2]
                    own.link(dve.reciprocal(r[:, tok(i // 2)], r[:, tok(i // 2)]))
                    dve.tensor_tensor(z[:, tok(i // 2)], z[:, tok(i // 2)], r[:, tok(i // 2)], ALU.mult).then_inc(S["qn"], 1)
                for t in range(NT):
                    dve.wait_ge(S["exp"], t + 1)
                    dve.wait_ge(S["qn"], 2 * NT)
                    own.link(dve.tensor_tensor(v[:, tok(t)], v[:, tok(t)], kk[:, tok(t)], ALU.mult))
                    first = t % BT == 0
                    before = slice(TILE * t - 1, TILE * t)
                    own.did(dve.tensor_tensor_scan(a[:, tok(t)], ones[:, :], kk[:, tok(t)], 0.0 if first else a[:, before], ALU.mult, ALU.add))
                    own.link(dve.tensor_tensor_scan(y[:, tok(t)], ones[:, :], v[:, tok(t)], 0.0 if first else y[:, before], ALU.mult, ALU.add))
                for t in range(NT):
                    own.link(dve.tensor_scalar(a[:, tok(t)], a[:, tok(t)], 1e-6, None, ALU.add))
                    own.link(dve.reciprocal(a[:, tok(t)], a[:, tok(t)]))
                    own.link(dve.tensor_tensor(y[:, tok(t)], y[:, tok(t)], a[:, tok(t)], ALU.mult))
                    dve.wait_ge(S["sig"], t + 1)
                    dve.tensor_tensor(y[:, tok(t)], y[:, tok(t)], q[:, tok(t)], ALU.mult).then_inc(S["y"], 1)
                for t in range(NT):
                    dve.wait_ge(S["silu"], t + 1)
                    dve.tensor_tensor(a[:, tok(t)], k.bank[:, 2 + 2 * (t % 2), :], b[:, tok(t)], ALU.mult).then_inc(S["h"], 1)
                for t in range(NT):
                    dve.wait_ge(S["out"], t + 1)
                    dve.tensor_tensor(k.s[:, tok(t)], k.xn[:, tok(t)], k.bank[:, 6 + t % 2, :], ALU.add).then_inc(S["stored"], 1)


def ternary_ffn(k, w):
    nc = k.nc
    H = 4
    with ExitStack() as ctx:
        w12 = k.sb(ctx, "l0f_w12", [P, 2, 512])
        wh = k.sb(ctx, "l0f_wh", [P, 2, H, 512])
        w3 = k.sb(ctx, "l0f_w3", [P, H, D])
        sc = k.sb(ctx, "l0f_scales", [P, 17])
        act_a = k.sb(ctx, "l0f_act", [P, 2, TILE])
        ha = k.sb(ctx, "l0f_ha", [P, H, N])
        hb = k.sb(ctx, "l0f_hb", [P, H, N])
        S = {n: k.sem(k.ctx, "l0f_" + n) for n in ("loaded", "gate", "up", "silu", "h0", "mm1", "h1", "mm2", "h2", "mm3", "g")}
        with nc.Block() as block:
            @block.sync
            def _(sp):
                sp.dma_start(w12[:, :, :], w["w12"]).then_inc(S["loaded"], 16)
                sp.dma_start(sc[:, :], w["scales"]).then_inc(S["loaded"], 16)
                sp.dma_start(wh[:, :, :, :], w["h"]).then_inc(S["loaded"], 16)
                sp.dma_start(w3[:, :, :], w["w3"]).then_inc(S["loaded"], 16)

            @block.tensor
            def _(pe):
                pe.wait_ge(S["loaded"], 64)
                for i in range(NT * H):
                    t, o = i // H, i % H
                    if i >= 2:
                        pe.wait_ge(S["silu"], i - 1)
                    pe.matmul(k.bank[:, i % 2, :], w12[:, 0, P * o:P * o + P], k.xn[:, tok(t)], start=True, stop=True).then_inc(S["gate"], 1)
                    if i >= 2:
                        pe.wait_ge(S["h0"], i - 1)
                    pe.matmul(k.bank[:, 2 + i % 2, :], w12[:, 1, P * o:P * o + P], k.xn[:, tok(t)], start=True, stop=True).then_inc(S["up"], 1)
                for layer, (src, before, mm, after) in enumerate(((ha, "h0", "mm1", "h1"), (hb, "h1", "mm2", "h2"))):
                    for i in range(NT * H):
                        t, o = i // H, i % H
                        pe.wait_ge(S[before], H * (t + 1))
                        if i >= 4:
                            pe.wait_ge(S[after], i - 3)
                        elif layer:
                            pe.wait_ge(S[before], NT * H)
                        for c in range(H):
                            ins = pe.matmul(k.bank[:, 4 + i % 4, :], wh[:, layer, c, P * o:P * o + P], src[:, c, tok(t)], start=c == 0, stop=c == H - 1)
                        ins.then_inc(S[mm], 1)
                for t in range(NT):
                    pe.wait_ge(S["h2"], H * (t + 1))
                    for c in range(H):
                        ins = pe.matmul(k.bank[:, t, :], w3[:, c, :], ha[:, c, tok(t)], start=c == 0, stop=c == H - 1)
                    ins.then_inc(S["mm3"], 1)

            @block.scalar
            def _(act):
                act.wait_ge(S["loaded"], 64)
                for i in range(NT * H):
                    act.wait_ge(S["gate"], i + 1)
                    if i >= 2:
                        act.wait_ge(S["h0"], i - 1)
                    act.activation(act_a[:, i % 2, :], k.bank[:, i % 2, :], ACT.Silu, scale=sc[:, i % H:i % H + 1]).then_inc(S["silu"], 1)
                for layer, (dst, mm, after) in enumerate(((hb, "mm1", "h1"), (ha, "mm2", "h2"))):
                    for i in range(NT * H):
                        t, o = i // H, i % H
                        act.wait_ge(S[mm], i + 1)
                        if layer:
                            act.wait_ge(S["mm1"], NT * H)
                        act.activation(dst[:, o, tok(t)], k.bank[:, 4 + i % 4, :], ACT.Gelu,
                                       scale=sc[:, 8 + 4 * layer + o:9 + 4 * layer + o]).then_inc(S[after], 1)
                for t in range(NT):
                    act.wait_ge(S["mm3"], t + 1)
                    act.activation(k.g[:, tok(t)], k.bank[:, t, :], ACT.Silu, scale=sc[:, 16:17]).then_inc(S["g"], 1)

            @block.vector
            def _(dve):
                dve.wait_ge(S["loaded"], 64)
                for i in range(NT * H):
                    t, o = i // H, i % H
                    dve.wait_ge(S["silu"], i + 1)
                    dve.wait_ge(S["up"], i + 1)
                    dve.scalar_tensor_tensor(ha[:, o, tok(t)], k.bank[:, 2 + i % 2, :], sc[:, 4 + o:5 + o], act_a[:, i % 2, :],
                                             op0=ALU.mult, op1=ALU.mult).then_inc(S["h0"], 1)


class Local:

    def __init__(self, k, ctx, name, win):
        self.name, self.win, self.halo = name, win, 64 - win
        self.nw = TILE // win
        self.q = k.sb(ctx, name + "_q", [P, PAIRS, TILE])
        self.k = k.sb(ctx, name + "_k", [P, PAIRS, self.halo + TILE])
        self.v = k.sb(ctx, name + "_v", [P, self.nw, PAIRS * DH])
        self.p = k.sb(ctx, name + "_p", [P, 2, PAIRS, 2, 64])
        self.pt = k.sb(ctx, name + "_pt", [P, 2, PAIRS, P])
        self.ov = k.sb(ctx, name + "_ov", [P, PAIRS, 2, DH])
        self.o = k.sb(ctx, name + "_o", [P, PAIRS, TILE])
        self.top = k.sb(ctx, name + "_top", [P, 2, 2 * PAIRS])
        self.sum = k.sb(ctx, name + "_sum", [P, 2, 2 * PAIRS])
        self.S = {n: k.sem(k.ctx, f"{name}_{n}") for n in (
            "scores", "read", "masked", "shifted", "exp", "recip", "turned", "pt", "pv", "ov", "back", "o", "dve", "values", "vcopied", "out", "stored")}


def local_attention(k, m, scale, wo, store, qscale=None, mask=None, values=None):
    nc, S, W = k.nc, m.S, m.win
    TI = TILE // P
    JW = P // W
    project, late = values or (None, range(0))
    with nc.Block() as block:
        @block.tensor
        def _(pe):
            def scores(i):
                if i >= 2:
                    pe.wait_ge(S["read"], i - 1)
                for j in range(JW):
                    for pair in range(PAIRS):
                        for p in range(2):
                            r = slice(64 * p, 64 * p + 64)
                            ins = pe.matmul(k.bank[W * j:W * j + W, 2 * (i % 2) + p, 64 * pair:64 * pair + 64],
                                            m.q[r, pair, P * i + W * j:P * i + W * j + W],
                                            m.k[r, pair, P * i + W * j:P * i + W * j + 64], start=True, stop=True)
                ins.then_inc(S["scores"], 1)

            def turn(i):
                pe.wait_ge(S["exp"], i + 1)
                if i >= 2:
                    pe.wait_ge(S["o"], i - 1)
                for pair in range(PAIRS):
                    ins = pe.transpose(k.bank[:, 4 + pair // 4, P * (pair % 4):P * (pair % 4) + P],
                                       m.p[:, i % 2, pair, :, :].rearrange("p a b -> p (a b)"), k.ident[:, :])
                ins.then_inc(S["turned"], 1)

            def back(i):
                pe.wait_ge(S["ov"], i + 1)
                pe.wait_ge(S["pt"], min(i + 2, TI))
                if i:
                    pe.wait_ge(S["o"], i)
                for pair in range(PAIRS):
                    ins = pe.transpose(k.bank[:, 4 + pair // 4, P * (pair % 4):P * (pair % 4) + P],
                                       m.ov[:, pair, :, :].rearrange("p a b -> p (a b)"), k.ident[:, :])
                ins.then_inc(S["back"], 1)

            def weigh(i):
                pe.wait_ge(S["pt"], i + 1)
                if i:
                    pe.wait_ge(S["ov"], i)
                for j in range(JW):
                    for pair in range(PAIRS):
                        for p in range(2):
                            r = slice(64 * p, 64 * p + 64)
                            ins = pe.matmul(k.bank[W * j:W * j + W, 6 + p, DH * pair:DH * pair + DH],
                                            m.pt[r, i % 2, pair, W * j:W * j + W], m.v[r, JW * i + j, DH * pair:DH * pair + DH], start=True, stop=True)
                ins.then_inc(S["pv"], 1)

            scores(0)
            scores(1)
            for n, i in enumerate(late):
                if n >= 4:
                    pe.wait_ge(S["vcopied"], n - 3)
                project(pe, i, k.bank[:, 4 + n % 4, :]).then_inc(S["values"], 1)
            if late:
                pe.wait_ge(S["vcopied"], len(late))
            for i in range(TI):
                turn(i)
                if i + 2 < TI:
                    scores(i + 2)
                if i:
                    back(i - 1)
                weigh(i)
            back(TI - 1)
            pe.wait_ge(S["o"], TI)
            for pair in range(PAIRS):
                ins = pe.matmul(k.bank[:, 6, :], wo[:, pair, :], m.o[:, pair, :], start=pair == 0, stop=pair == PAIRS - 1)
            ins.then_inc(S["out"], 1)

        @block.vector
        def _(dve):
            own = Steps(dve, S["dve"])

            def wide(ap):
                return ap.rearrange("p (a b) -> p a b", b=2).unsqueeze(3).to_broadcast([P, PAIRS, 2, 64])

            def by_pair(banks):
                return banks.rearrange("p b (a c) -> p a b c", c=64)

            def finish(i):
                dve.wait_ge(S["pv"], i + 1)
                dve.wait_ge(S["recip"], i + 1)
                if i:
                    dve.wait_ge(S["back"], i)
                dve.tensor_tensor(m.ov[:, :, :, :], by_pair(k.bank[:, 6:8, :]), wide(m.sum[:, i % 2, :]), ALU.mult).then_inc(S["ov"], 1)

            def first(i):
                raw = by_pair(k.bank[:, 2 * (i % 2):2 * (i % 2) + 2, :])
                prob = m.p[:, i % 2, :, :, :]
                dve.wait_ge(S["scores"], i + 1)
                if i >= 2:
                    dve.wait_ge(S["turned"], i - 1)
                if qscale is None:
                    top = m.top[:, i % 2, :]
                    own.link(dve.tensor_reduce(top.rearrange("p (a b) -> p a b", b=2), raw, AX.X, ALU.max))
                    own.link(dve.tensor_tensor(prob, raw, wide(top), ALU.subtract))
                    dve.sem_inc(S["read"], 1)
                    dve.sem_inc(S["shifted"], 1)
                else:
                    dve.tensor_tensor(prob, raw, wide(qscale(i)), ALU.mult).then_inc(S["read"], 1)

            def second(i):
                flat = m.p[:, i % 2, :, :, :].rearrange("p a b c -> p (a b) c")
                top, total = m.top[:, i % 2, :], m.sum[:, i % 2, :]
                if qscale is not None:
                    dve.wait_ge(S["masked"], i + 1)
                    own.link(dve.tensor_reduce(top, flat, AX.X, ALU.max))
                    dve.tensor_tensor(flat, flat, top.unsqueeze(2).to_broadcast([P, 2 * PAIRS, 64]), ALU.subtract).then_inc(S["shifted"], 1)
                dve.wait_ge(S["exp"], i + 1)
                own.link(dve.tensor_reduce(total, flat, AX.X, ALU.add))
                dve.reciprocal(total, total).then_inc(S["recip"], 1)

            first(0)
            for i in range(TI):
                if i + 1 < TI:
                    first(i + 1)
                if i >= 2:
                    dve.wait_ge(S["ov"], i - 1)
                second(i)
                if i:
                    finish(i - 1)
            finish(TI - 1)
            dve.wait_ge(S["out"], 1)
            store(dve, k.bank[:, 6, :]).then_inc(S["stored"], 1)

        @block.scalar
        def _(act):
            def copy_values(ns):
                for n in ns:
                    act.wait_ge(S["values"], n + 1)
                    act.copy(m.v[:, late[n], :], k.bank[:, 4 + n % 4, :]).then_inc(S["vcopied"], 1)

            def exp(i):
                act.wait_ge(S["shifted"], i + 1)
                flat = m.p[:, i % 2, :, :, :].rearrange("p a b c -> p (a b c)")
                act.activation(flat, flat, ACT.Exp, scale=scale).then_inc(S["exp"], 1)

            def copy_back(i):
                act.wait_ge(S["back"], i + 1)
                act.copy(m.o[:, :, P * i:P * i + P], k.bank[:, 4:6, :].rearrange("p a (b c) -> p (a b) c", c=P)).then_inc(S["o"], 1)

            copy_values(range(min(2, len(late))))
            exp(0)
            copy_values(range(2, len(late)))
            for i in range(TI):
                act.wait_ge(S["turned"], i + 1)
                if i >= 2:
                    act.wait_ge(S["pv"], i - 1)
                act.copy(m.pt[:, i % 2, :, :].rearrange("p a b -> p (a b)"), k.bank[:, 4:6, :].rearrange("p a b -> p (a b)")).then_inc(S["pt"], 1)
                if i + 1 < TI:
                    exp(i + 1)
                if i:
                    copy_back(i - 1)
            copy_back(TI - 1)

        if mask:
            @block.gpsimd
            def _(pool):
                for i in range(TI):
                    pool.wait_ge(S["read"], i + 1)
                    flat = m.p[:, i % 2, :, :, :].rearrange("p a b c -> p (a b) c")
                    pool.tensor_tensor(flat, flat, mask(i), ALU.add).then_inc(S["masked"], 1)


def chunk_attention(k, w):
    nc = k.nc
    with ExitStack() as ctx:
        m = Local(k, ctx, "l1a", 64)
        wqk = k.sb(ctx, "l1a_wqk", [P, 2 * PAIRS, P])
        wv = k.sb(ctx, "l1a_wv", [P, 2, PAIRS * DH])
        wo = k.sb(ctx, "l1a_wo", [P, PAIRS, D])
        bo = k.sb(ctx, "l1a_bo", [P, 1])
        xb = k.sb(ctx, "l1a_xb", [P, TILE])
        loaded = k.sem(k.ctx, "l1a_loaded")
        R = {n: k.sem(k.ctx, "l1a_" + n) for n in ("xb", "mm", "even", "odd")}
        with nc.Block() as block:
            @block.sync
            def _(sp):
                sp.dma_start(wqk[:, :, :], w["qk"]).then_inc(loaded, 16)
                sp.dma_start(wv[:, :, :], w["v"]).then_inc(loaded, 16)
                sp.dma_start(wo[:, :, :], w["out"]).then_inc(loaded, 16)
                sp.dma_start(bo[:, :], w["b"]).then_inc(loaded, 16)
                sp.wait_ge(loaded, 64)
        with nc.Fori(0, NT) as c:
            with nc.Block() as block:
                steps = 2 * PAIRS + m.nw

                def dest(i):
                    if i < PAIRS:
                        return m.q[:, i, :]
                    if i < 2 * PAIRS:
                        return m.k[:, i - PAIRS, :]
                    return m.v[:, i - 2 * PAIRS, :]

                @block.tensor
                def _(pe):
                    pe.wait_ge(R["xb"], 1)
                    for i in range(steps):
                        if i >= 8:
                            pe.wait_ge(R["odd" if i % 2 else "even"], (i - 8) // 2 + 1)
                        if i < 2 * PAIRS:
                            ins = pe.matmul(k.bank[:, i % 8, :], wqk[:, i, :], xb[:, :], start=True, stop=True)
                        else:
                            at = m.win * (i - 2 * PAIRS)
                            for p in range(2):
                                ins = pe.matmul(k.bank[64 * p:64 * p + 64, i % 8, :], xb[:, at:at + 64], wv[:, p, :], start=True, stop=True)
                        ins.then_inc(R["mm"], 1)

                @block.scalar
                def _(act):
                    act.copy(xb[:, :], k.xn[:, bass.ds(c * TILE, TILE)]).then_inc(R["xb"], 1)
                    for i in range(0, steps, 2):
                        act.wait_ge(R["mm"], i + 1)
                        act.copy(dest(i), k.bank[:, i % 8, :]).then_inc(R["even"], 1)

                @block.vector
                def _(dve):
                    for i in range(1, steps, 2):
                        dve.wait_ge(R["mm"], i + 1)
                        dve.tensor_copy(dest(i), k.bank[:, i % 8, :]).then_inc(R["odd"], 1)

            def store(dve, psum):
                return dve.tensor_scalar(k.s[:, bass.ds(c * TILE, TILE)], psum, bo[:, 0:1], None, ALU.add)

            local_attention(k, m, DH ** -0.5, wo, store)
            clear(nc, list(m.S.values()) + list(R.values()))


def mixture(k, w):
    nc = k.nc
    MT = N // P
    QT = TILE // P
    EW = 2 * EH + 2 * D + 4
    with ExitStack() as ctx:
        y = k.sb(ctx, "moe_y", [P, MT, D])
        gates = k.sb(ctx, "moe_gates", [P, EXPERTS, MT])
        a = k.sb(ctx, "moe_silu", [P, 2, TILE])
        ws = k.sb(ctx, "moe_ws", [P, 2, SH])
        ws2 = k.sb(ctx, "moe_ws2", [P, SH // P, D])
        bs = k.sb(ctx, "moe_bs", [P, 9])
        S = {n: k.sem(k.ctx, "moe_" + n) for n in (
            "loaded", "logits", "dve", "gap", "expgap", "gates", "turned", "gt", "by", "y0",
            "shared_gate", "shared_up", "shared_silu", "shared_h", "z", "g")}
        with ExitStack() as gctx:
            wg = k.sb(gctx, "moe_wg", [P, EXPERTS])
            b2 = k.sb(gctx, "moe_b2", [EXPERTS, D])
            rank = k.sb(gctx, "moe_rank", [P, EXPERTS])
            lg, eq, key, one1, one2 = (k.sb(gctx, "moe_" + n, [P, MT, EXPERTS]) for n in ("lg", "eq", "key", "one1", "one2"))
            m1, m2, km, gap, ex, g1, g2 = (k.sb(gctx, "moe_" + n, [P, MT]) for n in ("m1", "m2", "km", "gap_", "ex", "g1", "g2"))
            gt = k.sb(gctx, "moe_gt", [EXPERTS, N])
            with nc.Block() as block:
                @block.sync
                def _(sp):
                    for dst, src in ((wg[:, :], w["wg"]), (b2[:, :], w["b2"]), (rank[:, :], w["rank"]), (ws[:, :, :], w["ws"]),
                                     (ws2[:, :, :], w["ws2"]), (bs[:, :], w["bs"])):
                        sp.dma_start(dst, src).then_inc(S["loaded"], 16)

                @block.tensor
                def _(pe):
                    pe.wait_ge(S["loaded"], 96)
                    for i in range(MT):
                        ins = pe.matmul(k.bank[:, 0, EXPERTS * i:EXPERTS * i + EXPERTS], k.xn[:, P * i:P * i + P], wg[:, :], start=True, stop=True)
                    ins.then_inc(S["logits"], 1)
                    pe.wait_ge(S["gates"], 1)
                    for i in range(MT):
                        ins = pe.transpose(k.bank[0:EXPERTS, 1 + i // QT, P * (i % QT):P * (i % QT) + P], gates[:, :, i], k.ident[:, :])
                    ins.then_inc(S["turned"], 1)
                    pe.wait_ge(S["gt"], 1)
                    for i in range(MT):
                        ins = pe.matmul(k.bank[:, 1 + i // QT, P * (i % QT):P * (i % QT) + P], gt[:, P * i:P * i + P], b2[:, :], start=True, stop=True)
                    ins.then_inc(S["by"], 1)

                @block.scalar
                def _(act):
                    act.wait_ge(S["gap"], 1)
                    act.activation(ex[:, :], gap[:, :], ACT.Exp).then_inc(S["expgap"], 1)
                    act.wait_ge(S["turned"], 1)
                    act.copy(gt[:, :], k.bank[0:EXPERTS, 1:5, :].rearrange("p a b -> p (a b)")).then_inc(S["gt"], 1)
                    act.wait_ge(S["by"], 1)
                    act.copy(y[:, :, :].rearrange("p a b -> p (a b)"), k.bank[:, 1:5, :].rearrange("p a b -> p (a b)")).then_inc(S["y0"], 1)

                @block.vector
                def _(dve):
                    own = Steps(dve, S["dve"])

                    def wide(ap):
                        return ap.unsqueeze(2).to_broadcast([P, MT, EXPERTS])

                    def first_best(top, one):
                        own.link(dve.tensor_reduce(top, lg[:, :, :], AX.X, ALU.max))
                        own.link(dve.tensor_tensor(eq[:, :, :], lg[:, :, :], wide(top), ALU.is_equal))
                        own.link(dve.tensor_tensor(key[:, :, :], eq[:, :, :], rank[:, :].unsqueeze(1).to_broadcast([P, MT, EXPERTS]), ALU.mult))
                        own.link(dve.tensor_reduce(km[:, :], key[:, :, :], AX.X, ALU.max))
                        own.link(dve.tensor_tensor(one, key[:, :, :], wide(km[:, :]), ALU.is_equal))

                    dve.wait_ge(S["logits"], 1)
                    own.link(dve.tensor_copy(lg[:, :, :].rearrange("p a b -> p (a b)"), k.bank[:, 0, 0:MT * EXPERTS]))
                    first_best(m1[:, :], one1[:, :, :])
                    own.link(dve.scalar_tensor_tensor(lg[:, :, :], one1[:, :, :], -1e30, lg[:, :, :], op0=ALU.mult, op1=ALU.add))
                    first_best(m2[:, :], one2[:, :, :])
                    dve.tensor_tensor(gap[:, :], m2[:, :], m1[:, :], ALU.subtract).then_inc(S["gap"], 1)
                    dve.wait_ge(S["expgap"], 1)
                    own.link(dve.tensor_scalar(g1[:, :], ex[:, :], 1.0, None, ALU.add))
                    own.link(dve.reciprocal(g1[:, :], g1[:, :]))
                    own.link(dve.tensor_tensor(g2[:, :], ex[:, :], g1[:, :], ALU.mult))
                    own.did(dve.tensor_tensor(one1[:, :, :], one1[:, :, :], wide(g1[:, :]), ALU.mult))
                    own.link(dve.tensor_tensor(one2[:, :, :], one2[:, :, :], wide(g2[:, :]), ALU.mult))
                    dve.tensor_tensor(gates[:, :, :].rearrange("p e i -> p i e"), one1[:, :, :], one2[:, :, :], ALU.add).then_inc(S["gates"], 1)

        ew = k.sb(ctx, "moe_ew", [P, 2, EW])
        h = k.sb(ctx, "moe_h", [P, 2, 2, TILE])
        gcol = k.sb(ctx, "moe_gcol", [P, 2, MT])
        R = {n: k.sem(k.ctx, "moe_e_" + n) for n in ("w0", "w1", "gcol", "gate", "up", "silu", "h", "mm", "y")}
        with nc.Block() as block:
            @block.sync
            def _(sp):
                sp.dma_start(ew[:, 0, :], w["experts"][0]).then_inc(S["loaded"], 16)
                sp.dma_start(ew[:, 1, :], w["experts"][1]).then_inc(S["loaded"], 16)
                sp.wait_ge(S["loaded"], 128)
        with nc.Fori(0, EXPERTS // 2) as turn:
            with nc.Block() as block:
                steps = 2 * NT

                @block.sync
                def _(sp):
                    for slot in range(2):
                        sp.wait_ge(R["mm"], NT * (slot + 1))
                        sp.dma_start(ew[:, slot, :], w["experts"][bass.ds(turn * 2 + (2 + slot), 1)].rearrange("a p n -> p (a n)")).then_inc(R["w0"], 16)
                    sp.wait_ge(R["w0"], 32)

                @block.tensor
                def _(pe):
                    def first(u):
                        slot, t = u // NT, u % NT
                        for o in range(2):
                            i = 2 * u + o
                            if i >= 2:
                                pe.wait_ge(R["silu"], i - 1)
                            pe.matmul(k.bank[:, i % 2, :], ew[:, slot, P * o:P * o + P], k.xn[:, tok(t)], start=True, stop=True).then_inc(R["gate"], 1)
                            if i >= 2:
                                pe.wait_ge(R["h"], i - 1)
                            pe.matmul(k.bank[:, 2 + i % 2, :], ew[:, slot, EH + P * o:EH + P * o + P], k.xn[:, tok(t)], start=True, stop=True).then_inc(R["up"], 1)

                    first(0)
                    for u in range(steps):
                        if u + 1 < steps:
                            first(u + 1)
                        slot = u // NT
                        pe.wait_ge(R["h"], 2 * u + 2)
                        if u >= 2:
                            pe.wait_ge(R["y"], u - 1)
                        for q in range(QT):
                            for o in range(2):
                                ins = pe.matmul(k.bank[:, 4 + u % 2, P * q:P * q + P], h[:, u % 2, o, P * q:P * q + P],
                                                ew[:, slot, 2 * EH + D * o:2 * EH + D * o + D], start=o == 0, stop=o == 1)
                        ins.then_inc(R["mm"], 1)

                @block.scalar
                def _(act):
                    for i in range(2 * steps):
                        slot = i // (2 * NT)
                        act.wait_ge(R["gate"], i + 1)
                        if i >= 2:
                            act.wait_ge(R["h"], i - 1)
                        bias = 2 * EH + 2 * D + i % 2
                        act.activation(a[:, i % 2, :], k.bank[:, i % 2, :], ACT.Silu, bias=ew[:, slot, bias:bias + 1]).then_inc(R["silu"], 1)

                @block.vector
                def _(dve):
                    dve.tensor_copy(gcol[:, :, :], gates[:, bass.ds(turn * 2, 2), :]).then_inc(R["gcol"], 1)
                    dve.wait_ge(R["gcol"], 1)

                    def add(u):
                        slot, t = u // NT, u % NT
                        dve.wait_ge(R["mm"], u + 1)
                        for q in range(QT):
                            i = QT * t + q
                            ins = dve.scalar_tensor_tensor(y[:, i, :], k.bank[:, 4 + u % 2, P * q:P * q + P], gcol[:, slot, i:i + 1], y[:, i, :],
                                                           op0=ALU.mult, op1=ALU.add)
                        ins.then_inc(R["y"], 1)

                    for u in range(steps):
                        slot = u // NT
                        if u >= 2:
                            dve.wait_ge(R["mm"], u - 1)
                        for o in range(2):
                            i = 2 * u + o
                            dve.wait_ge(R["silu"], i + 1)
                            dve.wait_ge(R["up"], i + 1)
                            bias = 2 * EH + 2 * D + 2 + o
                            dve.scalar_tensor_tensor(h[:, u % 2, o, :], k.bank[:, 2 + i % 2, :], ew[:, slot, bias:bias + 1], a[:, i % 2, :],
                                                     op0=ALU.add, op1=ALU.mult).then_inc(R["h"], 1)
                        if u:
                            if u >= NT + 1:
                                dve.wait_ge(R["y"], u - NT)
                            add(u - 1)
                    add(steps - 1)
            clear(nc, R.values())

        hs = k.sb(ctx, "moe_hs", [P, 2, SH // P, TILE])
        with nc.Block() as block:
            H = SH // P

            @block.tensor
            def _(pe):
                def first(t):
                    for o in range(H):
                        i = H * t + o
                        if i >= 2:
                            pe.wait_ge(S["shared_silu"], i - 1)
                        pe.matmul(k.bank[:, i % 2, :], ws[:, 0, P * o:P * o + P], k.xn[:, tok(t)], start=True, stop=True).then_inc(S["shared_gate"], 1)
                        if i >= 2:
                            pe.wait_ge(S["shared_h"], i - 1)
                        pe.matmul(k.bank[:, 2 + i % 2, :], ws[:, 1, P * o:P * o + P], k.xn[:, tok(t)], start=True, stop=True).then_inc(S["shared_up"], 1)

                first(0)
                for t in range(NT):
                    if t + 1 < NT:
                        first(t + 1)
                    pe.wait_ge(S["shared_h"], H * (t + 1))
                    if t >= 2:
                        pe.wait_ge(S["g"], t - 1)
                    for o in range(H):
                        pe.matmul(k.bank[:, 4 + t % 2, :], ws2[:, o, :], hs[:, t % 2, o, :], start=o == 0, stop=False)
                    for q in range(QT):
                        ins = pe.matmul(k.bank[:, 4 + t % 2, P * q:P * q + P], y[:, QT * t + q, :], k.ident[:, :], start=False, stop=q == QT - 1)
                    ins.then_inc(S["z"], 1)

            @block.scalar
            def _(act):
                for t in range(NT):
                    for o in range(H):
                        i = H * t + o
                        act.wait_ge(S["shared_gate"], i + 1)
                        if i >= 2:
                            act.wait_ge(S["shared_h"], i - 1)
                        act.activation(a[:, i % 2, :], k.bank[:, i % 2, :], ACT.Silu, bias=bs[:, o:o + 1]).then_inc(S["shared_silu"], 1)
                    if t:
                        act.wait_ge(S["z"], t)
                        act.activation(k.g[:, tok(t - 1)], k.bank[:, 4 + (t - 1) % 2, :], ACT.Silu, bias=bs[:, 8:9]).then_inc(S["g"], 1)
                act.wait_ge(S["z"], NT)
                act.activation(k.g[:, tok(NT - 1)], k.bank[:, 4 + (NT - 1) % 2, :], ACT.Silu, bias=bs[:, 8:9]).then_inc(S["g"], 1)

            @block.vector
            def _(dve):
                for t in range(NT):
                    if t >= 2:
                        dve.wait_ge(S["z"], t - 1)
                    for o in range(H):
                        i = H * t + o
                        dve.wait_ge(S["shared_silu"], i + 1)
                        dve.wait_ge(S["shared_up"], i + 1)
                        dve.scalar_tensor_tensor(hs[:, t % 2, o, :], k.bank[:, 2 + i % 2, :], bs[:, 4 + o:5 + o], a[:, i % 2, :],
                                                 op0=ALU.add, op1=ALU.mult).then_inc(S["shared_h"], 1)


class Full:

    def __init__(self, k, ctx, name, heads, dh):
        self.heads, self.dh = heads, dh
        self.q = k.sb(ctx, name + "_q", [P, heads, T])
        self.k = k.sb(ctx, name + "_k", [P, T])
        self.v = k.sb(ctx, name + "_v", [P, T // P, heads * dh])
        self.vp = k.sb(ctx, name + "_vp", [P, T // P, heads, 3, dh], BF16)
        self.o = k.sb(ctx, name + "_o", [P, T // P, heads * dh])
        self.p = k.sb(ctx, name + "_p", [P, 2, T])
        self.pt = k.sb(ctx, name + "_pt", [P, 3, 2, T // P, P], BF16)
        self.top = k.sb(ctx, name + "_top", [P, 4])
        self.sum = k.sb(ctx, name + "_sum", [P, 4])
        self.raw = k.sb(ctx, name + "_raw", [P, 2, dh])
        self.S = {n: k.sem(k.ctx, f"{name}_{n}") for n in (
            "scores", "top", "exp", "turned_a", "turned_b", "high", "low", "pv", "recip", "read", "o", "vsplit")}


def full_attention(k, m):
    nc, S = k.nc, m.S
    KT = T // P
    units = [(qi, h) for qi in range(KT) for h in range(m.heads)]
    U = len(units)
    with nc.Block() as block:
        @block.tensor
        def _(pe):
            def scores(u):
                qi, h = units[u]
                if u >= 2:
                    pe.wait_ge(S["exp"], u - 1)
                for c in range(T // TILE):
                    ins = pe.matmul(k.bank[:, 2 * (u % 2) + c, :], m.q[:, h, P * qi:P * qi + P], m.k[:, tok(c)], start=True, stop=True)
                ins.then_inc(S["scores"], 1)

            def turn(u):
                pe.wait_ge(S["exp"], u + 1)
                for half in range(2):
                    if u >= 1:
                        pe.wait_ge(S["low"], 2 * (u - 1) + half + 1)
                    for c in range(4):
                        at = P * (4 * half + c)
                        ins = pe.transpose(k.bank[:, 4 + half, P * c:P * c + P], m.p[:, u % 2, at:at + P], k.ident[:, :])
                    ins.then_inc(S[("turned_a", "turned_b")[half]], 1)

            def weigh(u):
                qi, h = units[u]
                pe.wait_ge(S["high"], 2 * u + 2)
                if u >= 2:
                    pe.wait_ge(S["read"], u - 1)
                for c in range(KT):
                    pe.matmul(k.bank[:, 6 + u % 2, 0:3 * m.dh], m.pt[:, u % 3, 0, c, :], m.vp[:, c, h, :, :].rearrange("p a b -> p (a b)"), start=c == 0, stop=False)
                pe.wait_ge(S["low"], 2 * u + 2)
                for c in range(KT):
                    ins = pe.matmul(k.bank[:, 6 + u % 2, 0:2 * m.dh], m.pt[:, u % 3, 1, c, :], m.vp[:, c, h, 0:2, :].rearrange("p a b -> p (a b)"), start=False, stop=c == KT - 1)
                ins.then_inc(S["pv"], 1)

            scores(0)
            scores(1)
            for u in range(U):
                turn(u)
                if u:
                    weigh(u - 1)
                if u + 2 < U:
                    scores(u + 2)
            weigh(U - 1)

        @block.vector
        def _(dve):
            def low_part(u):
                for half in range(2):
                    dve.wait_ge(S["high"], 2 * u + half + 1)
                    if u >= 3:
                        dve.wait_ge(S["pv"], u - 2)
                    high, low = (m.pt[:, u % 3, n, 4 * half:4 * half + 4, :].rearrange("p a b -> p (a b)") for n in range(2))
                    dve.tensor_tensor(low, k.bank[:, 4 + half, :], high, ALU.subtract).then_inc(S["low"], 1)

            def finish(u):
                qi, h = units[u]
                dve.wait_ge(S["exp"], u + 1)
                dve.reciprocal(m.sum[:, u % 4:u % 4 + 1], m.sum[:, u % 4:u % 4 + 1]).then_inc(S["recip"], 1)
                dve.wait_ge(S["pv"], u + 1)
                dve.tensor_reduce(m.raw[:, u % 2, :], k.bank[:, 6 + u % 2, 0:3 * m.dh].rearrange("p (a b) -> p b a", a=3), AX.X, ALU.add).then_inc(S["read"], 1)
                dve.wait_ge(S["recip"], u + 1)
                dve.wait_ge(S["read"], u + 1)
                dve.tensor_scalar(m.o[:, qi, m.dh * h:m.dh * h + m.dh], m.raw[:, u % 2, :], m.sum[:, u % 4:u % 4 + 1], None, ALU.mult).then_inc(S["o"], 1)

            for u in range(U):
                dve.wait_ge(S["scores"], u + 1)
                if u >= 4:
                    dve.wait_ge(S["exp"], u - 3)
                raw = k.bank[:, 2 * (u % 2):2 * (u % 2) + 2, :].rearrange("p a b -> p (a b)")
                dve.tensor_reduce(m.top[:, u % 4:u % 4 + 1], raw, AX.X, ALU.max, negate=True).then_inc(S["top"], 1)
                if u:
                    low_part(u - 1)
                if u >= 2:
                    finish(u - 2)
            low_part(U - 1)
            finish(U - 2)
            finish(U - 1)

        @block.scalar
        def _(act):
            def high_part(u):
                for half in range(2):
                    act.wait_ge(S[("turned_a", "turned_b")[half]], u + 1)
                    if u >= 3:
                        act.wait_ge(S["pv"], u - 2)
                    act.copy(m.pt[:, u % 3, 0, 4 * half:4 * half + 4, :].rearrange("p a b -> p (a b)"), k.bank[:, 4 + half, :]).then_inc(S["high"], 1)

            for u in range(U):
                if u:
                    high_part(u - 1)
                act.wait_ge(S["top"], u + 1)
                if u >= 2:
                    act.wait_ge(S["turned_b"], u - 1)
                if u >= 4:
                    act.wait_ge(S["o"], u - 3)
                raw = k.bank[:, 2 * (u % 2):2 * (u % 2) + 2, :].rearrange("p a b -> p (a b)")
                act.activation(m.p[:, u % 2, :], raw, ACT.Exp, bias=m.top[:, u % 4:u % 4 + 1],
                               accum_out=m.sum[:, u % 4:u % 4 + 1]).then_inc(S["exp"], 1)
            high_part(U - 1)


def split_values(dve, own, m, v):
    whole = v.rearrange("p a (h d) -> p a h d", h=m.heads)
    rest = m.v[:, :, :].rearrange("p a (h d) -> p a h d", h=m.heads)
    own.link(dve.tensor_copy(m.vp[:, :, :, 0, :], whole))
    own.link(dve.tensor_tensor(rest, whole, m.vp[:, :, :, 0, :], ALU.subtract))
    own.link(dve.tensor_copy(m.vp[:, :, :, 1, :], rest))
    own.link(dve.tensor_tensor(rest, rest, m.vp[:, :, :, 1, :], ALU.subtract))
    own.did(dve.tensor_copy(m.vp[:, :, :, 2, :], rest))


def wide_attention(k, w):
    nc = k.nc
    KT = T // P
    with ExitStack() as ctx:
        ot = k.sb(ctx, "l2a_ot", [P, PAIRS, N])
        S = {n: k.sem(k.ctx, "l2a_" + n) for n in ("head", "loaded", "xb", "q", "k", "v", "qc", "kc", "vc", "turned", "ot", "post", "gelu", "mm", "s")}
        with ExitStack() as actx:
            m = Full(k, actx, "l2a", 2, DH)
            xb = k.sb(actx, "l2a_xb", [P, T])
            wt = k.sb(actx, "l2a_w", [P, 3, P])
            head = k.sb(actx, "l2a_head", [P, 2])
            with nc.Block() as block:
                @block.sync
                def _(sp):
                    sp.dma_start(head[:, :], w["head"]).then_inc(S["head"], 16)
                    sp.wait_ge(S["head"], 16)
            with nc.Fori(0, B) as b:
                with nc.Block() as block:
                    @block.vector
                    def _(dve):
                        dve.tensor_copy(xb[:, :], k.xn[:, bass.ds(b * T, T)]).then_inc(S["xb"], 1)
                        dve.wait_ge(S["xb"], 1)
                with nc.Fori(0, PAIRS) as pair:
                    with nc.Block() as block:
                        @block.sync
                        def _(sp):
                            sp.dma_start(wt[:, :, :].rearrange("p a b -> p (a b)"), w["qkv"][bass.ds(pair, 1)].rearrange("a p n -> p (a n)")).then_inc(S["loaded"], 16)

                        @block.tensor
                        def _(pe):
                            pe.wait_ge(S["loaded"], 16)
                            for i in range(KT):
                                ins = pe.matmul(k.bank[:, 4 + i // 4, P * (i % 4):P * (i % 4) + P], xb[:, P * i:P * i + P], wt[:, 2, :], start=True, stop=True)
                            ins.then_inc(S["v"], 1)
                            for c in range(BT):
                                ins = pe.matmul(k.bank[:, c, :], wt[:, 0, :], xb[:, tok(c)], start=True, stop=True)
                            ins.then_inc(S["q"], 1)
                            for c in range(BT):
                                ins = pe.matmul(k.bank[:, 2 + c, :], wt[:, 1, :], xb[:, tok(c)], start=True, stop=True)
                            ins.then_inc(S["k"], 1)

                        @block.scalar
                        def _(act):
                            act.wait_ge(S["k"], 1)
                            act.copy(m.k[:, :], k.bank[:, 2:4, :].rearrange("p a b -> p (a b)")).then_inc(S["kc"], 1)
                            act.wait_ge(S["q"], 1)
                            for h in range(2):
                                act.activation(m.q[:, h, :], k.bank[:, 0:2, :].rearrange("p a b -> p (a b)"), ACT.Copy, scale=head[:, h:h + 1]).then_inc(S["qc"], 1)

                        @block.vector
                        def _(dve):
                            dve.wait_ge(S["v"], 1)
                            split_values(dve, Steps(dve, m.S["vsplit"]), m, k.bank[:, 4:6, :].rearrange("p a (b c) -> p (a b) c", c=P))

                    full_attention(k, m)
                    with nc.Block() as block:
                        @block.tensor
                        def _(pe):
                            for i in range(KT):
                                ins = pe.transpose(k.bank[:, i // 4, P * (i % 4):P * (i % 4) + P], m.o[:, i, :], k.ident[:, :])
                            ins.then_inc(S["turned"], 1)

                        @block.scalar
                        def _(act):
                            act.wait_ge(S["turned"], 1)
                            flat = ot[:, :, :].rearrange("p a b -> p (a b)")
                            act.copy(flat[:, bass.ds(pair * N + b * T, T)], k.bank[:, 0:2, :].rearrange("p a b -> p (a b)")).then_inc(S["ot"], 1)
                    clear(nc, [S[n] for n in ("loaded", "q", "k", "v", "qc", "kc", "vc", "turned", "ot")] + list(m.S.values()))
                clear(nc, [S["xb"]])
        wp = k.sb(ctx, "l2a_wp", [P, PAIRS, D])
        with nc.Block() as block:
            @block.sync
            def _(sp):
                sp.dma_start(wp[:, :, :], w["post"]).then_inc(S["post"], 16)

            @block.scalar
            def _(act):
                for t in range(NT):
                    for pair in range(PAIRS):
                        act.activation(ot[:, pair, tok(t)], ot[:, pair, tok(t)], ACT.Gelu).then_inc(S["gelu"], 1)

            @block.tensor
            def _(pe):
                pe.wait_ge(S["post"], 16)
                for t in range(NT):
                    for pair in range(PAIRS):
                        pe.wait_ge(S["gelu"], PAIRS * t + pair + 1)
                        ins = pe.matmul(k.bank[:, t, :], wp[:, pair, :], ot[:, pair, tok(t)], start=pair == 0, stop=pair == PAIRS - 1)
                    ins.then_inc(S["mm"], 1)

            @block.vector
            def _(dve):
                for t in range(NT):
                    dve.wait_ge(S["mm"], t + 1)
                    dve.tensor_tensor(k.s[:, tok(t)], k.xn[:, tok(t)], k.bank[:, t, :], ALU.add).then_inc(S["s"], 1)


def rope_attention(k, w):
    nc = k.nc
    KT = T // P
    G, GH, HD = 4, 4, D // HEADS
    GW = 4 * P + GH * HD + 4 + GH * HD
    with ExitStack() as ctx:
        S = {n: k.sem(k.ctx, "l3a_" + n) for n in (
            "fixed", "loaded", "xb", "qz", "qk", "cos", "sin", "sum", "v", "vc", "kept", "turned", "ot", "mm", "s")}
        lx = k.sb(ctx, "l3a_lx", [P, N])
        col = k.sb(ctx, "l3a_cols", [P, 3])
        wo = k.sb(ctx, "l3a_wo", [P, D])
        rope = k.sb(ctx, "l3a_rope", [P, 4, T])
        m = Full(k, ctx, "l3a", GH, HD)
        xb = k.sb(ctx, "l3a_xb", [P, T])
        wt = k.sb(ctx, "l3a_w", [P, GW])
        q = k.sb(ctx, "l3a_qall", [P, T])
        head = k.sb(ctx, "l3a_head", [P, GH])
        part = k.sb(ctx, "l3a_part", [P, 2, 2, TILE])
        o = k.sb(ctx, "l3a_oall", [P, KT, D])
        ot = k.sb(ctx, "l3a_ot", [P, T])
        with nc.Block() as block:
            @block.sync
            def _(sp):
                for dst, src in ((col[:, :], w["cols"]), (wo[:, :], w["out"]), (rope[:, :, :], w["rope"]), (head[:, :], w["head"])):
                    sp.dma_start(dst, src).then_inc(S["fixed"], 16)
                sp.wait_ge(S["fixed"], 64)
        layer_norm(k, "l3a_ln", k.xn, lx, gamma=col[:, 0:1], beta=col[:, 1:2])
        with nc.Fori(0, B) as b:
            with nc.Block() as block:
                @block.vector
                def _(dve):
                    dve.tensor_copy(xb[:, :], lx[:, bass.ds(b * T, T)]).then_inc(S["xb"], 1)
                    dve.wait_ge(S["xb"], 1)
            with nc.Fori(0, G) as g:
                with nc.Block() as block:
                    @block.sync
                    def _(sp):
                        sp.dma_start(wt[:, :], w["qkv"][bass.ds(g, 1)].rearrange("a p n -> p (a n)")).then_inc(S["loaded"], 16)

                    @block.tensor
                    def _(pe):
                        pe.wait_ge(S["loaded"], 16)
                        for i in range(2 * BT):
                            if i >= 3:
                                pe.wait_ge(S["sin"], i - 2)
                            for j in range(2):
                                ins = pe.matmul(k.bank[:, 2 * (i % 3) + j, :], wt[:, P * (2 * (i // BT) + j):P * (2 * (i // BT) + j) + P], xb[:, tok(i % BT)], start=True, stop=True)
                            ins.then_inc(S["qk"], 1)
                        for i in range(KT):
                            ins = pe.matmul(k.bank[:, 6, GH * HD * i:GH * HD * i + GH * HD], xb[:, P * i:P * i + P], wt[:, 4 * P:4 * P + GH * HD], start=True, stop=True)
                        ins.then_inc(S["v"], 1)

                    @block.vector
                    def _(dve):
                        bias = 4 * P + GH * HD
                        dve.wait_ge(S["loaded"], 16)
                        for i in range(2 * BT):
                            dve.wait_ge(S["qk"], i + 1)
                            if i >= 2:
                                dve.wait_ge(S["sum"], i - 1)
                            for j, sem in enumerate(("cos", "sin")):
                                at = bias + 2 * (i // BT) + j
                                dve.scalar_tensor_tensor(part[:, i % 2, j, :], k.bank[:, 2 * (i % 3) + j, :], wt[:, at:at + 1],
                                                         rope[:, 2 * (i // BT) + j, tok(i % BT)], op0=ALU.add, op1=ALU.mult).then_inc(S[sem], 1)
                        dve.wait_ge(S["v"], 1)
                        dve.tensor_tensor(m.v[:, :, :], k.bank[:, 6, 0:GH * HD * KT].rearrange("p (a b) -> p a b", a=KT),
                                          wt[:, bias + 4:bias + 4 + GH * HD].unsqueeze(1).to_broadcast([P, KT, GH * HD]), ALU.add).then_inc(S["vc"], 1)
                        dve.wait_ge(S["vc"], 1)
                        split_values(dve, Steps(dve, m.S["vsplit"]), m, m.v[:, :, :])

                    @block.gpsimd
                    def _(pool):
                        for i in range(2 * BT):
                            pool.wait_ge(S["cos"], i + 1)
                            pool.wait_ge(S["sin"], i + 1)
                            pool.tensor_tensor((q, m.k)[i // BT][:, tok(i % BT)], part[:, i % 2, 0, :], part[:, i % 2, 1, :], ALU.add).then_inc(S["sum"], 1)

                    @block.scalar
                    def _(act):
                        act.wait_ge(S["sum"], BT)
                        for h in range(GH):
                            act.activation(m.q[:, h, :], q[:, :], ACT.Copy, scale=head[:, h:h + 1]).then_inc(S["qz"], 1)

                full_attention(k, m)
                with nc.Block() as block:
                    @block.vector
                    def _(dve):
                        dve.tensor_copy(o[:, :, bass.ds(g * (GH * HD), GH * HD)], m.o[:, :, :]).then_inc(S["kept"], 1)
                clear(nc, [S[n] for n in ("loaded", "qz", "qk", "cos", "sin", "sum", "v", "vc", "kept")] + list(m.S.values()))
            with nc.Block() as block:
                @block.tensor
                def _(pe):
                    for i in range(KT):
                        ins = pe.transpose(k.bank[:, i // 4, P * (i % 4):P * (i % 4) + P], o[:, i, :], k.ident[:, :])
                    ins.then_inc(S["turned"], 1)
                    pe.wait_ge(S["ot"], 1)
                    for c in range(BT):
                        ins = pe.matmul(k.bank[:, 2 + c, :], wo[:, :], ot[:, tok(c)], start=True, stop=True)
                    ins.then_inc(S["mm"], 1)

                @block.scalar
                def _(act):
                    act.wait_ge(S["turned"], 1)
                    act.copy(ot[:, :], k.bank[:, 0:2, :].rearrange("p a b -> p (a b)")).then_inc(S["ot"], 1)

                @block.vector
                def _(dve):
                    dve.wait_ge(S["mm"], 1)
                    dve.scalar_tensor_tensor(k.s[:, bass.ds(b * T, T)], k.bank[:, 2:4, :].rearrange("p a b -> p (a b)"), col[:, 2:3],
                                             k.xn[:, bass.ds(b * T, T)], op0=ALU.add, op1=ALU.add).then_inc(S["s"], 1)
            clear(nc, [S[n] for n in ("xb", "turned", "ot", "mm", "s")])


class Quantiser:

    def __init__(self, k, ctx, name, most):
        self.most, self.sl = most, []
        for i in range(2):
            self.sl.append({n: k.sb(ctx, f"{name}_{n}{i}", [P, most // (QB if n in ("top", "scale", "inv") else 1)])
                            for n in ("a", "sign", "t", "q", "top", "scale", "inv")})
        self.S = {n: k.sem(k.ctx, f"{name}_{n}") for n in ("own", "a", "signed", "q", "done")}

    def views(self, j, x):
        nb = x.shape[1] // QB
        b = self.sl[j % 2]

        def blocks(ap):
            return ap.rearrange("p (a b) -> p a b", b=QB)

        def wide(t):
            return t[:, 0:nb].unsqueeze(2).to_broadcast([P, nb, QB])

        return b, nb, blocks, wide

    def vector_scale(self, dve, own, j, x):
        b, nb, blocks, wide = self.views(j, x)
        F = x.shape[1]
        if j >= 2:
            dve.wait_ge(self.S["done"], j - 1)
        own.link(dve.tensor_reduce(b["top"][:, 0:nb], blocks(x), AX.X, ALU.max, apply_absolute_value=True))
        own.link(dve.tensor_scalar(b["scale"][:, 0:nb], b["top"][:, 0:nb], 1.0 / 6.0, 1e-12, ALU.mult, ALU.max))
        own.link(dve.reciprocal(b["inv"][:, 0:nb], b["scale"][:, 0:nb]))
        dve.tensor_tensor(blocks(b["a"][:, 0:F]), blocks(x), wide(b["inv"]), ALU.mult).then_inc(self.S["a"], 1)

    def scalar_sign(self, act, j, x):
        b, nb, blocks, wide = self.views(j, x)
        F = x.shape[1]
        act.wait_ge(self.S["a"], j + 1)
        act.activation(b["sign"][:, 0:F], b["a"][:, 0:F], ACT.Sign).then_inc(self.S["signed"], 1)
        act.activation(b["t"][:, 0:F], b["a"][:, 0:F], ACT.Abs).then_inc(self.S["signed"], 1)

    def vector_round(self, dve, own, j, x):
        b, nb, blocks, wide = self.views(j, x)
        F = x.shape[1]
        t, q, a, sign = (b[n][:, 0:F] for n in ("t", "q", "a", "sign"))
        dve.wait_ge(self.S["signed"], 2 * j + 2)
        own.did(dve.tensor_scalar(a, t, 1.75, None, ALU.is_gt))
        own.link(dve.tensor_scalar(q, t, 5.0, 2.0, ALU.is_gt, ALU.mult))
        own.link(dve.scalar_tensor_tensor(q, t, 3.5, q, op0=ALU.is_gt, op1=ALU.add))
        own.link(dve.scalar_tensor_tensor(q, t, 2.5, q, op0=ALU.is_gt, op1=ALU.add))
        own.link(dve.scalar_tensor_tensor(q, q, 2.0, a, op0=ALU.mult, op1=ALU.add))
        for mid in (1.25, 0.75, 0.25):
            own.link(dve.scalar_tensor_tensor(q, t, mid, q, op0=ALU.is_gt, op1=ALU.add))
        dve.scalar_tensor_tensor(q, q, 0.5, sign, op0=ALU.mult, op1=ALU.mult).then_inc(self.S["q"], 1)

    def pool_rescale(self, pool, j, x):
        b, nb, blocks, wide = self.views(j, x)
        pool.wait_ge(self.S["q"], j + 1)
        pool.tensor_tensor(blocks(x), blocks(b["q"][:, 0:x.shape[1]]), wide(b["scale"]), ALU.mult).then_inc(self.S["done"], 1)


def fp4_ffn(k, w):
    nc = k.nc
    MT = N // P
    HC = (FFI + P - 1) // P
    LAST = FFI - P * (HC - 1)
    WW = 2 * HC * P + FFI
    with ExitStack() as ctx:
        z = k.sb(ctx, "fp4_z", [P, WW + N])
        wt = k.sb(ctx, "fp4_wt", [P, 3, HC, P])
        xq = k.sb(ctx, "fp4_xq", [P, N])
        h = k.sb(ctx, "fp4_h", [P, MT, FFI])
        ht = k.sb(ctx, "fp4_ht", [P, HC, N])
        a = k.sb(ctx, "fp4_silu", [P, 2, FFI])
        qz = Quantiser(k, ctx, "fp4_q", 1056)
        S = {n: k.sem(k.ctx, "fp4_" + n) for n in ("loaded", "turned", "xt", "wturned", "wt", "xturned", "xq",
                                                   "gate", "up", "silu", "h", "hturned", "ht", "mm", "g")}
        slices = [slice(1056 * j, min(1056 * j + 1056, WW + N)) for j in range(-(-(WW + N) // 1056))]
        assert all((s.stop - s.start) % QB == 0 for s in slices)
        with nc.Block() as block:
            @block.sync
            def _(sp):
                sp.dma_start(z[:, 0:WW], w["w"]).then_inc(S["loaded"], 16)

            @block.tensor
            def _(pe):
                for i in range(MT):
                    pe.transpose(k.bank[:, i // 4, P * (i % 4):P * (i % 4) + P], k.xn[:, P * i:P * i + P], k.ident[:, :]).then_inc(S["turned"], 1)
                pe.wait_ge(qz.S["done"], len(slices))
                for n in range(3):
                    for c in range(HC):
                        at = P * (HC * n + c)
                        width = LAST if n == 2 and c == HC - 1 else P
                        ins = pe.transpose(k.bank[0:width, 4 + n, P * c:P * c + P], z[:, at:at + width], k.ident[:, :])
                    ins.then_inc(S["wturned"], 1)
                pe.wait_ge(S["xt"], 1)
                for i in range(MT):
                    pe.transpose(k.bank[:, i // 4, P * (i % 4):P * (i % 4) + P], z[:, WW + P * i:WW + P * i + P], k.ident[:, :]).then_inc(S["xturned"], 1)

            @block.scalar
            def _(act):
                act.wait_ge(S["turned"], MT)
                act.copy(z[:, WW:WW + N], k.bank[:, 0:4, :].rearrange("p a b -> p (a b)")).then_inc(S["xt"], 1)
                for j, s in enumerate(slices):
                    qz.scalar_sign(act, j, z[:, s])
                act.wait_ge(S["xturned"], MT)
                act.copy(xq[:, :], k.bank[:, 0:4, :].rearrange("p a b -> p (a b)")).then_inc(S["xq"], 1)

            @block.vector
            def _(dve):
                own = Steps(dve, qz.S["own"])
                dve.wait_ge(S["loaded"], 16)
                dve.wait_ge(S["xt"], 1)
                for j, s in enumerate(slices):
                    qz.vector_scale(dve, own, j, z[:, s])
                    if j:
                        qz.vector_round(dve, own, j - 1, z[:, slices[j - 1]])
                qz.vector_round(dve, own, len(slices) - 1, z[:, slices[-1]])
                dve.wait_ge(S["wturned"], 3)
                dve.tensor_copy(wt[:, 0:2, :, :].rearrange("p a b c -> p a (b c)"), k.bank[:, 4:6, 0:HC * P]).then_inc(S["wt"], 1)
                dve.tensor_copy(wt[:, 2, 0:HC - 1, :].rearrange("p a b -> p (a b)"), k.bank[:, 6, 0:(HC - 1) * P]).then_inc(S["wt"], 1)
                dve.tensor_copy(wt[0:LAST, 2, HC - 1, :], k.bank[0:LAST, 6, (HC - 1) * P:HC * P]).then_inc(S["wt"], 1)

            @block.gpsimd
            def _(pool):
                for j, s in enumerate(slices):
                    qz.pool_rescale(pool, j, z[:, s])

        clear(nc, qz.S.values())
        with nc.Block() as block:
            GROUP = 2
            hs = [h[:, GROUP * j:GROUP * j + GROUP, :].rearrange("p a b -> p (a b)") for j in range(MT // GROUP)]

            @block.tensor
            def _(pe):
                for i in range(MT):
                    if i >= 2:
                        pe.wait_ge(S["silu"], i - 1)
                    pe.matmul(k.bank[:, i % 2, 0:FFI], xq[:, P * i:P * i + P], wt[:, 0, :, :].rearrange("p a b -> p (a b)")[:, 0:FFI], start=True, stop=True).then_inc(S["gate"], 1)
                    if i >= 2:
                        pe.wait_ge(S["h"], i - 1)
                    pe.matmul(k.bank[:, 2 + i % 2, 0:FFI], xq[:, P * i:P * i + P], wt[:, 1, :, :].rearrange("p a b -> p (a b)")[:, 0:FFI], start=True, stop=True).then_inc(S["up"], 1)
                for i in range(MT):
                    pe.wait_ge(qz.S["done"], i // GROUP + 1)
                    if i >= 2:
                        pe.wait_ge(S["ht"], 2 * i - 2)
                    for c in range(HC):
                        width = min(P, FFI - P * c)
                        ins = pe.transpose(k.bank[0:width, 4 + i % 2, P * c:P * c + P], h[:, i, P * c:P * c + width], k.ident[:, :])
                    ins.then_inc(S["hturned"], 1)
                    if i % 4 == 3:
                        t = i // 4
                        pe.wait_ge(S["ht"], 2 * i + 2)
                        if t >= 2:
                            pe.wait_ge(S["g"], t - 1)
                        for c in range(HC):
                            width = min(P, FFI - P * c)
                            ins = pe.matmul(k.bank[:, 6 + t % 2, :], wt[0:width, 2, c, :], ht[0:width, c, tok(t)], start=c == 0, stop=c == HC - 1)
                        ins.then_inc(S["mm"], 1)

            @block.scalar
            def _(act):
                def finish(i):
                    act.wait_ge(S["hturned"], i + 1)
                    act.copy(ht[:, 0:HC - 1, P * i:P * i + P], k.bank[:, 4 + i % 2, 0:(HC - 1) * P].rearrange("p (a b) -> p a b", b=P)).then_inc(S["ht"], 1)
                    act.copy(ht[0:LAST, HC - 1, P * i:P * i + P], k.bank[0:LAST, 4 + i % 2, (HC - 1) * P:HC * P]).then_inc(S["ht"], 1)

                for i in range(MT):
                    act.wait_ge(S["gate"], i + 1)
                    if i >= 2:
                        act.wait_ge(S["h"], i - 1)
                    act.activation(a[:, i % 2, :], k.bank[:, i % 2, 0:FFI], ACT.Silu).then_inc(S["silu"], 1)
                for j in range(MT // GROUP):
                    qz.scalar_sign(act, j, hs[j])
                for i in range(MT):
                    finish(i)
                    if i % 4 == 3:
                        t = i // 4
                        act.wait_ge(S["mm"], t + 1)
                        act.activation(k.g[:, tok(t)], k.bank[:, 6 + t % 2, :], ACT.Silu).then_inc(S["g"], 1)

            @block.vector
            def _(dve):
                own = Steps(dve, qz.S["own"])
                for i in range(MT):
                    dve.wait_ge(S["silu"], i + 1)
                    dve.wait_ge(S["up"], i + 1)
                    dve.tensor_tensor(h[:, i, :], k.bank[:, 2 + i % 2, 0:FFI], a[:, i % 2, :], ALU.mult).then_inc(S["h"], 1)
                dve.wait_ge(S["h"], MT)
                for j in range(MT // GROUP):
                    qz.vector_scale(dve, own, j, hs[j])
                    if j:
                        qz.vector_round(dve, own, j - 1, hs[j - 1])
                qz.vector_round(dve, own, MT // GROUP - 1, hs[-1])

            @block.gpsimd
            def _(pool):
                for j in range(MT // GROUP):
                    qz.pool_rescale(pool, j, hs[j])


def window_layers(k, w):
    nc = k.nc
    HALO = 32
    CT = HALO + T
    TI = TILE // P
    NR = 2 * PAIRS
    with ExitStack() as ctx:
        x = k.xn
        sh = k.sb(ctx, "l3f_sh", [P, B, CT])
        raw = k.sb(ctx, "l3f_tables", [P, 4, T])
        mask = k.sb(ctx, "l3f_mask", [P, 2, 64])
        heads = k.sb(ctx, "l3f_heads", [P, NR, 2 * NR])
        sel = k.sb(ctx, "l3f_sel", [2 * PAIRS, PAIRS, P])
        S = {n: k.sem(k.ctx, "l3f_" + n) for n in (
            "fixed", "zeros", "wloaded", "shift", "xb", "table", "qk", "sq", "n2", "nt", "ntt", "inv", "iturned", "it", "spread",
            "cos", "sin", "sum", "kdone", "vmm", "vc", "rq", "carry", "nothing", "own", "g")}
        with nc.Block() as block:
            @block.sync
            def _(sp):
                for dst, src in ((raw[:, :, :], w["tables"]), (mask[:, :, :], w["mask"]), (heads[:, :, :], w["heads"]), (sel[:, :, :], w["sel"])):
                    sp.dma_start(dst, src).then_inc(S["fixed"], 16)
                sp.wait_ge(S["fixed"], 64)

            @block.vector
            def _(dve):
                dve.memset(sh[:, :, :], 0.0).then_inc(S["zeros"], 1)
                dve.wait_ge(S["zeros"], 1)
        with nc.Fori(0, DEPTH) as layer:
            with nc.Block() as block:
                @block.scalar
                def _(act):
                    act.copy(sh[0:64, :, HALO:], x[0:64, :].rearrange("p (a b) -> p a b", a=B)).then_inc(S["shift"], 1)

                @block.vector
                def _(dve):
                    dve.tensor_copy(sh[64:P, :, HALO + 1:], x[64:P, :].rearrange("p (a b) -> p a b", a=B)[:, :, 0:T - 1]).then_inc(S["zeros"], 1)
                    dve.memset(sh[64:P, :, HALO:HALO + 1], 0.0).then_inc(S["zeros"], 1)
            with ExitStack() as actx:
                m = Local(k, actx, "l3f", WIN)
                wq = k.sb(actx, "l3f_wq", [P, 2, NR, P])
                wv = k.sb(actx, "l3f_wv", [P, 2, PAIRS * DH])
                wo = k.sb(actx, "l3f_wo", [P, PAIRS, D])
                qs = k.sb(actx, "l3f_qs", [P, 4])
                table = k.sb(actx, "l3f_table", [P, 4, TILE])
                xb = k.sb(actx, "l3f_xb", [P, HALO + TILE])
                sq = k.sb(actx, "l3f_sq", [P, 2, TILE])
                part = k.g[:, :].rearrange("p (a b c) -> p a b c", a=2, b=2)
                nt = k.sb(actx, "l3f_nt", [2 * NR, TILE])
                n2 = k.sb(actx, "l3f_norm", [P, TI, 2 * NR])
                ik = k.sb(actx, "l3f_ik", [2 * PAIRS, TILE])
                with nc.Block() as block:
                    @block.sync
                    def _(sp):
                        for dst, src in ((wq[:, :, :, :].rearrange("p a b c -> p (a b c)"), w["wqk"]), (wv[:, :, :].rearrange("p a b -> p (a b)"), w["wv"]),
                                         (wo[:, :, :].rearrange("p a b -> p (a b)"), w["wo"]), (qs[:, :], w["qs"])):
                            sp.dma_start(dst, src[bass.ds(layer, 1)].rearrange("a p n -> p (a n)")).then_inc(S["wloaded"], 16)
                        sp.wait_ge(S["wloaded"], 64)

                with nc.Fori(0, B) as b:
                    with nc.Block() as block:
                        @block.gpsimd
                        def _(pool):
                            pool.memset(m.k[:, :, 0:HALO], 0.0).then_inc(S["nothing"], 1)
                    with nc.Fori(0, BT) as c:
                        EARLY = m.nw // 2

                        def window_values(pe, i, psum):
                            for p in range(2):
                                ins = pe.matmul(psum[64 * p:64 * p + 64, :], xb[:, WIN * i:WIN * i + 64], wv[:, p, :], start=True, stop=True)
                            return ins

                        with nc.Block() as block:
                            def dest(i):
                                return m.q[:, i, :] if i < PAIRS else m.k[:, i - PAIRS, HALO:]

                            @block.scalar
                            def _(act):
                                act.copy(xb[:, :], sh[:, :, :].rearrange("p a b -> p (a b)")[:, bass.ds(b * CT + c * TILE, HALO + TILE)]).then_inc(S["xb"], 1)
                                for i in range(NR):
                                    act.wait_ge(S["qk"], i + 1)
                                    if i >= 2:
                                        act.wait_ge(S["n2"], i - 1)
                                    act.activation(sq[:, i % 2, :], k.bank[:, 2 * (i % 3), :], ACT.Square).then_inc(S["sq"], 1)
                                act.wait_ge(S["n2"], NR)
                                act.activation(nt[:, :], k.bank[0:2 * NR, 6, :], ACT.Sqrt).then_inc(S["nt"], 1)
                                for i in range(0, EARLY, 2):
                                    act.wait_ge(S["vmm"], i + 1)
                                    act.copy(m.v[:, i, :], k.bank[:, i % 4, :]).then_inc(S["vc"], 1)
                                    if i == 4:
                                        act.wait_ge(S["iturned"], 1)
                                        act.copy(ik[:, :], k.bank[0:2 * PAIRS, 6, :]).then_inc(S["it"], 1)

                            @block.tensor
                            def _(pe):
                                def norms(i):
                                    pe.wait_ge(S["sq"], i + 1)
                                    pe.matmul(k.bank[0:2 * NR, 6, :], heads[:, i, :], sq[:, i % 2, :], start=i == 0, stop=i == NR - 1).then_inc(S["n2"], 1)

                                def early(i):
                                    if i >= 4:
                                        pe.wait_ge(S["vc" if i % 2 == 0 else "rq"], (i - 4) // 2 + 1)
                                    window_values(pe, i, k.bank[:, i % 4, :]).then_inc(S["vmm"], 1)

                                pe.wait_ge(S["xb"], 1)
                                for i in range(NR):
                                    if i >= 3:
                                        pe.wait_ge(S["cos"], i - 2)
                                        pe.wait_ge(S["sin"], i - 2)
                                        pe.wait_ge(S["sq"], i - 2)
                                    for j in range(2):
                                        ins = pe.matmul(k.bank[:, 2 * (i % 3) + j, :], wq[:, j, i, :], xb[:, HALO:], start=True, stop=True)
                                    ins.then_inc(S["qk"], 1)
                                    if i:
                                        norms(i - 1)
                                norms(NR - 1)
                                pe.wait_ge(S["sin"], NR)
                                pe.wait_ge(S["cos"], NR)
                                early(0)
                                pe.wait_ge(S["nt"], 1)
                                for j in range(TI):
                                    ins = pe.transpose(k.bank[:, 7, 2 * NR * j:2 * NR * j + 2 * NR], nt[:, P * j:P * j + P], k.ident[0:2 * NR, 0:2 * NR])
                                ins.then_inc(S["ntt"], 1)
                                for i in range(1, 4):
                                    early(i)
                                pe.wait_ge(S["inv"], 1)
                                for j in range(TI):
                                    ins = pe.transpose(k.bank[0:2 * PAIRS, 6, P * j:P * j + P], n2[:, j, NR:2 * NR], k.ident[:, :])
                                ins.then_inc(S["iturned"], 1)
                                for i in range(4, EARLY):
                                    early(i)
                                pe.wait_ge(S["it"], 1)
                                for i in range(PAIRS):
                                    if i >= 3:
                                        pe.wait_ge(S["kdone"], i - 2)
                                    pe.matmul(k.bank[:, (4, 5, 7)[i % 3], :], sel[:, i, :], ik[:, :], start=True, stop=True).then_inc(S["spread"], 1)

                            @block.gpsimd
                            def _(pool):
                                for i in range(NR):
                                    pool.wait_ge(S["cos"], i + 1)
                                    pool.wait_ge(S["sin"], i + 1)
                                    pool.tensor_tensor(dest(i), part[:, i % 2, 0, :], part[:, i % 2, 1, :], ALU.add).then_inc(S["sum"], 1)

                            @block.vector
                            def _(dve):
                                own = Steps(dve, S["own"])
                                for n in range(4):
                                    dve.tensor_scalar(table[:, n, :], raw[:, n, bass.ds(c * TILE, TILE)], qs[:, n:n + 1], None, ALU.mult).then_inc(S["table"], 1)
                                dve.wait_ge(S["table"], 4)
                                for i in range(NR):
                                    dve.wait_ge(S["qk"], i + 1)
                                    dve.wait_ge(S["sq"], i + 1)
                                    if i >= 2:
                                        dve.wait_ge(S["sum"], i - 1)
                                    for j, sem in enumerate(("cos", "sin")):
                                        dve.tensor_tensor(part[:, i % 2, j, :], k.bank[:, 2 * (i % 3) + j, :], table[:, 2 * (i // PAIRS) + j, :], ALU.mult).then_inc(S[sem], 1)
                                flat = n2[:, :, :].rearrange("p a b -> p (a b)")
                                dve.wait_ge(S["ntt"], 1)
                                own.link(dve.tensor_scalar(flat, k.bank[:, 7, 0:TI * 2 * NR], 1e-12, None, ALU.max))
                                own.link(dve.reciprocal(flat, flat))
                                dve.tensor_scalar(n2[:, :, 0:NR], n2[:, :, 0:NR], 8.0, None, ALU.mult).then_inc(S["inv"], 1)
                                for i in range(1, EARLY, 2):
                                    dve.wait_ge(S["vmm"], i + 1)
                                    dve.tensor_copy(m.v[:, i, :], k.bank[:, i % 4, :]).then_inc(S["rq"], 1)
                                for i in range(PAIRS):
                                    dve.wait_ge(S["spread"], i + 1)
                                    dve.wait_ge(S["sum"], PAIRS + i + 1)
                                    dve.tensor_tensor(m.k[:, i, HALO:], m.k[:, i, HALO:], k.bank[:, (4, 5, 7)[i % 3], :], ALU.mult).then_inc(S["kdone"], 1)

                        def store(dve, psum):
                            at = x[:, bass.ds(b * T + c * TILE, TILE)]
                            return dve.tensor_tensor(at, psum, at, ALU.add)

                        def add(i):
                            wide = [P, 2 * PAIRS, 64]
                            if i:
                                return mask[:, 1, :].unsqueeze(1).to_broadcast(wide)
                            return mask[:, bass.ds(c, 1), :].to_broadcast(wide)

                        local_attention(k, m, 1.0, wo, store, qscale=lambda i: n2[:, i, 0:NR], mask=add,
                                        values=(window_values, range(EARLY, m.nw)))
                        with nc.Block() as block:
                            @block.gpsimd
                            def _(pool):
                                pool.tensor_copy(m.k[:, :, 0:HALO], m.k[:, :, TILE:]).then_inc(S["carry"], 1)
                        clear(nc, [S[n] for n in ("xb", "table", "qk", "sq", "n2", "nt", "ntt", "inv", "iturned", "it", "spread", "cos", "sin",
                                                  "sum", "kdone", "vmm", "vc", "rq", "carry", "own")] + list(m.S.values()))
                clear(nc, [S["wloaded"], S["shift"], S["nothing"], S["zeros"]])
            gated_layer(k, w, S, layer, x, sh)
        with nc.Block() as block:
            @block.scalar
            def _(act):
                for t in range(NT):
                    act.activation(k.g[:, tok(t)], x[:, tok(t)], ACT.Silu).then_inc(S["g"], 1)


def gated_layer(k, w, S, layer, x, sh):
    nc = k.nc
    HALO = 32
    LAST = DI - P * (DI3 - 1)
    with ExitStack() as ctx:
        w1 = k.sb(ctx, "l3g_w1", [P, 2 * DI])
        w2 = k.sb(ctx, "l3g_w2", [P, DI3, D])
        col = k.sb(ctx, "l3g_cols", [P, 9])
        sx = k.sb(ctx, "l3g_sx", [P, N])
        nx = k.sb(ctx, "l3g_nx", [P, N])
        ge = k.sb(ctx, "l3g_gelu", [P, 2, TILE])
        h = k.sb(ctx, "l3g_h", [P, 2, DI3, TILE])
        R = {n: k.sem(k.ctx, "l3g_" + n) for n in ("w", "shift", "gate", "a", "gelu", "h", "mm", "x")}
        ln = [k.sem(k.ctx, "l3g_ln_" + n) for n in ("mean", "centred", "squared", "var", "std", "dve")]
        with nc.Block() as block:
            @block.sync
            def _(sp):
                for dst, src in ((w1[:, :], w["w1"]), (w2[:, :, :].rearrange("p a b -> p (a b)"), w["w2"]), (col[:, :], w["cols"])):
                    sp.dma_start(dst, src[bass.ds(layer, 1)].rearrange("a p n -> p (a n)")).then_inc(R["w"], 16)
                sp.wait_ge(R["w"], 48)

            @block.scalar
            def _(act):
                act.copy(sx[0:64, :], x[0:64, :]).then_inc(R["shift"], 1)

            @block.vector
            def _(dve):
                halves = (x[64:P, :].rearrange("p (a b) -> p a b", a=B), sx[64:P, :].rearrange("p (a b) -> p a b", a=B))
                dve.tensor_copy(halves[1][:, :, 1:], halves[0][:, :, 0:T - 1]).then_inc(R["shift"], 1)
                dve.memset(halves[1][:, :, 0:1], 0.0).then_inc(R["shift"], 1)
        layer_norm(k, "l3g_ln", sx, nx, gamma=col[:, 0:1], beta=col[:, 1:2], sems=ln)
        with nc.Block() as block:
            @block.tensor
            def _(pe):
                def first(t):
                    for o in range(DI3):
                        i = DI3 * t + o
                        width = min(P, DI - P * o)
                        if i >= 2:
                            pe.wait_ge(R["gelu"], i - 1)
                        pe.matmul(k.bank[0:width, i % 2, :], w1[:, DI + P * o:DI + P * o + width], nx[:, tok(t)], start=True, stop=True).then_inc(R["gate"], 1)
                        if i >= 2:
                            pe.wait_ge(R["h"], i - 1)
                        pe.matmul(k.bank[0:width, 2 + i % 2, :], w1[:, P * o:P * o + width], nx[:, tok(t)], start=True, stop=True).then_inc(R["a"], 1)

                first(0)
                for t in range(NT):
                    if t + 1 < NT:
                        first(t + 1)
                    pe.wait_ge(R["h"], DI3 * (t + 1))
                    if t >= 2:
                        pe.wait_ge(R["x"], t - 1)
                    for o in range(DI3):
                        width = min(P, DI - P * o)
                        ins = pe.matmul(k.bank[:, 4 + t % 2, :], w2[0:width, o, :], h[0:width, t % 2, o, :], start=o == 0, stop=o == DI3 - 1)
                    ins.then_inc(R["mm"], 1)

            @block.scalar
            def _(act):
                for i in range(NT * DI3):
                    o = i % DI3
                    width = min(P, DI - P * o)
                    act.wait_ge(R["gate"], i + 1)
                    if i >= 2:
                        act.wait_ge(R["h"], i - 1)
                    act.activation(ge[0:width, i % 2, :], k.bank[0:width, i % 2, :], ACT.Gelu, bias=col[0:width, 6 + o:7 + o]).then_inc(R["gelu"], 1)

            @block.vector
            def _(dve):
                def add(t):
                    dve.wait_ge(R["mm"], t + 1)
                    dve.scalar_tensor_tensor(x[:, tok(t)], k.bank[:, 4 + t % 2, :], col[:, 2:3], x[:, tok(t)], op0=ALU.add, op1=ALU.add).then_inc(R["x"], 1)

                for t in range(NT):
                    if t >= 2:
                        dve.wait_ge(R["mm"], t - 1)
                    for o in range(DI3):
                        i = DI3 * t + o
                        width = min(P, DI - P * o)
                        dve.wait_ge(R["gelu"], i + 1)
                        dve.wait_ge(R["a"], i + 1)
                        dve.scalar_tensor_tensor(h[0:width, t % 2, o, :], k.bank[0:width, 2 + i % 2, :], col[0:width, 3 + o:4 + o], ge[0:width, i % 2, :],
                                                 op0=ALU.add, op1=ALU.mult).then_inc(R["h"], 1)
                    if t:
                        add(t - 1)
                add(NT - 1)
        clear(nc, list(R.values()) + ln)


def store_out(k, src, out):
    nc = k.nc
    stored = k.sem(k.ctx, "out_stored")
    with nc.Block() as block:
        @block.sync
        def _(sp):
            sp.dma_start(out, src[:, :]).then_inc(stored, 16)
            sp.wait_ge(stored, 16)


def program(nc, a, out):
    with ExitStack() as ctx:
        k = Core(nc, ctx)
        load_start(k, a["x"], a)

        def arrays(prefix):
            return {n[len(prefix):]: v for n, v in a.items() if n.startswith(prefix)}

        with k.stage():
            layer_norm(k, "ln0", k.x, k.xn)
            gated_scan(k, arrays("l0a_"))
            ternary_ffn(k, arrays("l0f_"))
            combine(k, "l0")
        with k.stage():
            layer_norm(k, "ln1", k.x, k.xn)
            chunk_attention(k, arrays("l1a_"))
            mixture(k, arrays("moe_"))
            combine(k, "l1")
        with k.stage():
            layer_norm(k, "ln2", k.x, k.xn)
            wide_attention(k, arrays("l2a_"))
            fp4_ffn(k, arrays("fp4_"))
            combine(k, "l2")
        with k.stage():
            layer_norm(k, "ln3", k.x, k.xn)
            rope_attention(k, arrays("l3a_"))
            window_layers(k, arrays("l3f_"))
            combine(k, "l3")
        store_out(k, k.x, out)


def columns(v):
    return v.reshape(-1, P).T


def lay_out(i):
    a = {}
    a["x"] = i["L0_attn_x"].reshape(N, D).T
    a["ident"] = np.eye(P, dtype=np.float32)
    a["mean_w"] = np.full((P, P), 1.0 / P, np.float32)
    a["eps"] = np.tile(np.array([[LN_EPS, RMS_EPS]], np.float32), (P, 1))
    a["l0a_qkv"] = i["L0_attn_w_qkv"].T
    a["l0a_swiglu"] = i["L0_attn_w_swiglu"].T
    a["l0a_out"] = i["L0_attn_w_out"].T
    a["l0f_w12"] = np.stack([i["L0_ffn_w1_w"].T, i["L0_ffn_w2_w"].T], 1)
    a["l0f_h"] = np.stack([i[f"L0_ffn_{n}_w"].T.reshape(4, P, 512).transpose(1, 0, 2) for n in ("h1", "h2")], 1)
    a["l0f_w3"] = i["L0_ffn_w3_w"].T.reshape(4, P, D).transpose(1, 0, 2)
    a["l0f_scales"] = np.concatenate([columns(i[f"L0_ffn_{n}_s"]) for n in ("w1", "w2", "h1", "h2", "w3")], 1)
    qkv = i["L1_attn_w_qkv"].T
    a["l1a_qk"] = qkv[:, :2 * INNER].reshape(D, 2 * PAIRS, P)
    a["l1a_v"] = by_parity(qkv[:, 2 * INNER:])
    a["l1a_out"] = pair_rows(i["L1_attn_w_out"].T)
    a["l1a_b"] = i["L1_attn_b_out"].reshape(D, 1)
    a["moe_wg"] = i["L1_ffn_Wg"]
    a["moe_b2"] = i["L1_ffn_b2"]
    a["moe_rank"] = np.tile(np.arange(EXPERTS, 0, -1, dtype=np.float32), (P, 1))
    a["moe_ws"] = np.stack([i["L1_ffn_Ws1"], i["L1_ffn_Ws11"]], 1)
    a["moe_ws2"] = i["L1_ffn_Ws2"].reshape(SH // P, P, D).transpose(1, 0, 2)
    a["moe_bs"] = np.concatenate([columns(i["L1_ffn_bs1"]), columns(i["L1_ffn_bs11"]), columns(i["L1_ffn_bs2"])], 1)
    experts = [np.concatenate([i["L1_ffn_W1"][e], i["L1_ffn_W11"][e], i["L1_ffn_W2"][e][:P], i["L1_ffn_W2"][e][P:],
                               columns(i["L1_ffn_b1"][e]), columns(i["L1_ffn_b11"][e])], 1) for e in range(EXPERTS)]
    a["moe_experts"] = np.stack(experts + experts[:2])
    a["l2a_qkv"] = np.stack([i[f"L2_attn_W{n}"].reshape(D, PAIRS, P) for n in "qkv"], 2).transpose(1, 0, 2, 3).reshape(PAIRS, D, 3 * P)
    a["l2a_post"] = pair_rows(i["L2_attn_Wpost"])
    a["fp4_w"] = np.concatenate([np.pad(i[f"L2_ffn_w_{n}"], ((0, 3 * P - FFI), (0, 0))).reshape(3, P, D).transpose(1, 0, 2).reshape(P, 3 * P)
                                 for n in ("gate", "up")] + [i["L2_ffn_w_down"]], 1)
    for n, table in zip(("tables", "mask", "heads", "sel"), window_constants()):
        a["l3f_" + n] = table
    qkv = i["L3_ffn_Wqkv"]
    qk = qkv[:, :, :2 * INNER].reshape(DEPTH, D, 2 * PAIRS, 2, 2, 32)
    a["l3f_wqk"] = np.concatenate([qk.reshape(DEPTH, D, -1), qk[:, :, :, :, ::-1].reshape(DEPTH, D, -1)], 2)
    a["l3f_wv"] = np.stack([by_parity(v).reshape(D, -1) for v in qkv[:, :, 2 * INNER:]])
    a["l3f_wo"] = np.stack([pair_rows(v).reshape(P, -1) for v in i["L3_ffn_Wo"]])
    scales = [i["L3_ffn_q_scale"], i["L3_ffn_k_scale"]]
    a["l3f_qs"] = np.stack([np.tile(v, (1, 2)) for s in scales for v in (s, np.roll(s, 32, 1))], 2)
    a["l3f_w1"] = i["L3_ffn_W1"]
    a["l3f_w2"] = np.pad(i["L3_ffn_W2"], ((0, 0), (0, DI3 * P - DI), (0, 0))).reshape(DEPTH, DI3, P, D).transpose(0, 2, 1, 3).reshape(DEPTH, P, -1)
    b1 = np.pad(i["L3_ffn_b1"].reshape(DEPTH, 2, DI), ((0, 0), (0, 0), (0, DI3 * P - DI))).reshape(DEPTH, 2 * DI3, P).transpose(0, 2, 1)
    a["l3f_cols"] = np.concatenate([np.stack([i["L3_ffn_ln_g"], i["L3_ffn_ln_b"], i["L3_ffn_b2"]], 2), b1], 2)
    a["l2a_head"] = (np.repeat(np.eye(2), 64, 0) * DH ** -0.5).astype(np.float32)
    a["l3a_head"] = np.repeat(np.eye(4), 32, 0).astype(np.float32)
    a["l3a_cols"] = np.stack([i["L3_attn_gamma"], i["L3_attn_beta"], i["L3_attn_b_out"]], 1)
    a["l3a_out"] = i["L3_attn_W_out"]
    a["l3a_qkv"] = rope_weights(i["L3_attn_W_in"], i["L3_attn_b_in"])
    a["l3a_rope"] = rope_tables()
    return a


def by_parity(v):
    return v.reshape(D, PAIRS, 2, DH).transpose(0, 2, 1, 3).reshape(D, 2, PAIRS * DH)


def pair_rows(v):
    return v.reshape(PAIRS, P, -1).transpose(1, 0, 2)


def rope_weights(w, b):
    rows = []
    wb = np.concatenate([w, b[None]], 0).reshape(D + 1, 3, 4, 4, 8)
    partner = [1, 0, 3, 2]
    for g in range(4):
        tiles = []
        for n in range(2):
            straight, rotated = (np.zeros((D + 1, 4, 32), np.float32) for _ in range(2))
            straight[:, :, :8] = wb[:, n, g]
            rotated[:, :, :4] = wb[:, n, g][:, :, partner]
            tiles += [straight.reshape(D + 1, P), rotated.reshape(D + 1, P)]
        v = wb[:, 2, g].reshape(D + 1, 32)
        weights = [x[:D] for x in tiles] + [v[:D]]
        biases = [x[D].reshape(P, 1) for x in tiles] + [np.tile(v[D], (P, 1))]
        rows.append(np.concatenate(weights + biases, 1))
    return np.stack(rows)


def rope_tables():
    inv = (1.0 / 10000.0 ** (np.arange(0, 4, 2, dtype=np.float32) / np.float32(4))).astype(np.float32)
    angle = np.repeat(np.arange(T, dtype=np.float32)[:, None] * inv[None], 2, 1).T
    cos, sin = np.zeros((2, 4, 32, T), np.float32)
    cos[:, :4], cos[:, 4:8] = np.cos(angle), 1.0
    sin[:, :4] = np.sin(angle) * np.array([-1, 1, -1, 1], np.float32)[:, None]
    cos, sin = cos.reshape(P, T), sin.reshape(P, T)
    scale = np.float32(8 ** -0.5)
    return np.stack([cos * scale, sin * scale, cos, sin], 1)


def window_constants():
    half = np.arange(0, DH, 2, dtype=np.float32)
    inv = (1.0 / 10000.0 ** (half / np.float32(DH))).astype(np.float32)
    t = np.arange(T, dtype=np.float32)
    angle = t[:, None] * inv[None]
    angle = np.concatenate([angle, angle], 1).T
    base = ((half + np.float32(0.4 * DH)) / np.float32(1.4 * DH)).astype(np.float32)
    power = (t - T // 2) / (WIN // 2)
    scale = (base[None] ** power[:, None]).astype(np.float32)
    scale = np.concatenate([scale, scale], 1).T
    sign = np.where(np.arange(DH) < DH // 2, -1.0, 1.0).astype(np.float32)[:, None]
    tables = np.stack([np.cos(angle) * scale, sign * np.sin(angle) * scale, np.cos(angle) / scale, sign * np.sin(angle) / scale], 1)
    q, j = np.arange(WIN)[:, None], np.arange(2 * WIN)[None]
    fits = (q <= j) & (j <= q + WIN)
    usual = np.tile(np.where(fits, 0.0, -3e38), (4, 1))
    first = usual.copy()
    first[:WIN, :WIN] = -3e38
    masks = np.stack([first, usual], 1)
    heads = np.zeros((P, 2 * PAIRS, 4 * PAIRS))
    for i in range(2 * PAIRS):
        heads[:64, i, 2 * i] = heads[64:, i, 2 * i + 1] = 1.0
    sel = np.stack([np.repeat(np.eye(2 * PAIRS)[:, 2 * p:2 * p + 2], 64, 1) for p in range(PAIRS)], 1)
    return (np.tile(tables, (2, 1, 1)).astype(np.float32), masks.astype(np.float32),
            heads.astype(np.float32), sel.astype(np.float32))


def kernel(**inputs):
    import concourse.bacc as bacc
    from concourse.bass_utils import run_bass_kernel_spmd as run

    nc = bacc.Bacc("TRN2", target_bir_lowering=False, num_devices=1)
    arrays = {n: np.ascontiguousarray(v) for n, v in lay_out({n: np.asarray(v) for n, v in inputs.items()}).items()}
    aps = {n: nc.dram_tensor("in_" + n, v.shape, F32, kind="ExternalInput").ap() for n, v in arrays.items()}
    out = nc.dram_tensor("out", (D, N), F32, kind="ExternalOutput").ap()
    program(nc, aps, out)
    r = run(nc, [{"in_" + n: v for n, v in arrays.items()}], core_ids=[0])
    return np.ascontiguousarray(r.results[0]["out"].T).reshape(B, T, D)
```

```python
from contextlib import ExitStack, contextmanager

import numpy as np

import concourse.bass as bass
from concourse import mybir

F32 = mybir.dt.float32
BF16 = mybir.dt.bfloat16
ALU = mybir.AluOpType
ACT = mybir.ActivationFunctionType
AX = mybir.AxisListType

P = 128
D = 128
B, T = 2, 1024
N = B * T
TILE = 512
NT = N // TILE
BT = T // TILE
HEADS, DH = 16, 64
PAIRS = HEADS // 2
INNER = HEADS * DH
WIN = 32
DEPTH = 6
EXPERTS, EH, SH = 16, 256, 512
FFI = 352
QB = 16
DI = 341
DI3 = 3
RMS_EPS = 1.1920929e-07
LN_EPS = 1e-05


def tok(t):
    return slice(TILE * t, TILE * t + TILE)


class Steps:

    def __init__(self, eng, sem):
        self.eng, self.sem, self.n = eng, sem, 0

    def did(self, ins):
        ins.then_inc(self.sem, 1)
        self.n += 1

    def settle(self):
        self.eng.wait_ge(self.sem, self.n)

    def link(self, ins):
        self.did(ins)
        self.settle()


class Core:

    def __init__(self, nc, ctx):
        self.nc, self.ctx, self.sems = nc, ctx, []
        self.x = self.sb(ctx, "x_stream", [P, N])
        self.xn = self.sb(ctx, "x_normed", [P, N])
        self.s = self.sb(ctx, "s_branch", [P, N])
        self.g = self.sb(ctx, "g_branch", [P, N])
        self.ident = self.sb(ctx, "ident", [P, P])
        self.mean_w = self.sb(ctx, "mean_w", [P, P])
        self.eps = self.sb(ctx, "eps_cols", [P, 2])
        self.bank = ctx.enter_context(nc.psum_tensor("banks", [P, 8, TILE], F32))

    def sb(self, ctx, name, shape, dt=F32):
        return ctx.enter_context(self.nc.sbuf_tensor(name, shape, dt))

    def sem(self, ctx, name):
        self.sems.append(ctx.enter_context(self.nc.semaphore(name)))
        return self.sems[-1]

    @contextmanager
    def stage(self):
        outer, self.sems = self.ctx, []
        with ExitStack() as self.ctx:
            yield
            clear(self.nc, self.sems)
        self.ctx = outer


def clear(nc, sems):
    with nc.Block(no_gpsimd_drain=True) as block:
        @block.sync
        def _(sp):
            for s in sems:
                sp.sem_clear(s)


def load_start(k, x, consts):
    nc = k.nc
    loaded = k.sem(k.ctx, "start_loaded")
    with nc.Block() as block:
        @block.sync
        def _(sp):
            sp.dma_start(k.x[:, :], x).then_inc(loaded, 16)
            sp.dma_start(k.ident[:, :], consts["ident"]).then_inc(loaded, 16)
            sp.dma_start(k.mean_w[:, :], consts["mean_w"]).then_inc(loaded, 16)
            sp.dma_start(k.eps[:, :], consts["eps"]).then_inc(loaded, 16)
            sp.wait_ge(loaded, 64)


def layer_norm(k, name, src, dst, gamma=None, beta=None, sems=None):
    nc = k.nc
    with ExitStack() as ctx:
        sq = k.sb(ctx, f"{name}_sq", [P, 2, TILE])
        rstd = k.sb(ctx, f"{name}_rstd", [P, 2, TILE])
        mean_done, centred, squared, var_done, std_done, dve_own = sems or [
            k.sem(k.ctx, f"{name}_{s}") for s in ("mean", "centred", "squared", "var", "std", "dve")]
        with nc.Block() as block:
            @block.tensor
            def _(pe):
                def mean(t):
                    if t >= 2:
                        pe.wait_ge(centred, t - 1)
                    pe.matmul(k.bank[:, t % 2, :], k.mean_w[:, :], src[:, tok(t)], start=True, stop=True).then_inc(mean_done, 1)

                mean(0)
                for t in range(NT):
                    if t + 1 < NT:
                        mean(t + 1)
                    pe.wait_ge(squared, t + 1)
                    if t >= 2:
                        pe.wait_ge(std_done, t - 1)
                    pe.matmul(k.bank[:, 2 + t % 2, :], k.mean_w[:, :], sq[:, t % 2, :], start=True, stop=True).then_inc(var_done, 1)

            @block.vector
            def _(dve):
                own = Steps(dve, dve_own)

                def finish(t):
                    dve.wait_ge(std_done, t + 1)
                    own.link(dve.reciprocal(rstd[:, t % 2, :], rstd[:, t % 2, :]))
                    own.did(dve.tensor_tensor(dst[:, tok(t)], dst[:, tok(t)], rstd[:, t % 2, :], ALU.mult))
                    if gamma is not None:
                        own.settle()
                        own.did(dve.tensor_scalar(dst[:, tok(t)], dst[:, tok(t)], gamma, beta, ALU.mult, ALU.add))

                for t in range(NT):
                    dve.wait_ge(mean_done, t + 1)
                    dve.tensor_tensor(dst[:, tok(t)], src[:, tok(t)], k.bank[:, t % 2, :], ALU.subtract).then_inc(centred, 1)
                    if t:
                        finish(t - 1)
                finish(NT - 1)

            @block.scalar
            def _(act):
                for t in range(NT):
                    act.wait_ge(centred, t + 1)
                    if t >= 2:
                        act.wait_ge(var_done, t - 1)
                    act.activation(sq[:, t % 2, :], dst[:, tok(t)], ACT.Square).then_inc(squared, 1)
                    act.wait_ge(var_done, t + 1)
                    if t >= 2:
                        act.wait_ge(dve_own, (3 if gamma is not None else 2) * (t - 1))
                    act.activation(rstd[:, t % 2, :], k.bank[:, 2 + t % 2, :], ACT.Sqrt, bias=k.eps[:, 0:1]).then_inc(std_done, 1)


def combine(k, name):
    nc = k.nc
    done = k.sem(k.ctx, f"{name}_combined")
    with nc.Block() as block:
        @block.vector
        def _(dve):
            own = Steps(dve, done)
            for t in range(NT):
                own.did(dve.tensor_tensor(k.s[:, tok(t)], k.s[:, tok(t)], k.g[:, tok(t)], ALU.mult))
            for t in range(NT):
                dve.wait_ge(done, t + 1)
                own.did(dve.tensor_tensor(k.x[:, tok(t)], k.x[:, tok(t)], k.s[:, tok(t)], ALU.add))


def gated_scan(k, w):
    nc = k.nc
    with ExitStack() as ctx:
        wt = k.sb(ctx, "l0a_w", [P, 3 * D + 2 * D + D])
        wq, wsw, wo = wt[:, 0:3 * D], wt[:, 3 * D:5 * D], wt[:, 5 * D:6 * D]
        ones = k.sb(ctx, "l0a_ones", [P, TILE])
        bufs = {n: k.sb(ctx, "l0a_" + n, [P, N]) for n in ("a", "b", "xr", "q", "k", "v", "y")}
        a, b, xr, q, kk, v, y = (bufs[n] for n in ("a", "b", "xr", "q", "k", "v", "y"))
        S = {n: k.sem(k.ctx, "l0a_" + n) for n in (
            "loaded", "sq", "ms", "std", "xr", "mm", "qsq", "qms", "qstd", "qn", "copied",
            "sig", "exp", "y", "uv", "silu", "h", "out", "dve", "stored")}
        with nc.Block() as block:
            @block.sync
            def _(sp):
                sp.dma_start(wq, w["qkv"]).then_inc(S["loaded"], 16)
                sp.dma_start(wsw, w["swiglu"]).then_inc(S["loaded"], 16)
                sp.dma_start(wo, w["out"]).then_inc(S["loaded"], 16)

            @block.tensor
            def _(pe):
                for t in range(NT):
                    pe.wait_ge(S["sq"], t + 1)
                    if t >= 2:
                        pe.wait_ge(S["std"], t - 1)
                    pe.matmul(k.bank[:, t % 2, :], k.mean_w[:, :], a[:, tok(t)], start=True, stop=True).then_inc(S["ms"], 1)
                pe.wait_ge(S["loaded"], 48)
                for t in range(NT):
                    pe.wait_ge(S["xr"], t + 1)
                    for j in range(3):
                        i = 3 * t + j
                        if i >= 6:
                            pe.wait_ge(S["copied"], i - 5)
                        pe.matmul(k.bank[:, 2 + i % 6, :], wq[:, D * j:D * j + D], xr[:, tok(t)], start=True, stop=True).then_inc(S["mm"], 1)
                pe.wait_ge(S["std"], NT)
                for i in range(2 * NT):
                    pe.wait_ge(S["qsq"], i + 1)
                    if i >= 2:
                        pe.wait_ge(S["qstd"], i - 1)
                    src = (a if i % 2 == 0 else b)
                    pe.matmul(k.bank[:, i % 2, :], k.mean_w[:, :], src[:, tok(i // 2)], start=True, stop=True).then_inc(S["qms"], 1)
                pe.wait_ge(S["copied"], 3 * NT)
                for t in range(NT):
                    pe.wait_ge(S["y"], t + 1)
                    if t >= 2:
                        pe.wait_ge(S["h"], t - 1)
                    for j in range(2):
                        pe.matmul(k.bank[:, 2 + 2 * (t % 2) + j, :], wsw[:, D * j:D * j + D], y[:, tok(t)], start=True, stop=True).then_inc(S["uv"], 1)
                for t in range(NT):
                    pe.wait_ge(S["h"], t + 1)
                    if t >= 2:
                        pe.wait_ge(S["stored"], t - 1)
                    pe.matmul(k.bank[:, 6 + t % 2, :], wo, a[:, tok(t)], start=True, stop=True).then_inc(S["out"], 1)

            @block.scalar
            def _(act):
                for t in range(NT):
                    act.activation(a[:, tok(t)], k.xn[:, tok(t)], ACT.Square).then_inc(S["sq"], 1)
                for t in range(NT):
                    act.wait_ge(S["ms"], t + 1)
                    act.activation(b[:, tok(t)], k.bank[:, t % 2, :], ACT.Sqrt, bias=k.eps[:, 1:2]).then_inc(S["std"], 1)
                for t in range(NT):
                    for j, dst in enumerate((q, kk, v)):
                        act.wait_ge(S["mm"], 3 * t + j + 1)
                        act.copy(dst[:, tok(t)], k.bank[:, 2 + (3 * t + j) % 6, :]).then_inc(S["copied"], 1)
                act.wait_ge(S["xr"], NT)
                act.wait_ge(S["copied"], 3 * NT)
                for i in range(2 * NT):
                    dst, src = ((a, q), (b, kk))[i % 2]
                    act.activation(dst[:, tok(i // 2)], src[:, tok(i // 2)], ACT.Square).then_inc(S["qsq"], 1)
                for i in range(2 * NT):
                    act.wait_ge(S["qms"], i + 1)
                    dst = (a, b)[i % 2]
                    act.activation(dst[:, tok(i // 2)], k.bank[:, i % 2, :], ACT.Sqrt, bias=k.eps[:, 1:2]).then_inc(S["qstd"], 1)
                for t in range(NT):
                    act.wait_ge(S["qn"], 2 * t + 2)
                    act.activation(kk[:, tok(t)], kk[:, tok(t)], ACT.Exp).then_inc(S["exp"], 1)
                for t in range(NT):
                    act.activation(q[:, tok(t)], q[:, tok(t)], ACT.Sigmoid).then_inc(S["sig"], 1)
                for t in range(NT):
                    act.wait_ge(S["uv"], 2 * t + 2)
                    act.activation(b[:, tok(t)], k.bank[:, 3 + 2 * (t % 2), :], ACT.Silu).then_inc(S["silu"], 1)

            @block.vector
            def _(dve):
                own = Steps(dve, S["dve"])
                own.did(dve.memset(ones[:, :], 1.0))
                for t in range(NT):
                    dve.wait_ge(S["std"], t + 1)
                    own.link(dve.reciprocal(b[:, tok(t)], b[:, tok(t)]))
                    dve.tensor_tensor(xr[:, tok(t)], k.xn[:, tok(t)], b[:, tok(t)], ALU.mult).then_inc(S["xr"], 1)
                for i in range(2 * NT):
                    dve.wait_ge(S["qstd"], i + 1)
                    r, z = ((a, q), (b, kk))[i % 2]
                    own.link(dve.reciprocal(r[:, tok(i // 2)], r[:, tok(i // 2)]))
                    dve.tensor_tensor(z[:, tok(i // 2)], z[:, tok(i // 2)], r[:, tok(i // 2)], ALU.mult).then_inc(S["qn"], 1)
                for t in range(NT):
                    dve.wait_ge(S["exp"], t + 1)
                    dve.wait_ge(S["qn"], 2 * NT)
                    own.link(dve.tensor_tensor(v[:, tok(t)], v[:, tok(t)], kk[:, tok(t)], ALU.mult))
                    first = t % BT == 0
                    before = slice(TILE * t - 1, TILE * t)
                    own.did(dve.tensor_tensor_scan(a[:, tok(t)], ones[:, :], kk[:, tok(t)], 0.0 if first else a[:, before], ALU.mult, ALU.add))
                    own.link(dve.tensor_tensor_scan(y[:, tok(t)], ones[:, :], v[:, tok(t)], 0.0 if first else y[:, before], ALU.mult, ALU.add))
                for t in range(NT):
                    own.link(dve.tensor_scalar(a[:, tok(t)], a[:, tok(t)], 1e-6, None, ALU.add))
                    own.link(dve.reciprocal(a[:, tok(t)], a[:, tok(t)]))
                    own.link(dve.tensor_tensor(y[:, tok(t)], y[:, tok(t)], a[:, tok(t)], ALU.mult))
                    dve.wait_ge(S["sig"], t + 1)
                    dve.tensor_tensor(y[:, tok(t)], y[:, tok(t)], q[:, tok(t)], ALU.mult).then_inc(S["y"], 1)
                for t in range(NT):
                    dve.wait_ge(S["silu"], t + 1)
                    dve.tensor_tensor(a[:, tok(t)], k.bank[:, 2 + 2 * (t % 2), :], b[:, tok(t)], ALU.mult).then_inc(S["h"], 1)
                for t in range(NT):
                    dve.wait_ge(S["out"], t + 1)
                    dve.tensor_tensor(k.s[:, tok(t)], k.xn[:, tok(t)], k.bank[:, 6 + t % 2, :], ALU.add).then_inc(S["stored"], 1)


def ternary_ffn(k, w):
    nc = k.nc
    H = 4
    with ExitStack() as ctx:
        w12 = k.sb(ctx, "l0f_w12", [P, 2, 512])
        wh = k.sb(ctx, "l0f_wh", [P, 2, H, 512])
        w3 = k.sb(ctx, "l0f_w3", [P, H, D])
        sc = k.sb(ctx, "l0f_scales", [P, 17])
        act_a = k.sb(ctx, "l0f_act", [P, 2, TILE])
        ha = k.sb(ctx, "l0f_ha", [P, H, N])
        hb = k.sb(ctx, "l0f_hb", [P, H, N])
        S = {n: k.sem(k.ctx, "l0f_" + n) for n in ("loaded", "gate", "up", "silu", "h0", "mm1", "h1", "mm2", "h2", "mm3", "g")}
        with nc.Block() as block:
            @block.sync
            def _(sp):
                sp.dma_start(w12[:, :, :], w["w12"]).then_inc(S["loaded"], 16)
                sp.dma_start(sc[:, :], w["scales"]).then_inc(S["loaded"], 16)
                sp.dma_start(wh[:, :, :, :], w["h"]).then_inc(S["loaded"], 16)
                sp.dma_start(w3[:, :, :], w["w3"]).then_inc(S["loaded"], 16)

            @block.tensor
            def _(pe):
                pe.wait_ge(S["loaded"], 64)
                for i in range(NT * H):
                    t, o = i // H, i % H
                    if i >= 2:
                        pe.wait_ge(S["silu"], i - 1)
                    pe.matmul(k.bank[:, i % 2, :], w12[:, 0, P * o:P * o + P], k.xn[:, tok(t)], start=True, stop=True).then_inc(S["gate"], 1)
                    if i >= 2:
                        pe.wait_ge(S["h0"], i - 1)
                    pe.matmul(k.bank[:, 2 + i % 2, :], w12[:, 1, P * o:P * o + P], k.xn[:, tok(t)], start=True, stop=True).then_inc(S["up"], 1)
                for layer, (src, before, mm, after) in enumerate(((ha, "h0", "mm1", "h1"), (hb, "h1", "mm2", "h2"))):
                    for i in range(NT * H):
                        t, o = i // H, i % H
                        pe.wait_ge(S[before], H * (t + 1))
                        if i >= 4:
                            pe.wait_ge(S[after], i - 3)
                        elif layer:
                            pe.wait_ge(S[before], NT * H)
                        for c in range(H):
                            ins = pe.matmul(k.bank[:, 4 + i % 4, :], wh[:, layer, c, P * o:P * o + P], src[:, c, tok(t)], start=c == 0, stop=c == H - 1)
                        ins.then_inc(S[mm], 1)
                for t in range(NT):
                    pe.wait_ge(S["h2"], H * (t + 1))
                    for c in range(H):
                        ins = pe.matmul(k.bank[:, t, :], w3[:, c, :], ha[:, c, tok(t)], start=c == 0, stop=c == H - 1)
                    ins.then_inc(S["mm3"], 1)

            @block.scalar
            def _(act):
                act.wait_ge(S["loaded"], 64)
                for i in range(NT * H):
                    act.wait_ge(S["gate"], i + 1)
                    if i >= 2:
                        act.wait_ge(S["h0"], i - 1)
                    act.activation(act_a[:, i % 2, :], k.bank[:, i % 2, :], ACT.Silu, scale=sc[:, i % H:i % H + 1]).then_inc(S["silu"], 1)
                for layer, (dst, mm, after) in enumerate(((hb, "mm1", "h1"), (ha, "mm2", "h2"))):
                    for i in range(NT * H):
                        t, o = i // H, i % H
                        act.wait_ge(S[mm], i + 1)
                        if layer:
                            act.wait_ge(S["mm1"], NT * H)
                        act.activation(dst[:, o, tok(t)], k.bank[:, 4 + i % 4, :], ACT.Gelu,
                                       scale=sc[:, 8 + 4 * layer + o:9 + 4 * layer + o]).then_inc(S[after], 1)
                for t in range(NT):
                    act.wait_ge(S["mm3"], t + 1)
                    act.activation(k.g[:, tok(t)], k.bank[:, t, :], ACT.Silu, scale=sc[:, 16:17]).then_inc(S["g"], 1)

            @block.vector
            def _(dve):
                dve.wait_ge(S["loaded"], 64)
                for i in range(NT * H):
                    t, o = i // H, i % H
                    dve.wait_ge(S["silu"], i + 1)
                    dve.wait_ge(S["up"], i + 1)
                    dve.scalar_tensor_tensor(ha[:, o, tok(t)], k.bank[:, 2 + i % 2, :], sc[:, 4 + o:5 + o], act_a[:, i % 2, :],
                                             op0=ALU.mult, op1=ALU.mult).then_inc(S["h0"], 1)


class Local:

    def __init__(self, k, ctx, name, win):
        self.name, self.win, self.halo = name, win, 64 - win
        self.nw = TILE // win
        self.q = k.sb(ctx, name + "_q", [P, PAIRS, TILE])
        self.k = k.sb(ctx, name + "_k", [P, PAIRS, self.halo + TILE])
        self.v = k.sb(ctx, name + "_v", [P, self.nw, PAIRS * DH])
        self.p = k.sb(ctx, name + "_p", [P, 2, PAIRS, 2, 64])
        self.pt = k.sb(ctx, name + "_pt", [P, 2, PAIRS, P])
        self.ov = k.sb(ctx, name + "_ov", [P, PAIRS, 2, DH])
        self.o = k.sb(ctx, name + "_o", [P, PAIRS, TILE])
        self.top = k.sb(ctx, name + "_top", [P, 2, 2 * PAIRS])
        self.sum = k.sb(ctx, name + "_sum", [P, 2, 2 * PAIRS])
        self.S = {n: k.sem(k.ctx, f"{name}_{n}") for n in (
            "scores", "read", "masked", "shifted", "exp", "recip", "turned", "pt", "pv", "ov", "back", "o", "dve", "values", "vcopied", "vcopied_too", "carried", "out", "stored")}


def local_attention(k, m, scale, wo, store, qscale=None, mask=None, values=None, carry=None):
    nc, S, W = k.nc, m.S, m.win
    TI = TILE // P
    JW = P // W
    project, halves, late = values or (None, None, range(0))
    ahead, behind = range(min(4, len(late))), range(4, len(late))
    with nc.Block() as block:
        @block.tensor
        def _(pe):
            def scores(i):
                if i >= 2:
                    pe.wait_ge(S["read"], i - 1)
                for j in range(JW):
                    for pair in range(PAIRS):
                        for p in range(2):
                            r = slice(64 * p, 64 * p + 64)
                            ins = pe.matmul(k.bank[W * j:W * j + W, 2 * (i % 2) + p, 64 * pair:64 * pair + 64],
                                            m.q[r, pair, P * i + W * j:P * i + W * j + W],
                                            m.k[r, pair, P * i + W * j:P * i + W * j + 64], start=True, stop=True)
                ins.then_inc(S["scores"], 1)

            def turn(i):
                pe.wait_ge(S["exp"], i + 1)
                if i >= 2:
                    pe.wait_ge(S["o"], i - 1)
                for pair in range(PAIRS):
                    ins = pe.transpose(k.bank[:, 4 + pair // 4, P * (pair % 4):P * (pair % 4) + P],
                                       m.p[:, i % 2, pair, :, :].rearrange("p a b -> p (a b)"), k.ident[:, :])
                ins.then_inc(S["turned"], 1)

            def back(i):
                pe.wait_ge(S["ov"], i + 1)
                pe.wait_ge(S["pt"], min(i + 2, TI))
                if i:
                    pe.wait_ge(S["o"], i)
                for pair in range(PAIRS):
                    ins = pe.transpose(k.bank[:, 4 + pair // 4, P * (pair % 4):P * (pair % 4) + P],
                                       m.ov[:, pair, :, :].rearrange("p a b -> p (a b)"), k.ident[:, :])
                ins.then_inc(S["back"], 1)

            def weigh(i):
                pe.wait_ge(S["pt"], i + 1)
                if i:
                    pe.wait_ge(S["ov"], i)
                for j in range(JW):
                    for pair in range(PAIRS):
                        for p in range(2):
                            r = slice(64 * p, 64 * p + 64)
                            ins = pe.matmul(k.bank[W * j:W * j + W, 6 + p, DH * pair:DH * pair + DH],
                                            m.pt[r, i % 2, pair, W * j:W * j + W], m.v[r, JW * i + j, DH * pair:DH * pair + DH], start=True, stop=True)
                ins.then_inc(S["pv"], 1)

            def project_values(ns):
                for n in ns:
                    if n >= 4:
                        pe.wait_ge(S["vcopied"], n - 3)
                        pe.wait_ge(S["vcopied_too"], n - 3)
                    project(pe, late[n], k.bank[:, 4 + n % 4, :]).then_inc(S["values"], 1)

            project_values(ahead)
            scores(0)
            scores(1)
            project_values(behind)
            if late:
                pe.wait_ge(S["vcopied"], len(late))
                pe.wait_ge(S["vcopied_too"], len(late))
            for i in range(TI):
                turn(i)
                if i + 2 < TI:
                    scores(i + 2)
                if i:
                    back(i - 1)
                weigh(i)

            def output(of, to):
                for pair in range(PAIRS):
                    ins = pe.matmul(k.bank[:, 0, of:to], wo[:, pair, :], m.o[:, pair, of:to], start=pair == 0, stop=pair == PAIRS - 1)
                ins.then_inc(S["out"], 1)

            pe.wait_ge(S["read"], TI)
            pe.wait_ge(S["o"], TI - 1)
            output(0, TILE - P)
            back(TI - 1)
            pe.wait_ge(S["o"], TI)
            output(TILE - P, TILE)

        @block.vector
        def _(dve):
            own = Steps(dve, S["dve"])

            def wide(ap):
                return ap.rearrange("p (a b) -> p a b", b=2).unsqueeze(3).to_broadcast([P, PAIRS, 2, 64])

            def by_pair(banks):
                return banks.rearrange("p b (a c) -> p a b c", c=64)

            def finish(i):
                dve.wait_ge(S["pv"], i + 1)
                dve.wait_ge(S["recip"], i + 1)
                if i:
                    dve.wait_ge(S["back"], i)
                dve.tensor_tensor(m.ov[:, :, :, :], by_pair(k.bank[:, 6:8, :]), wide(m.sum[:, i % 2, :]), ALU.mult).then_inc(S["ov"], 1)

            def first(i):
                raw = by_pair(k.bank[:, 2 * (i % 2):2 * (i % 2) + 2, :])
                prob = m.p[:, i % 2, :, :, :]
                dve.wait_ge(S["scores"], i + 1)
                if i >= 2:
                    dve.wait_ge(S["turned"], i - 1)
                if qscale is None:
                    top = m.top[:, i % 2, :]
                    own.link(dve.tensor_reduce(top.rearrange("p (a b) -> p a b", b=2), raw, AX.X, ALU.max))
                    own.link(dve.tensor_tensor(prob, raw, wide(top), ALU.subtract))
                    dve.sem_inc(S["read"], 1)
                    dve.sem_inc(S["shifted"], 1)
                else:
                    dve.tensor_tensor(prob, raw, wide(qscale(i)), ALU.mult).then_inc(S["read"], 1)

            def shift(i):
                flat = m.p[:, i % 2, :, :, :].rearrange("p a b c -> p (a b) c")
                top = m.top[:, i % 2, :]
                if qscale is not None:
                    dve.wait_ge(S["masked"], i + 1)
                    own.link(dve.tensor_reduce(top, flat, AX.X, ALU.max))
                    dve.tensor_tensor(flat, flat, top.unsqueeze(2).to_broadcast([P, 2 * PAIRS, 64]), ALU.subtract).then_inc(S["shifted"], 1)

            def total_of(i):
                flat = m.p[:, i % 2, :, :, :].rearrange("p a b c -> p (a b) c")
                total = m.sum[:, i % 2, :]
                dve.wait_ge(S["exp"], i + 1)
                own.link(dve.tensor_reduce(total, flat, AX.X, ALU.add))
                dve.reciprocal(total, total).then_inc(S["recip"], 1)

            def copy_values(ns):
                for n in ns:
                    dve.wait_ge(S["values"], n + 1)
                    dve.tensor_copy(halves(late[n])[1], k.bank[64:P, 4 + n % 4, :]).then_inc(S["vcopied_too"], 1)

            copy_values(ahead)
            first(0)
            shift(0)
            copy_values(behind)
            for i in range(TI):
                if i + 1 < TI:
                    first(i + 1)
                if i >= 2:
                    dve.wait_ge(S["ov"], i - 1)
                if i:
                    shift(i)
                total_of(i)
                if i:
                    finish(i - 1)
            finish(TI - 1)
            dve.wait_ge(S["out"], 2)
            store(dve, k.bank[:, 0, :]).then_inc(S["stored"], 1)

        @block.scalar
        def _(act):
            def copy_values(ns):
                for n in ns:
                    act.wait_ge(S["values"], n + 1)
                    act.copy(halves(late[n])[0], k.bank[0:64, 4 + n % 4, :]).then_inc(S["vcopied"], 1)

            def exp(i):
                act.wait_ge(S["shifted"], i + 1)
                flat = m.p[:, i % 2, :, :, :].rearrange("p a b c -> p (a b c)")
                act.activation(flat, flat, ACT.Exp, scale=scale).then_inc(S["exp"], 1)

            def copy_back(i):
                act.wait_ge(S["back"], i + 1)
                act.copy(m.o[:, :, P * i:P * i + P], k.bank[:, 4:6, :].rearrange("p a (b c) -> p (a b) c", c=P)).then_inc(S["o"], 1)

            copy_values(ahead)
            exp(0)
            copy_values(behind)
            for i in range(TI):
                act.wait_ge(S["turned"], i + 1)
                if i >= 2:
                    act.wait_ge(S["pv"], i - 1)
                act.copy(m.pt[:, i % 2, :, :].rearrange("p a b -> p (a b)"), k.bank[:, 4:6, :].rearrange("p a b -> p (a b)")).then_inc(S["pt"], 1)
                if i + 1 < TI:
                    exp(i + 1)
                if i:
                    copy_back(i - 1)
            copy_back(TI - 1)

        if mask:
            @block.gpsimd
            def _(pool):
                for i in range(TI):
                    pool.wait_ge(S["read"], i + 1)
                    flat = m.p[:, i % 2, :, :, :].rearrange("p a b c -> p (a b) c")
                    pool.tensor_tensor(flat, flat, mask(i), ALU.add).then_inc(S["masked"], 1)
                if carry:
                    pool.wait_ge(S["scores"], TI)
                    carry(pool).then_inc(S["carried"], 1)


def chunk_attention(k, w):
    nc = k.nc
    with ExitStack() as ctx:
        m = Local(k, ctx, "l1a", 64)
        wqk = k.sb(ctx, "l1a_wqk", [P, 2 * PAIRS, P])
        wv = k.sb(ctx, "l1a_wv", [P, 2, PAIRS * DH])
        wo = k.sb(ctx, "l1a_wo", [P, PAIRS, D])
        bo = k.sb(ctx, "l1a_bo", [P, 1])
        xb = k.sb(ctx, "l1a_xb", [P, TILE])
        loaded = k.sem(k.ctx, "l1a_loaded")
        R = {n: k.sem(k.ctx, "l1a_" + n) for n in ("xb", "mm", "even", "odd")}
        with nc.Block() as block:
            @block.sync
            def _(sp):
                sp.dma_start(wqk[:, :, :], w["qk"]).then_inc(loaded, 16)
                sp.dma_start(wv[:, :, :], w["v"]).then_inc(loaded, 16)
                sp.dma_start(wo[:, :, :], w["out"]).then_inc(loaded, 16)
                sp.dma_start(bo[:, :], w["b"]).then_inc(loaded, 16)
                sp.wait_ge(loaded, 64)
        with nc.Fori(0, NT) as c:
            with nc.Block() as block:
                steps = 2 * PAIRS
                products = m.nw

                def dest(i):
                    if i < PAIRS:
                        return m.q[:, i, :]
                    return m.k[:, i - PAIRS, :]

                def half(e, n):
                    return m.v[64 * (e % 2):64 * (e % 2) + 64, e // 2 * 2 + n, :]

                @block.tensor
                def _(pe):
                    pe.wait_ge(R["xb"], 1)
                    for i in range(steps):
                        if i >= 8:
                            pe.wait_ge(R["odd" if i % 2 else "even"], (i - 8) // 2 + 1)
                        pe.matmul(k.bank[:, i % 8, :], wqk[:, i, :], xb[:, :], start=True, stop=True).then_inc(R["mm"], 1)
                    for e in range(products):
                        copied = steps // 2 - 8 // 2
                        if e < 8:
                            pe.wait_ge(R["odd" if e % 2 else "even"], copied + e // 2 + 1)
                        else:
                            pe.wait_ge(R["even"], steps // 2 + e - 7)
                            pe.wait_ge(R["odd"], steps // 2 + e - 7)
                        pe.matmul(k.bank[:, e % 8, :], xb[:, P * (e // 2):P * (e // 2) + P], wv[:, e % 2, :], start=True, stop=True).then_inc(R["mm"], 1)

                @block.scalar
                def _(act):
                    act.copy(xb[:, :], k.xn[:, bass.ds(c * TILE, TILE)]).then_inc(R["xb"], 1)
                    for i in range(0, steps, 2):
                        act.wait_ge(R["mm"], i + 1)
                        act.copy(dest(i), k.bank[:, i % 8, :]).then_inc(R["even"], 1)
                    for e in range(products):
                        act.wait_ge(R["mm"], steps + e + 1)
                        act.copy(half(e, 0), k.bank[0:64, e % 8, :]).then_inc(R["even"], 1)

                @block.vector
                def _(dve):
                    for i in range(1, steps, 2):
                        dve.wait_ge(R["mm"], i + 1)
                        dve.tensor_copy(dest(i), k.bank[:, i % 8, :]).then_inc(R["odd"], 1)
                    for e in range(products):
                        dve.wait_ge(R["mm"], steps + e + 1)
                        dve.tensor_copy(half(e, 1), k.bank[64:P, e % 8, :]).then_inc(R["odd"], 1)

            def store(dve, psum):
                return dve.tensor_scalar(k.s[:, bass.ds(c * TILE, TILE)], psum, bo[:, 0:1], None, ALU.add)

            local_attention(k, m, DH ** -0.5, wo, store)
            clear(nc, list(m.S.values()) + list(R.values()))


def mixture(k, w):
    nc = k.nc
    MT = N // P
    QT = TILE // P
    EW = 2 * EH + 2 * D + 4
    with ExitStack() as ctx:
        y = k.sb(ctx, "moe_y", [P, MT, D])
        gates = k.sb(ctx, "moe_gates", [P, EXPERTS, MT])
        a = k.sb(ctx, "moe_silu", [P, 2, TILE])
        ws = k.sb(ctx, "moe_ws", [P, 2, SH])
        ws2 = k.sb(ctx, "moe_ws2", [P, SH // P, D])
        bs = k.sb(ctx, "moe_bs", [P, 9])
        S = {n: k.sem(k.ctx, "moe_" + n) for n in (
            "loaded", "logits", "dve", "gap", "expgap", "gates", "turned", "gt", "by", "y0",
            "shared_gate", "shared_up", "shared_silu", "shared_h", "z", "g")}
        with ExitStack() as gctx:
            wg = k.sb(gctx, "moe_wg", [P, EXPERTS])
            b2 = k.sb(gctx, "moe_b2", [EXPERTS, D])
            rank = k.sb(gctx, "moe_rank", [P, EXPERTS])
            lg, eq, key, one1, one2 = (k.sb(gctx, "moe_" + n, [P, MT, EXPERTS]) for n in ("lg", "eq", "key", "one1", "one2"))
            m1, m2, km, gap, ex, g1, g2 = (k.sb(gctx, "moe_" + n, [P, MT]) for n in ("m1", "m2", "km", "gap_", "ex", "g1", "g2"))
            gt = k.sb(gctx, "moe_gt", [EXPERTS, N])
            with nc.Block() as block:
                @block.sync
                def _(sp):
                    for dst, src in ((wg[:, :], w["wg"]), (b2[:, :], w["b2"]), (rank[:, :], w["rank"]), (ws[:, :, :], w["ws"]),
                                     (ws2[:, :, :], w["ws2"]), (bs[:, :], w["bs"])):
                        sp.dma_start(dst, src).then_inc(S["loaded"], 16)

                @block.tensor
                def _(pe):
                    pe.wait_ge(S["loaded"], 96)
                    for i in range(MT):
                        ins = pe.matmul(k.bank[:, 0, EXPERTS * i:EXPERTS * i + EXPERTS], k.xn[:, P * i:P * i + P], wg[:, :], start=True, stop=True)
                    ins.then_inc(S["logits"], 1)
                    pe.wait_ge(S["gates"], 1)
                    for i in range(MT):
                        ins = pe.transpose(k.bank[0:EXPERTS, 1 + i // QT, P * (i % QT):P * (i % QT) + P], gates[:, :, i], k.ident[:, :])
                    ins.then_inc(S["turned"], 1)
                    pe.wait_ge(S["gt"], 1)
                    for i in range(MT):
                        ins = pe.matmul(k.bank[:, 1 + i // QT, P * (i % QT):P * (i % QT) + P], gt[:, P * i:P * i + P], b2[:, :], start=True, stop=True)
                    ins.then_inc(S["by"], 1)

                @block.scalar
                def _(act):
                    act.wait_ge(S["gap"], 1)
                    act.activation(ex[:, :], gap[:, :], ACT.Exp).then_inc(S["expgap"], 1)
                    act.wait_ge(S["turned"], 1)
                    act.copy(gt[:, :], k.bank[0:EXPERTS, 1:5, :].rearrange("p a b -> p (a b)")).then_inc(S["gt"], 1)
                    act.wait_ge(S["by"], 1)
                    act.copy(y[:, :, :].rearrange("p a b -> p (a b)"), k.bank[:, 1:5, :].rearrange("p a b -> p (a b)")).then_inc(S["y0"], 1)

                @block.vector
                def _(dve):
                    own = Steps(dve, S["dve"])

                    def wide(ap):
                        return ap.unsqueeze(2).to_broadcast([P, MT, EXPERTS])

                    def first_best(top, one):
                        own.link(dve.tensor_reduce(top, lg[:, :, :], AX.X, ALU.max))
                        own.link(dve.tensor_tensor(eq[:, :, :], lg[:, :, :], wide(top), ALU.is_equal))
                        own.link(dve.tensor_tensor(key[:, :, :], eq[:, :, :], rank[:, :].unsqueeze(1).to_broadcast([P, MT, EXPERTS]), ALU.mult))
                        own.link(dve.tensor_reduce(km[:, :], key[:, :, :], AX.X, ALU.max))
                        own.link(dve.tensor_tensor(one, key[:, :, :], wide(km[:, :]), ALU.is_equal))

                    dve.wait_ge(S["logits"], 1)
                    own.link(dve.tensor_copy(lg[:, :, :].rearrange("p a b -> p (a b)"), k.bank[:, 0, 0:MT * EXPERTS]))
                    first_best(m1[:, :], one1[:, :, :])
                    own.link(dve.scalar_tensor_tensor(lg[:, :, :], one1[:, :, :], -1e30, lg[:, :, :], op0=ALU.mult, op1=ALU.add))
                    first_best(m2[:, :], one2[:, :, :])
                    dve.tensor_tensor(gap[:, :], m2[:, :], m1[:, :], ALU.subtract).then_inc(S["gap"], 1)
                    dve.wait_ge(S["expgap"], 1)
                    own.link(dve.tensor_scalar(g1[:, :], ex[:, :], 1.0, None, ALU.add))
                    own.link(dve.reciprocal(g1[:, :], g1[:, :]))
                    own.link(dve.tensor_tensor(g2[:, :], ex[:, :], g1[:, :], ALU.mult))
                    own.did(dve.tensor_tensor(one1[:, :, :], one1[:, :, :], wide(g1[:, :]), ALU.mult))
                    own.link(dve.tensor_tensor(one2[:, :, :], one2[:, :, :], wide(g2[:, :]), ALU.mult))
                    dve.tensor_tensor(gates[:, :, :].rearrange("p e i -> p i e"), one1[:, :, :], one2[:, :, :], ALU.add).then_inc(S["gates"], 1)

        ew = k.sb(ctx, "moe_ew", [P, 2, EW])
        h = k.sb(ctx, "moe_h", [P, 2, 2, TILE])
        gcol = k.sb(ctx, "moe_gcol", [P, 2, MT])
        R = {n: k.sem(k.ctx, "moe_e_" + n) for n in ("w0", "w1", "gcol", "gate", "up", "silu", "h", "mm", "y")}
        with nc.Block() as block:
            @block.sync
            def _(sp):
                sp.dma_start(ew[:, 0, :], w["experts"][0]).then_inc(S["loaded"], 16)
                sp.dma_start(ew[:, 1, :], w["experts"][1]).then_inc(S["loaded"], 16)
                sp.wait_ge(S["loaded"], 128)
        with nc.Fori(0, EXPERTS // 2) as turn:
            with nc.Block() as block:
                steps = 2 * NT

                @block.sync
                def _(sp):
                    for slot in range(2):
                        sp.wait_ge(R["mm"], NT * (slot + 1))
                        sp.dma_start(ew[:, slot, :], w["experts"][bass.ds(turn * 2 + (2 + slot), 1)].rearrange("a p n -> p (a n)")).then_inc(R["w0"], 16)
                    sp.wait_ge(R["w0"], 32)

                @block.tensor
                def _(pe):
                    def first(u):
                        slot, t = u // NT, u % NT
                        for o in range(2):
                            i = 2 * u + o
                            if i >= 2:
                                pe.wait_ge(R["silu"], i - 1)
                            pe.matmul(k.bank[:, i % 2, :], ew[:, slot, P * o:P * o + P], k.xn[:, tok(t)], start=True, stop=True).then_inc(R["gate"], 1)
                            if i >= 2:
                                pe.wait_ge(R["h"], i - 1)
                            pe.matmul(k.bank[:, 2 + i % 2, :], ew[:, slot, EH + P * o:EH + P * o + P], k.xn[:, tok(t)], start=True, stop=True).then_inc(R["up"], 1)

                    first(0)
                    for u in range(steps):
                        if u + 1 < steps:
                            first(u + 1)
                        slot = u // NT
                        pe.wait_ge(R["h"], 2 * u + 2)
                        if u >= 2:
                            pe.wait_ge(R["y"], u - 1)
                        for q in range(QT):
                            for o in range(2):
                                ins = pe.matmul(k.bank[:, 4 + u % 2, P * q:P * q + P], h[:, u % 2, o, P * q:P * q + P],
                                                ew[:, slot, 2 * EH + D * o:2 * EH + D * o + D], start=o == 0, stop=o == 1)
                        ins.then_inc(R["mm"], 1)

                @block.scalar
                def _(act):
                    for i in range(2 * steps):
                        slot = i // (2 * NT)
                        act.wait_ge(R["gate"], i + 1)
                        if i >= 2:
                            act.wait_ge(R["h"], i - 1)
                        bias = 2 * EH + 2 * D + i % 2
                        act.activation(a[:, i % 2, :], k.bank[:, i % 2, :], ACT.Silu, bias=ew[:, slot, bias:bias + 1]).then_inc(R["silu"], 1)

                @block.vector
                def _(dve):
                    dve.tensor_copy(gcol[:, :, :], gates[:, bass.ds(turn * 2, 2), :]).then_inc(R["gcol"], 1)
                    dve.wait_ge(R["gcol"], 1)

                    def add(u):
                        slot, t = u // NT, u % NT
                        dve.wait_ge(R["mm"], u + 1)
                        for q in range(QT):
                            i = QT * t + q
                            ins = dve.scalar_tensor_tensor(y[:, i, :], k.bank[:, 4 + u % 2, P * q:P * q + P], gcol[:, slot, i:i + 1], y[:, i, :],
                                                           op0=ALU.mult, op1=ALU.add)
                        ins.then_inc(R["y"], 1)

                    for u in range(steps):
                        slot = u // NT
                        if u >= 2:
                            dve.wait_ge(R["mm"], u - 1)
                        for o in range(2):
                            i = 2 * u + o
                            dve.wait_ge(R["silu"], i + 1)
                            dve.wait_ge(R["up"], i + 1)
                            bias = 2 * EH + 2 * D + 2 + o
                            dve.scalar_tensor_tensor(h[:, u % 2, o, :], k.bank[:, 2 + i % 2, :], ew[:, slot, bias:bias + 1], a[:, i % 2, :],
                                                     op0=ALU.add, op1=ALU.mult).then_inc(R["h"], 1)
                        if u:
                            if u >= NT + 1:
                                dve.wait_ge(R["y"], u - NT)
                            add(u - 1)
                    add(steps - 1)
            clear(nc, R.values())

        hs = k.sb(ctx, "moe_hs", [P, 2, SH // P, TILE])
        with nc.Block() as block:
            H = SH // P

            @block.tensor
            def _(pe):
                def first(t):
                    for o in range(H):
                        i = H * t + o
                        if i >= 2:
                            pe.wait_ge(S["shared_silu"], i - 1)
                        pe.matmul(k.bank[:, i % 2, :], ws[:, 0, P * o:P * o + P], k.xn[:, tok(t)], start=True, stop=True).then_inc(S["shared_gate"], 1)
                        if i >= 2:
                            pe.wait_ge(S["shared_h"], i - 1)
                        pe.matmul(k.bank[:, 2 + i % 2, :], ws[:, 1, P * o:P * o + P], k.xn[:, tok(t)], start=True, stop=True).then_inc(S["shared_up"], 1)

                first(0)
                for t in range(NT):
                    if t + 1 < NT:
                        first(t + 1)
                    pe.wait_ge(S["shared_h"], H * (t + 1))
                    if t >= 2:
                        pe.wait_ge(S["g"], t - 1)
                    for o in range(H):
                        pe.matmul(k.bank[:, 4 + t % 2, :], ws2[:, o, :], hs[:, t % 2, o, :], start=o == 0, stop=False)
                    for q in range(QT):
                        ins = pe.matmul(k.bank[:, 4 + t % 2, P * q:P * q + P], y[:, QT * t + q, :], k.ident[:, :], start=False, stop=q == QT - 1)
                    ins.then_inc(S["z"], 1)

            @block.scalar
            def _(act):
                for t in range(NT):
                    for o in range(H):
                        i = H * t + o
                        act.wait_ge(S["shared_gate"], i + 1)
                        if i >= 2:
                            act.wait_ge(S["shared_h"], i - 1)
                        act.activation(a[:, i % 2, :], k.bank[:, i % 2, :], ACT.Silu, bias=bs[:, o:o + 1]).then_inc(S["shared_silu"], 1)
                    if t:
                        act.wait_ge(S["z"], t)
                        act.activation(k.g[:, tok(t - 1)], k.bank[:, 4 + (t - 1) % 2, :], ACT.Silu, bias=bs[:, 8:9]).then_inc(S["g"], 1)
                act.wait_ge(S["z"], NT)
                act.activation(k.g[:, tok(NT - 1)], k.bank[:, 4 + (NT - 1) % 2, :], ACT.Silu, bias=bs[:, 8:9]).then_inc(S["g"], 1)

            @block.vector
            def _(dve):
                for t in range(NT):
                    if t >= 2:
                        dve.wait_ge(S["z"], t - 1)
                    for o in range(H):
                        i = H * t + o
                        dve.wait_ge(S["shared_silu"], i + 1)
                        dve.wait_ge(S["shared_up"], i + 1)
                        dve.scalar_tensor_tensor(hs[:, t % 2, o, :], k.bank[:, 2 + i % 2, :], bs[:, 4 + o:5 + o], a[:, i % 2, :],
                                                 op0=ALU.add, op1=ALU.mult).then_inc(S["shared_h"], 1)


class Full:

    def __init__(self, k, ctx, name, heads, dh):
        self.heads, self.dh = heads, dh
        self.q = k.sb(ctx, name + "_q", [P, heads, T])
        self.k = k.sb(ctx, name + "_k", [P, T])
        self.v = k.sb(ctx, name + "_v", [P, T // P, heads * dh])
        self.vp = k.sb(ctx, name + "_vp", [P, T // P, heads, 3, dh], BF16)
        self.p = k.sb(ctx, name + "_p", [P, 2, T])
        self.pt = k.sb(ctx, name + "_pt", [P, 3, 2, T // P, P], BF16)
        self.top = k.sb(ctx, name + "_top", [P, 4])
        self.sum = k.sb(ctx, name + "_sum", [P, 4])
        self.raw = k.sb(ctx, name + "_raw", [P, 4, dh])
        self.S = {n: k.sem(k.ctx, f"{name}_{n}") for n in (
            "scores", "top", "exp", "turned_a", "turned_b", "high", "low", "pv", "recip", "read", "o", "vsplit")}


def full_attention(k, m, place, load, after=None):
    nc, S = k.nc, m.S
    KT = T // P
    units = [(qi, h) for qi in range(KT) for h in range(m.heads)]
    U = len(units)
    with nc.Block() as block:
        @block.tensor
        def _(pe):
            def scores(u):
                qi, h = units[u]
                if u >= 2:
                    pe.wait_ge(S["exp"], u - 1)
                for c in range(T // TILE):
                    ins = pe.matmul(k.bank[:, 2 * (u % 2) + c, :], m.q[:, h, P * qi:P * qi + P], m.k[:, tok(c)], start=True, stop=True)
                ins.then_inc(S["scores"], 1)

            def turn(u):
                pe.wait_ge(S["exp"], u + 1)
                for half in range(2):
                    if u >= 1:
                        pe.wait_ge(S["low"], 2 * (u - 1) + half + 1)
                    for c in range(4):
                        at = P * (4 * half + c)
                        ins = pe.transpose(k.bank[:, 4 + half, P * c:P * c + P], m.p[:, u % 2, at:at + P], k.ident[:, :])
                    ins.then_inc(S[("turned_a", "turned_b")[half]], 1)

            def weigh(u):
                qi, h = units[u]
                pe.wait_ge(S["high"], 2 * u + 2)
                if u >= 2:
                    pe.wait_ge(S["read"], u - 1)
                for c in range(KT):
                    pe.matmul(k.bank[:, 6 + u % 2, 0:3 * m.dh], m.pt[:, u % 3, 0, c, :], m.vp[:, c, h, :, :].rearrange("p a b -> p (a b)"), start=c == 0, stop=False)
                pe.wait_ge(S["low"], 2 * u + 2)
                for c in range(KT):
                    ins = pe.matmul(k.bank[:, 6 + u % 2, 0:2 * m.dh], m.pt[:, u % 3, 1, c, :], m.vp[:, c, h, 0:2, :].rearrange("p a b -> p (a b)"), start=False, stop=c == KT - 1)
                ins.then_inc(S["pv"], 1)

            scores(0)
            scores(1)
            for u in range(U):
                turn(u)
                if u:
                    weigh(u - 1)
                if u + 2 < U:
                    scores(u + 2)
            weigh(U - 1)
            if after:
                pe.wait_ge(S["o"], U)
                after[0](pe)

        @block.sync
        def _(sp):
            load(sp)

        @block.vector
        def _(dve):
            def low_part(u):
                for half in range(2):
                    dve.wait_ge(S["high"], 2 * u + half + 1)
                    if u >= 3:
                        dve.wait_ge(S["pv"], u - 2)
                    high, low = (m.pt[:, u % 3, n, 4 * half:4 * half + 4, :].rearrange("p a b -> p (a b)") for n in range(2))
                    dve.tensor_tensor(low, k.bank[:, 4 + half, :], high, ALU.subtract).then_inc(S["low"], 1)

            def finish(u):
                dve.wait_ge(S["exp"], u + 1)
                dve.reciprocal(m.sum[:, u % 4:u % 4 + 1], m.sum[:, u % 4:u % 4 + 1]).then_inc(S["recip"], 1)
                dve.wait_ge(S["pv"], u + 1)
                if u >= 4:
                    dve.wait_ge(S["o"], u - 3)
                dve.tensor_reduce(m.raw[:, u % 4, :], k.bank[:, 6 + u % 2, 0:3 * m.dh].rearrange("p (a b) -> p b a", a=3), AX.X, ALU.add).then_inc(S["read"], 1)

            for u in range(U):
                dve.wait_ge(S["scores"], u + 1)
                if u >= 4:
                    dve.wait_ge(S["exp"], u - 3)
                raw = k.bank[:, 2 * (u % 2):2 * (u % 2) + 2, :].rearrange("p a b -> p (a b)")
                dve.tensor_reduce(m.top[:, u % 4:u % 4 + 1], raw, AX.X, ALU.max, negate=True).then_inc(S["top"], 1)
                if u:
                    low_part(u - 1)
                if u >= 2:
                    finish(u - 2)
            low_part(U - 1)
            finish(U - 2)
            finish(U - 1)

        @block.scalar
        def _(act):
            def high_part(u):
                for half in range(2):
                    act.wait_ge(S[("turned_a", "turned_b")[half]], u + 1)
                    if u >= 3:
                        act.wait_ge(S["pv"], u - 2)
                    act.copy(m.pt[:, u % 3, 0, 4 * half:4 * half + 4, :].rearrange("p a b -> p (a b)"), k.bank[:, 4 + half, :]).then_inc(S["high"], 1)

            def divide(u):
                act.wait_ge(S["recip"], u + 1)
                act.wait_ge(S["read"], u + 1)
                act.activation(place(*units[u]), m.raw[:, u % 4, :], ACT.Copy, scale=m.sum[:, u % 4:u % 4 + 1]).then_inc(S["o"], 1)

            for u in range(U):
                if u:
                    high_part(u - 1)
                act.wait_ge(S["top"], u + 1)
                if u >= 2:
                    act.wait_ge(S["turned_b"], u - 1)
                if u >= 4:
                    act.wait_ge(S["o"], u - 3)
                raw = k.bank[:, 2 * (u % 2):2 * (u % 2) + 2, :].rearrange("p a b -> p (a b)")
                act.activation(m.p[:, u % 2, :], raw, ACT.Exp, bias=m.top[:, u % 4:u % 4 + 1],
                               accum_out=m.sum[:, u % 4:u % 4 + 1]).then_inc(S["exp"], 1)
                if u >= 3:
                    divide(u - 3)
            high_part(U - 1)
            for u in range(U - 3, U):
                divide(u)
            if after:
                after[1](act)


def split_values(dve, own, m, v):
    whole = v.rearrange("p a (h d) -> p a h d", h=m.heads)
    rest = m.v[:, :, :].rearrange("p a (h d) -> p a h d", h=m.heads)
    own.link(dve.tensor_copy(m.vp[:, :, :, 0, :], whole))
    own.link(dve.tensor_tensor(rest, whole, m.vp[:, :, :, 0, :], ALU.subtract))
    own.link(dve.tensor_copy(m.vp[:, :, :, 1, :], rest))
    own.link(dve.tensor_tensor(rest, rest, m.vp[:, :, :, 1, :], ALU.subtract))
    own.did(dve.tensor_copy(m.vp[:, :, :, 2, :], rest))


def wide_attention(k, w):
    nc = k.nc
    KT = T // P
    with ExitStack() as ctx:
        ot = k.sb(ctx, "l2a_ot", [P, PAIRS, N])
        S = {n: k.sem(k.ctx, "l2a_" + n) for n in ("head", "loaded", "xb", "q", "k", "v", "qc", "kc", "vc", "turned", "ot", "post", "gelu", "mm", "s")}
        with ExitStack() as actx:
            m = Full(k, actx, "l2a", 2, DH)
            xb = k.sb(actx, "l2a_xb", [P, T])
            wt = k.sb(actx, "l2a_w", [P, 3, P])
            head = k.sb(actx, "l2a_head", [P, 2])
            o = k.sb(actx, "l2a_o", [P, KT, P])

            def load(sp, pair, done):
                return sp.dma_start(wt[:, :, :].rearrange("p a b -> p (a b)"), w["qkv"][pair].rearrange("a p n -> p (a n)")).then_inc(done, 16)

            with nc.Block() as block:
                @block.sync
                def _(sp):
                    sp.dma_start(head[:, :], w["head"]).then_inc(S["head"], 16)
                    load(sp, slice(0, 1), S["head"])
                    sp.wait_ge(S["head"], 32)
            with nc.Fori(0, B) as b:
                with nc.Block() as block:
                    @block.vector
                    def _(dve):
                        dve.tensor_copy(xb[:, :], k.xn[:, bass.ds(b * T, T)]).then_inc(S["xb"], 1)
                        dve.wait_ge(S["xb"], 1)
                with nc.Fori(0, PAIRS) as pair:
                    with nc.Block() as block:
                        @block.tensor
                        def _(pe):
                            for i in range(KT):
                                ins = pe.matmul(k.bank[:, 4 + i // 4, P * (i % 4):P * (i % 4) + P], xb[:, P * i:P * i + P], wt[:, 2, :], start=True, stop=True)
                            ins.then_inc(S["v"], 1)
                            for c in range(BT):
                                ins = pe.matmul(k.bank[:, c, :], wt[:, 0, :], xb[:, tok(c)], start=True, stop=True)
                            ins.then_inc(S["q"], 1)
                            for c in range(BT):
                                ins = pe.matmul(k.bank[:, 2 + c, :], wt[:, 1, :], xb[:, tok(c)], start=True, stop=True)
                            ins.then_inc(S["k"], 1)

                        @block.scalar
                        def _(act):
                            act.wait_ge(S["q"], 1)
                            for h in range(2):
                                act.activation(m.q[:, h, :], k.bank[:, 0:2, :].rearrange("p a b -> p (a b)"), ACT.Copy, scale=head[:, h:h + 1]).then_inc(S["qc"], 1)
                            act.wait_ge(S["k"], 1)
                            act.copy(m.k[:, :], k.bank[:, 2:4, :].rearrange("p a b -> p (a b)")).then_inc(S["kc"], 1)

                        @block.vector
                        def _(dve):
                            dve.wait_ge(S["v"], 1)
                            split_values(dve, Steps(dve, m.S["vsplit"]), m, k.bank[:, 4:6, :].rearrange("p a (b c) -> p (a b) c", c=P))

                    def next_weights(sp):
                        load(sp, bass.ds(pair + 1, 1), S["loaded"])
                        sp.wait_ge(S["loaded"], 16)

                    def turn_outputs(pe):
                        for i in range(KT):
                            ins = pe.transpose(k.bank[:, i // 4, P * (i % 4):P * (i % 4) + P], o[:, i, :], k.ident[:, :])
                        ins.then_inc(S["turned"], 1)

                    def keep_outputs(act):
                        act.wait_ge(S["turned"], 1)
                        flat = ot[:, :, :].rearrange("p a b -> p (a b)")
                        act.copy(flat[:, bass.ds(pair * N + b * T, T)], k.bank[:, 0:2, :].rearrange("p a b -> p (a b)")).then_inc(S["ot"], 1)

                    full_attention(k, m, lambda qi, h: o[:, qi, DH * h:DH * h + DH], next_weights, (turn_outputs, keep_outputs))
                    clear(nc, [S[n] for n in ("loaded", "q", "k", "v", "qc", "kc", "vc", "turned", "ot")] + list(m.S.values()))
                clear(nc, [S["xb"]])
        wp = k.sb(ctx, "l2a_wp", [P, PAIRS, D])
        with nc.Block() as block:
            @block.sync
            def _(sp):
                sp.dma_start(wp[:, :, :], w["post"]).then_inc(S["post"], 16)

            @block.scalar
            def _(act):
                for t in range(NT):
                    for pair in range(PAIRS):
                        act.activation(ot[:, pair, tok(t)], ot[:, pair, tok(t)], ACT.Gelu).then_inc(S["gelu"], 1)

            @block.tensor
            def _(pe):
                pe.wait_ge(S["post"], 16)
                for t in range(NT):
                    for pair in range(PAIRS):
                        pe.wait_ge(S["gelu"], PAIRS * t + pair + 1)
                        ins = pe.matmul(k.bank[:, t, :], wp[:, pair, :], ot[:, pair, tok(t)], start=pair == 0, stop=pair == PAIRS - 1)
                    ins.then_inc(S["mm"], 1)

            @block.vector
            def _(dve):
                for t in range(NT):
                    dve.wait_ge(S["mm"], t + 1)
                    dve.tensor_tensor(k.s[:, tok(t)], k.xn[:, tok(t)], k.bank[:, t, :], ALU.add).then_inc(S["s"], 1)


def rope_attention(k, w):
    nc = k.nc
    KT = T // P
    G, GH, HD = 4, 4, D // HEADS
    GW = 4 * P + GH * HD + 4 + GH * HD
    with ExitStack() as ctx:
        S = {n: k.sem(k.ctx, "l3a_" + n) for n in (
            "fixed", "loaded", "xb", "qz", "qk", "cos", "sin", "sum", "v", "vc", "turned", "ot", "mm", "s")}
        lx = k.sb(ctx, "l3a_lx", [P, N])
        col = k.sb(ctx, "l3a_cols", [P, 3])
        wo = k.sb(ctx, "l3a_wo", [P, D])
        rope = k.sb(ctx, "l3a_rope", [P, 4, T])
        m = Full(k, ctx, "l3a", GH, HD)
        xb = k.sb(ctx, "l3a_xb", [P, T])
        wt = k.sb(ctx, "l3a_w", [P, GW])
        q = k.sb(ctx, "l3a_qall", [P, T])
        head = k.sb(ctx, "l3a_head", [P, GH])
        part = k.sb(ctx, "l3a_part", [P, 2, 2, TILE])
        o = k.sb(ctx, "l3a_oall", [P, KT, D])
        ot = k.sb(ctx, "l3a_ot", [P, T])

        def load(sp, g, done):
            return sp.dma_start(wt[:, :], w["qkv"][g].rearrange("a p n -> p (a n)")).then_inc(done, 16)

        with nc.Block() as block:
            @block.sync
            def _(sp):
                for dst, src in ((col[:, :], w["cols"]), (wo[:, :], w["out"]), (rope[:, :, :], w["rope"]), (head[:, :], w["head"])):
                    sp.dma_start(dst, src).then_inc(S["fixed"], 16)
                load(sp, slice(0, 1), S["fixed"])
                sp.wait_ge(S["fixed"], 80)
        layer_norm(k, "l3a_ln", k.xn, lx, gamma=col[:, 0:1], beta=col[:, 1:2])
        with nc.Fori(0, B) as b:
            with nc.Block() as block:
                @block.vector
                def _(dve):
                    dve.tensor_copy(xb[:, :], lx[:, bass.ds(b * T, T)]).then_inc(S["xb"], 1)
                    dve.wait_ge(S["xb"], 1)
            with nc.Fori(0, G) as g:
                with nc.Block() as block:
                    @block.tensor
                    def _(pe):
                        for i in range(2 * BT):
                            if i >= 3:
                                pe.wait_ge(S["sin"], i - 2)
                            for j in range(2):
                                ins = pe.matmul(k.bank[:, 2 * (i % 3) + j, :], wt[:, P * (2 * (i // BT) + j):P * (2 * (i // BT) + j) + P], xb[:, tok(i % BT)], start=True, stop=True)
                            ins.then_inc(S["qk"], 1)
                        for i in range(KT):
                            ins = pe.matmul(k.bank[:, 6, GH * HD * i:GH * HD * i + GH * HD], xb[:, P * i:P * i + P], wt[:, 4 * P:4 * P + GH * HD], start=True, stop=True)
                        ins.then_inc(S["v"], 1)

                    @block.vector
                    def _(dve):
                        bias = 4 * P + GH * HD
                        for i in range(2 * BT):
                            dve.wait_ge(S["qk"], i + 1)
                            if i >= 2:
                                dve.wait_ge(S["sum"], i - 1)
                            for j, sem in enumerate(("cos", "sin")):
                                at = bias + 2 * (i // BT) + j
                                dve.scalar_tensor_tensor(part[:, i % 2, j, :], k.bank[:, 2 * (i % 3) + j, :], wt[:, at:at + 1],
                                                         rope[:, 2 * (i // BT) + j, tok(i % BT)], op0=ALU.add, op1=ALU.mult).then_inc(S[sem], 1)
                        dve.wait_ge(S["v"], 1)
                        dve.tensor_tensor(m.v[:, :, :], k.bank[:, 6, 0:GH * HD * KT].rearrange("p (a b) -> p a b", a=KT),
                                          wt[:, bias + 4:bias + 4 + GH * HD].unsqueeze(1).to_broadcast([P, KT, GH * HD]), ALU.add).then_inc(S["vc"], 1)
                        dve.wait_ge(S["vc"], 1)
                        split_values(dve, Steps(dve, m.S["vsplit"]), m, m.v[:, :, :])

                    @block.gpsimd
                    def _(pool):
                        for i in range(2 * BT):
                            pool.wait_ge(S["cos"], i + 1)
                            pool.wait_ge(S["sin"], i + 1)
                            pool.tensor_tensor((q, m.k)[i // BT][:, tok(i % BT)], part[:, i % 2, 0, :], part[:, i % 2, 1, :], ALU.add).then_inc(S["sum"], 1)

                    @block.scalar
                    def _(act):
                        for c in range(BT):
                            act.wait_ge(S["sum"], c + 1)
                            for h in range(GH):
                                act.activation(m.q[:, h, tok(c)], q[:, tok(c)], ACT.Copy, scale=head[:, h:h + 1]).then_inc(S["qz"], 1)

                def next_weights(sp):
                    load(sp, bass.ds(g + 1, 1), S["loaded"])
                    sp.wait_ge(S["loaded"], 16)

                full_attention(k, m, lambda qi, h: o[:, qi, bass.ds(g * (GH * HD) + HD * h, HD)], next_weights)
                clear(nc, [S[n] for n in ("loaded", "qz", "qk", "cos", "sin", "sum", "v", "vc")] + list(m.S.values()))
            with nc.Block() as block:
                @block.tensor
                def _(pe):
                    for i in range(KT):
                        ins = pe.transpose(k.bank[:, i // 4, P * (i % 4):P * (i % 4) + P], o[:, i, :], k.ident[:, :])
                    ins.then_inc(S["turned"], 1)
                    pe.wait_ge(S["ot"], 1)
                    for c in range(BT):
                        ins = pe.matmul(k.bank[:, 2 + c, :], wo[:, :], ot[:, tok(c)], start=True, stop=True)
                    ins.then_inc(S["mm"], 1)

                @block.scalar
                def _(act):
                    act.wait_ge(S["turned"], 1)
                    act.copy(ot[:, :], k.bank[:, 0:2, :].rearrange("p a b -> p (a b)")).then_inc(S["ot"], 1)

                @block.vector
                def _(dve):
                    dve.wait_ge(S["mm"], 1)
                    dve.scalar_tensor_tensor(k.s[:, bass.ds(b * T, T)], k.bank[:, 2:4, :].rearrange("p a b -> p (a b)"), col[:, 2:3],
                                             k.xn[:, bass.ds(b * T, T)], op0=ALU.add, op1=ALU.add).then_inc(S["s"], 1)
            clear(nc, [S[n] for n in ("xb", "turned", "ot", "mm", "s")])


class Quantiser:

    def __init__(self, k, ctx, name, most):
        self.most, self.sl = most, []
        for i in range(2):
            self.sl.append({n: k.sb(ctx, f"{name}_{n}{i}", [P, most // (QB if n in ("top", "scale", "inv") else 1)])
                            for n in ("a", "sign", "t", "q", "top", "scale", "inv")})
        self.S = {n: k.sem(k.ctx, f"{name}_{n}") for n in ("own", "a", "signed", "q", "done")}

    def views(self, j, x):
        nb = x.shape[1] // QB
        b = self.sl[j % 2]

        def blocks(ap):
            return ap.rearrange("p (a b) -> p a b", b=QB)

        def wide(t):
            return t[:, 0:nb].unsqueeze(2).to_broadcast([P, nb, QB])

        return b, nb, blocks, wide

    def vector_scale(self, dve, own, j, x):
        b, nb, blocks, wide = self.views(j, x)
        F = x.shape[1]
        if j >= 2:
            dve.wait_ge(self.S["done"], j - 1)
        own.link(dve.tensor_reduce(b["top"][:, 0:nb], blocks(x), AX.X, ALU.max, apply_absolute_value=True))
        own.link(dve.tensor_scalar(b["scale"][:, 0:nb], b["top"][:, 0:nb], 1.0 / 6.0, 1e-12, ALU.mult, ALU.max))
        own.link(dve.reciprocal(b["inv"][:, 0:nb], b["scale"][:, 0:nb]))
        dve.tensor_tensor(blocks(b["a"][:, 0:F]), blocks(x), wide(b["inv"]), ALU.mult).then_inc(self.S["a"], 1)

    def scalar_sign(self, act, j, x):
        b, nb, blocks, wide = self.views(j, x)
        F = x.shape[1]
        act.wait_ge(self.S["a"], j + 1)
        act.activation(b["sign"][:, 0:F], b["a"][:, 0:F], ACT.Sign).then_inc(self.S["signed"], 1)
        act.activation(b["t"][:, 0:F], b["a"][:, 0:F], ACT.Abs).then_inc(self.S["signed"], 1)

    def vector_round(self, dve, own, j, x):
        b, nb, blocks, wide = self.views(j, x)
        F = x.shape[1]
        t, q, a, sign = (b[n][:, 0:F] for n in ("t", "q", "a", "sign"))
        dve.wait_ge(self.S["signed"], 2 * j + 2)
        own.did(dve.tensor_scalar(a, t, 1.75, None, ALU.is_gt))
        own.link(dve.tensor_scalar(q, t, 5.0, 2.0, ALU.is_gt, ALU.mult))
        own.link(dve.scalar_tensor_tensor(q, t, 3.5, q, op0=ALU.is_gt, op1=ALU.add))
        own.link(dve.scalar_tensor_tensor(q, t, 2.5, q, op0=ALU.is_gt, op1=ALU.add))
        own.link(dve.scalar_tensor_tensor(q, q, 2.0, a, op0=ALU.mult, op1=ALU.add))
        for mid in (1.25, 0.75, 0.25):
            own.link(dve.scalar_tensor_tensor(q, t, mid, q, op0=ALU.is_gt, op1=ALU.add))
        dve.scalar_tensor_tensor(q, q, 0.5, sign, op0=ALU.mult, op1=ALU.mult).then_inc(self.S["q"], 1)

    def pool_rescale(self, pool, j, x):
        b, nb, blocks, wide = self.views(j, x)
        pool.wait_ge(self.S["q"], j + 1)
        pool.tensor_tensor(blocks(x), blocks(b["q"][:, 0:x.shape[1]]), wide(b["scale"]), ALU.mult).then_inc(self.S["done"], 1)


def fp4_ffn(k, w):
    nc = k.nc
    MT = N // P
    HC = (FFI + P - 1) // P
    LAST = FFI - P * (HC - 1)
    WW = 2 * HC * P + FFI
    with ExitStack() as ctx:
        z = k.sb(ctx, "fp4_z", [P, WW + N])
        wt = k.sb(ctx, "fp4_wt", [P, 3, HC, P])
        xq = k.sb(ctx, "fp4_xq", [P, N])
        h = k.sb(ctx, "fp4_h", [P, MT, FFI])
        ht = k.sb(ctx, "fp4_ht", [P, HC, N])
        a = k.sb(ctx, "fp4_silu", [P, 2, FFI])
        qz = Quantiser(k, ctx, "fp4_q", 1056)
        S = {n: k.sem(k.ctx, "fp4_" + n) for n in ("loaded", "turned", "xt", "wturned", "wt", "xturned", "xq",
                                                   "gate", "up", "silu", "h", "hturned", "ht", "mm", "g")}
        slices = [slice(1056 * j, min(1056 * j + 1056, WW + N)) for j in range(-(-(WW + N) // 1056))]
        assert all((s.stop - s.start) % QB == 0 for s in slices)
        with nc.Block() as block:
            @block.sync
            def _(sp):
                sp.dma_start(z[:, 0:WW], w["w"]).then_inc(S["loaded"], 16)

            @block.tensor
            def _(pe):
                for i in range(MT):
                    pe.transpose(k.bank[:, i // 4, P * (i % 4):P * (i % 4) + P], k.xn[:, P * i:P * i + P], k.ident[:, :]).then_inc(S["turned"], 1)
                pe.wait_ge(qz.S["done"], len(slices))
                for n in range(3):
                    for c in range(HC):
                        at = P * (HC * n + c)
                        width = LAST if n == 2 and c == HC - 1 else P
                        ins = pe.transpose(k.bank[0:width, 4 + n, P * c:P * c + P], z[:, at:at + width], k.ident[:, :])
                    ins.then_inc(S["wturned"], 1)
                pe.wait_ge(S["xt"], 1)
                for i in range(MT):
                    pe.transpose(k.bank[:, i // 4, P * (i % 4):P * (i % 4) + P], z[:, WW + P * i:WW + P * i + P], k.ident[:, :]).then_inc(S["xturned"], 1)

            @block.scalar
            def _(act):
                act.wait_ge(S["turned"], MT)
                act.copy(z[:, WW:WW + N], k.bank[:, 0:4, :].rearrange("p a b -> p (a b)")).then_inc(S["xt"], 1)
                for j, s in enumerate(slices):
                    qz.scalar_sign(act, j, z[:, s])
                act.wait_ge(S["xturned"], MT)
                act.copy(xq[:, :], k.bank[:, 0:4, :].rearrange("p a b -> p (a b)")).then_inc(S["xq"], 1)

            @block.vector
            def _(dve):
                own = Steps(dve, qz.S["own"])
                dve.wait_ge(S["loaded"], 16)
                dve.wait_ge(S["xt"], 1)
                for j, s in enumerate(slices):
                    qz.vector_scale(dve, own, j, z[:, s])
                    if j:
                        qz.vector_round(dve, own, j - 1, z[:, slices[j - 1]])
                qz.vector_round(dve, own, len(slices) - 1, z[:, slices[-1]])
                dve.wait_ge(S["wturned"], 3)
                dve.tensor_copy(wt[:, 0:2, :, :].rearrange("p a b c -> p a (b c)"), k.bank[:, 4:6, 0:HC * P]).then_inc(S["wt"], 1)
                dve.tensor_copy(wt[:, 2, 0:HC - 1, :].rearrange("p a b -> p (a b)"), k.bank[:, 6, 0:(HC - 1) * P]).then_inc(S["wt"], 1)
                dve.tensor_copy(wt[0:LAST, 2, HC - 1, :], k.bank[0:LAST, 6, (HC - 1) * P:HC * P]).then_inc(S["wt"], 1)

            @block.gpsimd
            def _(pool):
                for j, s in enumerate(slices):
                    qz.pool_rescale(pool, j, z[:, s])

        clear(nc, qz.S.values())
        with nc.Block() as block:
            GROUP = 2
            hs = [h[:, GROUP * j:GROUP * j + GROUP, :].rearrange("p a b -> p (a b)") for j in range(MT // GROUP)]

            @block.tensor
            def _(pe):
                for i in range(MT):
                    if i >= 2:
                        pe.wait_ge(S["silu"], i - 1)
                    pe.matmul(k.bank[:, i % 2, 0:FFI], xq[:, P * i:P * i + P], wt[:, 0, :, :].rearrange("p a b -> p (a b)")[:, 0:FFI], start=True, stop=True).then_inc(S["gate"], 1)
                    if i >= 2:
                        pe.wait_ge(S["h"], i - 1)
                    pe.matmul(k.bank[:, 2 + i % 2, 0:FFI], xq[:, P * i:P * i + P], wt[:, 1, :, :].rearrange("p a b -> p (a b)")[:, 0:FFI], start=True, stop=True).then_inc(S["up"], 1)
                for i in range(MT):
                    pe.wait_ge(qz.S["done"], i // GROUP + 1)
                    if i >= 2:
                        pe.wait_ge(S["ht"], 2 * i - 2)
                    for c in range(HC):
                        width = min(P, FFI - P * c)
                        ins = pe.transpose(k.bank[0:width, 4 + i % 2, P * c:P * c + P], h[:, i, P * c:P * c + width], k.ident[:, :])
                    ins.then_inc(S["hturned"], 1)
                    if i % 4 == 3:
                        t = i // 4
                        pe.wait_ge(S["ht"], 2 * i + 2)
                        if t >= 2:
                            pe.wait_ge(S["g"], t - 1)
                        for c in range(HC):
                            width = min(P, FFI - P * c)
                            ins = pe.matmul(k.bank[:, 6 + t % 2, :], wt[0:width, 2, c, :], ht[0:width, c, tok(t)], start=c == 0, stop=c == HC - 1)
                        ins.then_inc(S["mm"], 1)

            @block.scalar
            def _(act):
                def finish(i):
                    act.wait_ge(S["hturned"], i + 1)
                    act.copy(ht[:, 0:HC - 1, P * i:P * i + P], k.bank[:, 4 + i % 2, 0:(HC - 1) * P].rearrange("p (a b) -> p a b", b=P)).then_inc(S["ht"], 1)
                    act.copy(ht[0:LAST, HC - 1, P * i:P * i + P], k.bank[0:LAST, 4 + i % 2, (HC - 1) * P:HC * P]).then_inc(S["ht"], 1)

                for i in range(MT):
                    act.wait_ge(S["gate"], i + 1)
                    if i >= 2:
                        act.wait_ge(S["h"], i - 1)
                    act.activation(a[:, i % 2, :], k.bank[:, i % 2, 0:FFI], ACT.Silu).then_inc(S["silu"], 1)
                for j in range(MT // GROUP):
                    qz.scalar_sign(act, j, hs[j])
                for i in range(MT):
                    finish(i)
                    if i % 4 == 3:
                        t = i // 4
                        act.wait_ge(S["mm"], t + 1)
                        act.activation(k.g[:, tok(t)], k.bank[:, 6 + t % 2, :], ACT.Silu).then_inc(S["g"], 1)

            @block.vector
            def _(dve):
                own = Steps(dve, qz.S["own"])
                for i in range(MT):
                    dve.wait_ge(S["silu"], i + 1)
                    dve.wait_ge(S["up"], i + 1)
                    dve.tensor_tensor(h[:, i, :], k.bank[:, 2 + i % 2, 0:FFI], a[:, i % 2, :], ALU.mult).then_inc(S["h"], 1)
                dve.wait_ge(S["h"], MT)
                for j in range(MT // GROUP):
                    qz.vector_scale(dve, own, j, hs[j])
                    if j:
                        qz.vector_round(dve, own, j - 1, hs[j - 1])
                qz.vector_round(dve, own, MT // GROUP - 1, hs[-1])

            @block.gpsimd
            def _(pool):
                for j in range(MT // GROUP):
                    qz.pool_rescale(pool, j, hs[j])


def window_layers(k, w):
    nc = k.nc
    HALO = 32
    CT = HALO + T
    TI = TILE // P
    NR = 2 * PAIRS
    with ExitStack() as ctx:
        x = k.xn
        sh = k.sb(ctx, "l3f_sh", [P, B, CT])
        raw = k.sb(ctx, "l3f_tables", [P, 4, T])
        mask = k.sb(ctx, "l3f_mask", [P, 2, 64])
        heads = k.sb(ctx, "l3f_heads", [P, PAIRS, NR])
        sel = k.sb(ctx, "l3f_sel", [P, PAIRS, P], BF16)
        S = {n: k.sem(k.ctx, "l3f_" + n) for n in (
            "fixed", "sel", "zeros", "wloaded", "shift", "xb", "raw", "rotated_0", "rotated_1", "rotated_2", "qk", "sq", "n2", "nt", "ntt", "parts", "inv", "iturned", "it", "spread",
            "cos", "sin", "sum", "kdone", "vmm", "vc", "vd", "nothing", "own", "g")}
        with nc.Block() as block:
            @block.sync
            def _(sp):
                for dst, src in ((raw[:, :, :], w["tables"]), (mask[:, :, :], w["mask"]), (heads[:, :, :], w["heads"])):
                    sp.dma_start(dst, src).then_inc(S["fixed"], 16)
                sp.wait_ge(S["fixed"], 48)

            @block.gpsimd
            def _(pool):
                pool.dma_start(sel[:, :, :], w["sel"]).then_inc(S["sel"], 16)
                pool.wait_ge(S["sel"], 16)

            @block.vector
            def _(dve):
                dve.memset(sh[:, :, :], 0.0).then_inc(S["zeros"], 1)
                dve.wait_ge(S["zeros"], 1)
        with nc.Fori(0, DEPTH) as layer:
            with nc.Block() as block:
                @block.scalar
                def _(act):
                    act.copy(sh[0:64, :, HALO:], x[0:64, :].rearrange("p (a b) -> p a b", a=B)).then_inc(S["shift"], 1)

                @block.vector
                def _(dve):
                    dve.tensor_copy(sh[64:P, :, HALO + 1:], x[64:P, :].rearrange("p (a b) -> p a b", a=B)[:, :, 0:T - 1]).then_inc(S["zeros"], 1)
                    dve.memset(sh[64:P, :, HALO:HALO + 1], 0.0).then_inc(S["zeros"], 1)
            with ExitStack() as actx:
                m = Local(k, actx, "l3f", WIN)
                wq = k.sb(actx, "l3f_wq", [P, NR, P])
                wv = k.sb(actx, "l3f_wv", [P, 2, PAIRS * DH])
                wo = k.sb(actx, "l3f_wo", [P, PAIRS, D])
                qs = k.sb(actx, "l3f_qs", [P, 4])
                table = k.sb(actx, "l3f_table", [P, 4, TILE])
                xb = k.sb(actx, "l3f_xb", [P, HALO + TILE])
                sq = k.sb(actx, "l3f_sq", [P, 2, TILE])
                spare = k.g[:, :].rearrange("p (a b c) -> p a b c", a=2, b=2)
                straight, part = spare[:, 0, :, :], spare[:, 1, :, :]
                rot = k.sb(actx, "l3f_rot", [P, 3, TILE])
                nt = k.sb(actx, "l3f_nt", [NR, TILE])
                kn = k.sb(actx, "l3f_knorm", [P, TI, NR])
                qn = k.sb(actx, "l3f_qnorm", [P, TI, NR])
                ik = k.sb(actx, "l3f_ik", [P, TILE], BF16)
                rest = k.sb(actx, "l3f_rest", [2 * PAIRS, TILE])
                with nc.Block() as block:
                    @block.sync
                    def _(sp):
                        for dst, src in ((wq[:, :, :].rearrange("p a b -> p (a b)"), w["wqk"]), (wv[:, :, :].rearrange("p a b -> p (a b)"), w["wv"]),
                                         (wo[:, :, :].rearrange("p a b -> p (a b)"), w["wo"]), (qs[:, :], w["qs"])):
                            sp.dma_start(dst, src[bass.ds(layer, 1)].rearrange("a p n -> p (a n)")).then_inc(S["wloaded"], 16)
                        sp.wait_ge(S["wloaded"], 64)

                with nc.Block() as block:
                    @block.vector
                    def _(dve):
                        dve.memset(ik[:, :], 0.0).then_inc(S["parts"], 1)
                clear(nc, [S["parts"]])
                with nc.Fori(0, B) as b:
                    with nc.Block() as block:
                        @block.gpsimd
                        def _(pool):
                            pool.memset(m.k[:, :, 0:HALO], 0.0).then_inc(S["nothing"], 1)
                    with nc.Fori(0, BT) as c:
                        FIRSTS = [i for i in range(m.nw) if i % 4 < 2]
                        PRODUCTS = 2 * len(FIRSTS)
                        EARLY = 9

                        def window_values(pe, e, psum):
                            i = FIRSTS[e // 2]
                            return pe.matmul(psum, xb[:, WIN * i:WIN * i + P], wv[:, e % 2, :], start=True, stop=True)

                        def value_halves(e):
                            r = slice(64 * (e % 2), 64 * (e % 2) + 64)
                            return [m.v[r, FIRSTS[e // 2] + 2 * half, :] for half in range(2)]

                        LAG = 2
                        K_NORMS, K_TURNED, K_SPREAD = PAIRS + 1, PAIRS + 2, PAIRS + 4
                        PER_STEP = PAIRS // (NR - K_SPREAD)

                        def wait_rotated(engine, i):
                            engine.wait_ge(S[f"rotated_{i % 3}"], 64 * (i // 3 + 1))

                        shifted = sh[:, :, :].rearrange("p a b -> p (a b)")

                        with nc.Block() as block:
                            def tile(i):
                                return (i + PAIRS) % NR

                            def dest(i):
                                return m.k[:, i, HALO:] if i < PAIRS else m.q[:, i - PAIRS, :]

                            @block.scalar
                            def _(act):
                                act.copy(xb[:, :], shifted[:, bass.ds(b * CT + c * TILE, HALO + TILE)]).then_inc(S["xb"], 1)
                                for i in range(NR):
                                    act.wait_ge(S["qk"], i + 1)
                                    if i >= 2:
                                        wait_rotated(act, i - 2)
                                    act.copy(straight[:, i % 2, :], k.bank[:, i % 4, :]).then_inc(S["raw"], 1)
                                    if i >= 2:
                                        act.wait_ge(S["n2"], i - 1)
                                    act.activation(sq[:, i % 2, :], k.bank[:, i % 4, :], ACT.Square).then_inc(S["sq"], 1)
                                    if i == PAIRS:
                                        act.wait_ge(S["n2"], PAIRS)
                                        act.activation(nt[:, :], k.bank[0:NR, 6, :], ACT.Sqrt).then_inc(S["nt"], 1)
                                    if i == K_TURNED:
                                        act.wait_ge(S["iturned"], 1)
                                        act.copy(ik[0:NR, :], k.bank[0:NR, 6, :]).then_inc(S["it"], 1)
                                    if i < EARLY:
                                        act.wait_ge(S["vmm"], i + 1)
                                        act.copy(value_halves(i)[0], k.bank[0:64, 4, :]).then_inc(S["vc"], 1)
                                act.wait_ge(S["n2"], NR)
                                act.wait_ge(S["ntt"], 1)
                                act.activation(nt[:, :], k.bank[0:NR, 5, :], ACT.Sqrt).then_inc(S["nt"], 1)

                            @block.tensor
                            def _(pe):
                                def norms(i):
                                    pe.wait_ge(S["sq"], i + 1)
                                    j = i % PAIRS
                                    pe.matmul(k.bank[0:NR, 6 - i // PAIRS, :], heads[:, j, :], sq[:, i % 2, :], start=j == 0, stop=j == PAIRS - 1).then_inc(S["n2"], 1)

                                def turn_norms(n, psum):
                                    pe.wait_ge(S["nt"], n)
                                    for j in range(TI):
                                        ins = pe.transpose(psum[:, NR * j:NR * j + NR], nt[:, P * j:P * j + P], k.ident[0:NR, 0:NR])
                                    ins.then_inc(S["ntt"], 1)

                                for i in range(NR):
                                    if i >= 4:
                                        pe.wait_ge(S["cos"], i - 3)
                                        pe.wait_ge(S["sq"], i - 3)
                                    pe.matmul(k.bank[:, i % 4, :], wq[:, tile(i), :], shifted[:, bass.ds(b * CT + c * TILE + HALO, TILE)], start=True, stop=True).then_inc(S["qk"], 1)
                                    if i == K_NORMS:
                                        turn_norms(1, k.bank[:, 7, :])
                                    if i == K_TURNED:
                                        pe.wait_ge(S["inv"], 1)
                                        for j in range(TI):
                                            ins = pe.transpose(k.bank[0:NR, 6, P * j:P * j + P], kn[:, j, :], k.ident[:, :])
                                        ins.then_inc(S["iturned"], 1)
                                    if i:
                                        norms(i - 1)
                                    for n in range(PER_STEP * (i - K_SPREAD), PER_STEP * (i + 1 - K_SPREAD)) if i >= K_SPREAD else ():
                                        if n == 0:
                                            pe.wait_ge(S["parts"], 1)
                                        if n >= 2:
                                            pe.wait_ge(S["kdone"], n - 1)
                                        pe.matmul(k.bank[:, 6 + n % 2, :], sel[:, n, :], ik[:, :], start=True, stop=True).then_inc(S["spread"], 1)
                                    if i == NR - 1:
                                        norms(i)
                                    if i < EARLY:
                                        if i == 0:
                                            pe.wait_ge(S["xb"], 1)
                                        if i:
                                            pe.wait_ge(S["vc"], i)
                                            pe.wait_ge(S["vd"], i)
                                        window_values(pe, i, k.bank[:, 4, :]).then_inc(S["vmm"], 1)
                                turn_norms(2, k.bank[:, 5, :])

                            @block.sync
                            def _(sp):
                                for i in range(NR):
                                    sp.wait_ge(S["raw"], i + 1)
                                    if i >= 3:
                                        sp.wait_ge(S["sin"], i - 2)
                                    for quarter in range(4):
                                        to, of = 32 * quarter, 32 * (quarter ^ 1)
                                        sp.dma_start(rot[to:to + 32, i % 3, :], straight[of:of + 32, i % 2, :]).then_inc(S[f"rotated_{i % 3}"], 16)

                            @block.gpsimd
                            def _(pool):
                                for i in range(NR):
                                    pool.wait_ge(S["cos"], i + 1)
                                    pool.wait_ge(S["sin"], i + 1)
                                    pool.tensor_tensor(dest(i), dest(i), part[:, i % 2, :], ALU.add).then_inc(S["sum"], 1)

                            @block.vector
                            def _(dve):
                                own = Steps(dve, S["own"])

                                def tables(ns):
                                    for n in ns:
                                        ins = dve.tensor_scalar(table[:, n, :], raw[:, n, bass.ds(c * TILE, TILE)], qs[:, n:n + 1], None, ALU.mult)
                                        own.link(ins)

                                def invert(n, to, psum):
                                    flat = to[:, :, :].rearrange("p a b -> p (a b)")
                                    dve.wait_ge(S["ntt"], n)
                                    own.link(dve.tensor_scalar(flat, psum[:, 0:TI * NR], 1e-12, None, ALU.max))
                                    return flat

                                tables((2, 3))
                                def sine(i):
                                    wait_rotated(dve, i)
                                    if i >= 2:
                                        dve.wait_ge(S["sum"], i - 1)
                                    dve.tensor_tensor(part[:, i % 2, :], rot[:, i % 3, :], table[:, 2 * (tile(i) // PAIRS) + 1, :], ALU.mult).then_inc(S["sin"], 1)

                                for i in range(NR):
                                    if i == 1:
                                        tables((0, 1))
                                    dve.wait_ge(S["qk"], i + 1)
                                    dve.wait_ge(S["sq"], i + 1)
                                    dve.tensor_tensor(dest(i), k.bank[:, i % 4, :], table[:, 2 * (tile(i) // PAIRS), :], ALU.mult).then_inc(S["cos"], 1)
                                    if i >= LAG:
                                        sine(i - LAG)
                                    if i == K_NORMS:
                                        flat = invert(1, kn, k.bank[:, 7, :])
                                        dve.reciprocal(flat, flat).then_inc(S["inv"], 1)
                                    if i == K_TURNED:
                                        dve.wait_ge(S["it"], 1)
                                        own.link(dve.tensor_tensor(rest[:, :], k.bank[0:NR, 6, :], ik[0:NR, :], ALU.subtract))
                                        own.link(dve.tensor_copy(ik[32:32 + NR, :], rest[:, :]))
                                        own.link(dve.tensor_tensor(rest[:, :], rest[:, :], ik[32:32 + NR, :], ALU.subtract))
                                        dve.tensor_copy(ik[64:64 + NR, :], rest[:, :]).then_inc(S["parts"], 1)
                                    for n in range(PER_STEP * (i - K_SPREAD), PER_STEP * (i + 1 - K_SPREAD)) if i >= K_SPREAD else ():
                                        if n == 0:
                                            dve.wait_ge(S["sum"], PAIRS)
                                        dve.wait_ge(S["spread"], n + 1)
                                        dve.tensor_tensor(m.k[:, n, HALO:], m.k[:, n, HALO:], k.bank[:, 6 + n % 2, :], ALU.mult).then_inc(S["kdone"], 1)
                                    if i < EARLY:
                                        dve.wait_ge(S["vmm"], i + 1)
                                        dve.tensor_copy(value_halves(i)[1], k.bank[64:P, 4, :]).then_inc(S["vd"], 1)
                                for i in range(NR - LAG, NR):
                                    sine(i)
                                flat = invert(2, qn, k.bank[:, 5, :])
                                own.link(dve.reciprocal(flat, flat))
                                dve.tensor_scalar(flat, flat, 8.0, None, ALU.mult).then_inc(S["inv"], 1)

                        def store(dve, psum):
                            at = x[:, bass.ds(b * T + c * TILE, TILE)]
                            return dve.tensor_tensor(at, psum, at, ALU.add)

                        def carry(pool):
                            return pool.tensor_copy(m.k[:, :, 0:HALO], m.k[:, :, TILE:])

                        def add(i):
                            wide = [P, 2 * PAIRS, 64]
                            if i:
                                return mask[:, 1, :].unsqueeze(1).to_broadcast(wide)
                            return mask[:, bass.ds(c, 1), :].to_broadcast(wide)

                        local_attention(k, m, 1.0, wo, store, qscale=lambda i: qn[:, i, :], mask=add, carry=carry,
                                        values=(window_values, value_halves, range(EARLY, PRODUCTS)))
                        clear(nc, [S[n] for n in ("xb", "raw", "rotated_0", "rotated_1", "rotated_2", "qk", "sq", "n2", "nt", "ntt", "parts", "inv", "iturned", "it", "spread", "cos", "sin",
                                                  "sum", "kdone", "vmm", "vc", "vd", "own")] + list(m.S.values()))
                clear(nc, [S["wloaded"], S["shift"], S["nothing"], S["zeros"]])
            gated_layer(k, w, S, layer, x, sh)
        with nc.Block() as block:
            @block.scalar
            def _(act):
                for t in range(NT):
                    act.activation(k.g[:, tok(t)], x[:, tok(t)], ACT.Silu).then_inc(S["g"], 1)


def gated_layer(k, w, S, layer, x, sh):
    nc = k.nc
    HALO = 32
    LAST = DI - P * (DI3 - 1)
    with ExitStack() as ctx:
        w1 = k.sb(ctx, "l3g_w1", [P, 2 * DI])
        w2 = k.sb(ctx, "l3g_w2", [P, DI3, D])
        col = k.sb(ctx, "l3g_cols", [P, 9])
        sx = k.sb(ctx, "l3g_sx", [P, N])
        nx = k.sb(ctx, "l3g_nx", [P, N])
        ge = k.sb(ctx, "l3g_gelu", [P, 2, TILE])
        h = k.sb(ctx, "l3g_h", [P, 2, DI3, TILE])
        R = {n: k.sem(k.ctx, "l3g_" + n) for n in ("w", "shift", "gate", "a", "gelu", "h", "mm", "x")}
        ln = [k.sem(k.ctx, "l3g_ln_" + n) for n in ("mean", "centred", "squared", "var", "std", "dve")]
        with nc.Block() as block:
            @block.sync
            def _(sp):
                for dst, src in ((w1[:, :], w["w1"]), (w2[:, :, :].rearrange("p a b -> p (a b)"), w["w2"]), (col[:, :], w["cols"])):
                    sp.dma_start(dst, src[bass.ds(layer, 1)].rearrange("a p n -> p (a n)")).then_inc(R["w"], 16)
                sp.wait_ge(R["w"], 48)

            @block.scalar
            def _(act):
                act.copy(sx[0:64, :], x[0:64, :]).then_inc(R["shift"], 1)

            @block.vector
            def _(dve):
                halves = (x[64:P, :].rearrange("p (a b) -> p a b", a=B), sx[64:P, :].rearrange("p (a b) -> p a b", a=B))
                dve.tensor_copy(halves[1][:, :, 1:], halves[0][:, :, 0:T - 1]).then_inc(R["shift"], 1)
                dve.memset(halves[1][:, :, 0:1], 0.0).then_inc(R["shift"], 1)
        layer_norm(k, "l3g_ln", sx, nx, gamma=col[:, 0:1], beta=col[:, 1:2], sems=ln)
        with nc.Block() as block:
            @block.tensor
            def _(pe):
                def first(t):
                    for o in range(DI3):
                        i = DI3 * t + o
                        width = min(P, DI - P * o)
                        if i >= 2:
                            pe.wait_ge(R["gelu"], i - 1)
                        pe.matmul(k.bank[0:width, i % 2, :], w1[:, DI + P * o:DI + P * o + width], nx[:, tok(t)], start=True, stop=True).then_inc(R["gate"], 1)
                        if i >= 2:
                            pe.wait_ge(R["h"], i - 1)
                        pe.matmul(k.bank[0:width, 2 + i % 2, :], w1[:, P * o:P * o + width], nx[:, tok(t)], start=True, stop=True).then_inc(R["a"], 1)

                first(0)
                for t in range(NT):
                    if t + 1 < NT:
                        first(t + 1)
                    pe.wait_ge(R["h"], DI3 * (t + 1))
                    if t >= 2:
                        pe.wait_ge(R["x"], t - 1)
                    for o in range(DI3):
                        width = min(P, DI - P * o)
                        ins = pe.matmul(k.bank[:, 4 + t % 2, :], w2[0:width, o, :], h[0:width, t % 2, o, :], start=o == 0, stop=o == DI3 - 1)
                    ins.then_inc(R["mm"], 1)

            @block.scalar
            def _(act):
                for i in range(NT * DI3):
                    o = i % DI3
                    width = min(P, DI - P * o)
                    act.wait_ge(R["gate"], i + 1)
                    if i >= 2:
                        act.wait_ge(R["h"], i - 1)
                    act.activation(ge[0:width, i % 2, :], k.bank[0:width, i % 2, :], ACT.Gelu, bias=col[0:width, 6 + o:7 + o]).then_inc(R["gelu"], 1)

            @block.vector
            def _(dve):
                def add(t):
                    dve.wait_ge(R["mm"], t + 1)
                    dve.scalar_tensor_tensor(x[:, tok(t)], k.bank[:, 4 + t % 2, :], col[:, 2:3], x[:, tok(t)], op0=ALU.add, op1=ALU.add).then_inc(R["x"], 1)

                for t in range(NT):
                    if t >= 2:
                        dve.wait_ge(R["mm"], t - 1)
                    for o in range(DI3):
                        i = DI3 * t + o
                        width = min(P, DI - P * o)
                        dve.wait_ge(R["gelu"], i + 1)
                        dve.wait_ge(R["a"], i + 1)
                        dve.scalar_tensor_tensor(h[0:width, t % 2, o, :], k.bank[0:width, 2 + i % 2, :], col[0:width, 3 + o:4 + o], ge[0:width, i % 2, :],
                                                 op0=ALU.add, op1=ALU.mult).then_inc(R["h"], 1)
                    if t:
                        add(t - 1)
                add(NT - 1)
        clear(nc, list(R.values()) + ln)


def store_out(k, src, out):
    nc = k.nc
    stored = k.sem(k.ctx, "out_stored")
    with nc.Block() as block:
        @block.sync
        def _(sp):
            sp.dma_start(out, src[:, :]).then_inc(stored, 16)
            sp.wait_ge(stored, 16)


def program(nc, a, out):
    with ExitStack() as ctx:
        k = Core(nc, ctx)
        load_start(k, a["x"], a)

        def arrays(prefix):
            return {n[len(prefix):]: v for n, v in a.items() if n.startswith(prefix)}

        with k.stage():
            layer_norm(k, "ln0", k.x, k.xn)
            gated_scan(k, arrays("l0a_"))
            ternary_ffn(k, arrays("l0f_"))
            combine(k, "l0")
        with k.stage():
            layer_norm(k, "ln1", k.x, k.xn)
            chunk_attention(k, arrays("l1a_"))
            mixture(k, arrays("moe_"))
            combine(k, "l1")
        with k.stage():
            layer_norm(k, "ln2", k.x, k.xn)
            wide_attention(k, arrays("l2a_"))
            fp4_ffn(k, arrays("fp4_"))
            combine(k, "l2")
        with k.stage():
            layer_norm(k, "ln3", k.x, k.xn)
            rope_attention(k, arrays("l3a_"))
            window_layers(k, arrays("l3f_"))
            combine(k, "l3")
        store_out(k, k.x, out)


def columns(v):
    return v.reshape(-1, P).T


def lay_out(i):
    a = {}
    a["x"] = i["L0_attn_x"].reshape(N, D).T
    a["ident"] = np.eye(P, dtype=np.float32)
    a["mean_w"] = np.full((P, P), 1.0 / P, np.float32)
    a["eps"] = np.tile(np.array([[LN_EPS, RMS_EPS]], np.float32), (P, 1))
    a["l0a_qkv"] = i["L0_attn_w_qkv"].T
    a["l0a_swiglu"] = i["L0_attn_w_swiglu"].T
    a["l0a_out"] = i["L0_attn_w_out"].T
    a["l0f_w12"] = np.stack([i["L0_ffn_w1_w"].T, i["L0_ffn_w2_w"].T], 1)
    a["l0f_h"] = np.stack([i[f"L0_ffn_{n}_w"].T.reshape(4, P, 512).transpose(1, 0, 2) for n in ("h1", "h2")], 1)
    a["l0f_w3"] = i["L0_ffn_w3_w"].T.reshape(4, P, D).transpose(1, 0, 2)
    a["l0f_scales"] = np.concatenate([columns(i[f"L0_ffn_{n}_s"]) for n in ("w1", "w2", "h1", "h2", "w3")], 1)
    qkv = i["L1_attn_w_qkv"].T
    a["l1a_qk"] = qkv[:, :2 * INNER].reshape(D, 2 * PAIRS, P)
    a["l1a_v"] = by_parity(qkv[:, 2 * INNER:])
    a["l1a_out"] = pair_rows(i["L1_attn_w_out"].T)
    a["l1a_b"] = i["L1_attn_b_out"].reshape(D, 1)
    a["moe_wg"] = i["L1_ffn_Wg"]
    a["moe_b2"] = i["L1_ffn_b2"]
    a["moe_rank"] = np.tile(np.arange(EXPERTS, 0, -1, dtype=np.float32), (P, 1))
    a["moe_ws"] = np.stack([i["L1_ffn_Ws1"], i["L1_ffn_Ws11"]], 1)
    a["moe_ws2"] = i["L1_ffn_Ws2"].reshape(SH // P, P, D).transpose(1, 0, 2)
    a["moe_bs"] = np.concatenate([columns(i["L1_ffn_bs1"]), columns(i["L1_ffn_bs11"]), columns(i["L1_ffn_bs2"])], 1)
    experts = [np.concatenate([i["L1_ffn_W1"][e], i["L1_ffn_W11"][e], i["L1_ffn_W2"][e][:P], i["L1_ffn_W2"][e][P:],
                               columns(i["L1_ffn_b1"][e]), columns(i["L1_ffn_b11"][e])], 1) for e in range(EXPERTS)]
    a["moe_experts"] = np.stack(experts + experts[:2])
    a["l2a_qkv"] = np.stack([i[f"L2_attn_W{n}"].reshape(D, PAIRS, P) for n in "qkv"], 2).transpose(1, 0, 2, 3).reshape(PAIRS, D, 3 * P)
    a["l2a_post"] = pair_rows(i["L2_attn_Wpost"])
    a["fp4_w"] = np.concatenate([np.pad(i[f"L2_ffn_w_{n}"], ((0, 3 * P - FFI), (0, 0))).reshape(3, P, D).transpose(1, 0, 2).reshape(P, 3 * P)
                                 for n in ("gate", "up")] + [i["L2_ffn_w_down"]], 1)
    for n, table in zip(("tables", "mask", "heads", "sel"), window_constants()):
        a["l3f_" + n] = table
    qkv = i["L3_ffn_Wqkv"]
    a["l3f_wqk"] = qkv[:, :, :2 * INNER]
    a["l3f_wv"] = np.stack([by_parity(v).reshape(D, -1) for v in qkv[:, :, 2 * INNER:]])
    a["l3f_wo"] = np.stack([pair_rows(v).reshape(P, -1) for v in i["L3_ffn_Wo"]])
    scales = [i["L3_ffn_q_scale"], i["L3_ffn_k_scale"]]
    a["l3f_qs"] = np.stack([np.tile(v, (1, 2)) for s in scales for v in (s, np.roll(s, 32, 1))], 2)
    a["l3f_w1"] = i["L3_ffn_W1"]
    a["l3f_w2"] = np.pad(i["L3_ffn_W2"], ((0, 0), (0, DI3 * P - DI), (0, 0))).reshape(DEPTH, DI3, P, D).transpose(0, 2, 1, 3).reshape(DEPTH, P, -1)
    b1 = np.pad(i["L3_ffn_b1"].reshape(DEPTH, 2, DI), ((0, 0), (0, 0), (0, DI3 * P - DI))).reshape(DEPTH, 2 * DI3, P).transpose(0, 2, 1)
    a["l3f_cols"] = np.concatenate([np.stack([i["L3_ffn_ln_g"], i["L3_ffn_ln_b"], i["L3_ffn_b2"]], 2), b1], 2)
    a["l2a_head"] = (np.repeat(np.eye(2), 64, 0) * DH ** -0.5).astype(np.float32)
    a["l3a_head"] = np.repeat(np.eye(4), 32, 0).astype(np.float32)
    a["l3a_cols"] = np.stack([i["L3_attn_gamma"], i["L3_attn_beta"], i["L3_attn_b_out"]], 1)
    a["l3a_out"] = i["L3_attn_W_out"]
    a["l3a_qkv"] = rope_weights(i["L3_attn_W_in"], i["L3_attn_b_in"])
    a["l3a_rope"] = rope_tables()
    for n in ("l2a_qkv", "l3a_qkv"):
        a[n] = np.concatenate([a[n], a[n][:1]])
    return a


def by_parity(v):
    return v.reshape(D, PAIRS, 2, DH).transpose(0, 2, 1, 3).reshape(D, 2, PAIRS * DH)


def pair_rows(v):
    return v.reshape(PAIRS, P, -1).transpose(1, 0, 2)


def rope_weights(w, b):
    rows = []
    wb = np.concatenate([w, b[None]], 0).reshape(D + 1, 3, 4, 4, 8)
    partner = [1, 0, 3, 2]
    for g in range(4):
        tiles = []
        for n in range(2):
            straight, rotated = (np.zeros((D + 1, 4, 32), np.float32) for _ in range(2))
            straight[:, :, :8] = wb[:, n, g]
            rotated[:, :, :4] = wb[:, n, g][:, :, partner]
            tiles += [straight.reshape(D + 1, P), rotated.reshape(D + 1, P)]
        v = wb[:, 2, g].reshape(D + 1, 32)
        weights = [x[:D] for x in tiles] + [v[:D]]
        biases = [x[D].reshape(P, 1) for x in tiles] + [np.tile(v[D], (P, 1))]
        rows.append(np.concatenate(weights + biases, 1))
    return np.stack(rows)


def rope_tables():
    inv = (1.0 / 10000.0 ** (np.arange(0, 4, 2, dtype=np.float32) / np.float32(4))).astype(np.float32)
    angle = np.repeat(np.arange(T, dtype=np.float32)[:, None] * inv[None], 2, 1).T
    cos, sin = np.zeros((2, 4, 32, T), np.float32)
    cos[:, :4], cos[:, 4:8] = np.cos(angle), 1.0
    sin[:, :4] = np.sin(angle) * np.array([-1, 1, -1, 1], np.float32)[:, None]
    cos, sin = cos.reshape(P, T), sin.reshape(P, T)
    scale = np.float32(8 ** -0.5)
    return np.stack([cos * scale, sin * scale, cos, sin], 1)


def window_constants():
    half = np.arange(0, DH, 2, dtype=np.float32)
    inv = (1.0 / 10000.0 ** (half / np.float32(DH))).astype(np.float32)
    t = np.arange(T, dtype=np.float32)
    angle = t[:, None] * inv[None]
    angle = np.concatenate([angle, angle], 1).T
    base = ((half + np.float32(0.4 * DH)) / np.float32(1.4 * DH)).astype(np.float32)
    power = (t - T // 2) / (WIN // 2)
    scale = (base[None] ** power[:, None]).astype(np.float32)
    scale = np.concatenate([scale, scale], 1).T
    sign = np.where(np.arange(DH) < DH // 2, -1.0, 1.0).astype(np.float32)[:, None]
    tables = np.stack([np.cos(angle) * scale, sign * np.sin(angle) * scale, np.cos(angle) / scale, sign * np.sin(angle) / scale], 1)
    q, j = np.arange(WIN)[:, None], np.arange(2 * WIN)[None]
    fits = (q <= j) & (j <= q + WIN)
    usual = np.tile(np.where(fits, 0.0, -3e38), (4, 1))
    first = usual.copy()
    first[:WIN, :WIN] = -3e38
    masks = np.stack([first, usual], 1)
    heads = np.zeros((P, PAIRS, 2 * PAIRS))
    for i in range(PAIRS):
        heads[:64, i, 2 * i] = heads[64:, i, 2 * i + 1] = 1.0
    sel = np.zeros((P, PAIRS, P))
    for part in range(3):
        for head in range(2 * PAIRS):
            sel[32 * part + head, head // 2, 64 * (head % 2):64 * (head % 2) + 64] = 1.0
    return (np.tile(tables, (2, 1, 1)).astype(np.float32), masks.astype(np.float32),
            heads.astype(np.float32), sel.astype(np.float32))


def kernel(**inputs):
    import concourse.bacc as bacc
    from concourse.bass_utils import run_bass_kernel_spmd as run

    nc = bacc.Bacc("TRN2", target_bir_lowering=False, num_devices=1)
    arrays = {n: np.ascontiguousarray(v) for n, v in lay_out({n: np.asarray(v) for n, v in inputs.items()}).items()}
    aps = {n: nc.dram_tensor("in_" + n, v.shape, F32, kind="ExternalInput").ap() for n, v in arrays.items()}
    out = nc.dram_tensor("out", (D, N), F32, kind="ExternalOutput").ap()
    program(nc, aps, out)
    r = run(nc, [{"in_" + n: v for n, v in arrays.items()}], core_ids=[0])
    return np.ascontiguousarray(r.results[0]["out"].T).reshape(B, T, D)
```
